# Optimizing a Trainium2 kernel written in Bass

```python
import numpy as np
import jax
import jax.numpy as jnp

def _softmax(x, axis=-1):
    return jax.nn.softmax(x, axis=axis)

def _gelu(x):
    return jax.nn.gelu(x, approximate=True)

def _silu(x):
    return jax.nn.silu(x)

def _sigmoid(x):
    return jax.nn.sigmoid(x)

def _layernorm(x, axis=-1, eps=1e-05):
    m = jnp.mean(x, axis=axis, keepdims=True)
    v = jnp.var(x, axis=axis, keepdims=True)
    return (x - m) / jnp.sqrt(v + eps)

def _scatter_add(tgt, idx, src, axis=0):
    return tgt.at[idx].add(src)

def _segment_sum(src, seg, n):
    return jax.ops.segment_sum(src, seg, n)
kernel_name = 'mk_gnn_resnorm_d4_gnn_r8_f0e264'

def setup_inputs(seed: int=0):
    np.random.seed(seed)
    _w = jnp.asarray

    def _rec_inputs():
        import jax
        import jax.numpy as jnp
        _gk = jax.random.key(seed)
        x = -0.0002928 + 1 * jax.random.normal(jax.random.fold_in(_gk, 1), (1024, 512), jnp.float32)
        _s = jax.random.randint(jax.random.fold_in(_gk, 2), (8192,), 0, 1024, jnp.int32)
        _d = jax.random.randint(jax.random.fold_in(_gk, 3), (8192,), 0, 1024, jnp.int32)
        _loop = jnp.arange(1024, dtype=jnp.int32)
        src = jnp.concatenate([_s, _d, _loop])
        dst = jnp.concatenate([_d, _s, _loop])
        _o = jnp.argsort(dst, stable=True)
        src = src[_o]
        dst = dst[_o]
        edge_attr_32 = jax.random.uniform(jax.random.fold_in(_gk, 11), (17408, 32), jnp.float32, 0.0, 1)
        edge_attr_4 = 0.000937891 + 0.999965 * jax.random.normal(jax.random.fold_in(_gk, 12), (17408, 4), jnp.float32)
        edge_weight = jax.random.uniform(jax.random.fold_in(_gk, 14), (17408,), jnp.float32, 0.0, 0.999994)
        return (x, src, dst, edge_attr_32, edge_attr_4, edge_weight)
    x, src, dst, edge_attr_32, edge_attr_4, edge_weight = _rec_inputs()

    def _L0_gnn_setup():
        import jax, jax.numpy as jnp
        import numpy as np
        N_NODES = 1024
        D_MODEL = 512
        N_LAYERS = 2
        N_EDGES = 32768
        LEAKY_SLOPE = 0.01

        def _normalized_adj(edge_index, edge_weights, num_nodes):
            A = jnp.zeros((num_nodes, num_nodes), dtype=edge_weights.dtype)
            A = A.at[edge_index[0], edge_index[1]].add(edge_weights)
            deg = jnp.sum(A, axis=1)
            dinv = jnp.where(deg > 0, deg ** (-0.5), 0.0)
            return dinv[:, None] * A * dinv[None, :]
        key = jax.random.key(seed)
        ks = jax.random.split(key, 6)
        x = jax.random.normal(ks[0], (N_NODES, D_MODEL), dtype=jnp.float32)
        edge_weights = jax.random.uniform(ks[1], (N_EDGES,), dtype=jnp.float32)
        edge_index = jax.random.randint(ks[2], (2, N_EDGES), 0, N_NODES, dtype=jnp.int64)
        scale = 0.02
        W_gcn = jax.random.normal(ks[3], (N_LAYERS, D_MODEL, D_MODEL), dtype=jnp.float32) * scale
        b_gcn = jnp.zeros((N_LAYERS, D_MODEL), dtype=jnp.float32)
        W_mlp = jax.random.normal(ks[4], (N_LAYERS, D_MODEL, D_MODEL), dtype=jnp.float32) * scale
        b_mlp = jnp.zeros((N_LAYERS, D_MODEL), dtype=jnp.float32)
        return {'x': x, 'edge_weights': edge_weights, 'W_gcn': W_gcn, 'b_gcn': b_gcn, 'W_mlp': W_mlp, 'b_mlp': b_mlp, 'edge_index': edge_index}
    _L0_gnn_all = _L0_gnn_setup()
    _L0_gnn_in = {k: v for k, v in _L0_gnn_all.items() if k in ('W_gcn', 'b_gcn', 'W_mlp', 'b_mlp')}
    del _L0_gnn_all

    def _L1_gnn_setup():
        import jax, jax.numpy as jnp
        import numpy as np
        N, E, H, D_IN, D_PRIME = (6250, 100000, 8, 512, 64)

        def _segment_softmax(scores, seg, num_segments):
            smax = jax.ops.segment_max(scores, seg, num_segments=num_segments)
            ex = jnp.exp(scores - smax[seg])
            denom = jax.ops.segment_sum(ex, seg, num_segments=num_segments)
            return ex / denom[seg]
        key = jax.random.key(seed)
        ks = jax.random.split(key, 6)
        x = jax.random.normal(ks[0], (N, D_IN), dtype=jnp.float32)
        edge_index = jax.random.randint(ks[1], (2, E), 0, N)
        Ws = jax.random.normal(ks[2], (H, D_IN, D_PRIME), dtype=jnp.float32) * 0.05
        Wb = jax.random.normal(ks[3], (H, D_PRIME), dtype=jnp.float32) * 0.05
        a_w = jax.random.normal(ks[4], (H, 2 * D_PRIME), dtype=jnp.float32) * 0.05
        a_b = jax.random.normal(ks[5], (H,), dtype=jnp.float32) * 0.05
        return dict(x=x, edge_index=edge_index, Ws=Ws, Wb=Wb, a_w=a_w, a_b=a_b)
    _L1_gnn_all = _L1_gnn_setup()
    _L1_gnn_in = {k: v for k, v in _L1_gnn_all.items() if k in ('Ws', 'Wb', 'a_w', 'a_b')}
    del _L1_gnn_all

    def _L2_gnn_setup():
        import jax, jax.numpy as jnp
        import numpy as np
        import math
        N, E = (2500, 25000)
        MUL = 128
        D = MUL + 3 * MUL
        EDGE_ATTR = 32
        HID = 32
        LOG2 = math.log(2.0)

        def ssp(x):
            return jax.nn.softplus(x) - LOG2

        def split_irreps(x):
            return (x[:, :MUL], x[:, MUL:].reshape(x.shape[0], MUL, 3))

        def merge_irreps(x0, x1):
            return jnp.concatenate([x0, x1.reshape(x1.shape[0], MUL * 3)], axis=-1)

        def irrep_linear(x, W0, b0, W1):
            x0, x1 = split_irreps(x)
            y0 = x0 @ W0 + b0
            y1 = jnp.einsum('nuc,uv->nvc', x1, W1)
            return merge_irreps(y0, y1)
        key = jax.random.key(seed)
        ks = iter(jax.random.split(key, 32))

        def randn(shape, scale=1.0):
            return (scale * jax.random.normal(next(ks), shape)).astype(jnp.float32)
        inp = {'x': randn((N, D)), 'edge_sh': randn((E, 4)), 'edge_attr': jax.random.uniform(next(ks), (E, EDGE_ATTR), dtype=jnp.float32), 'edge_index': jax.random.randint(next(ks), (2, E), 0, N, dtype=jnp.int32), 'W_pre0': randn((MUL, MUL), MUL ** (-0.5)), 'b_pre0': jnp.zeros((MUL,), jnp.float32), 'W_pre1': randn((MUL, MUL), MUL ** (-0.5)), 'W_nd0': randn((MUL, MUL), MUL ** (-0.5)), 'b_nd0': jnp.zeros((MUL,), jnp.float32), 'W_nd1': randn((MUL, MUL), MUL ** (-0.5)), 'W_g1': randn((2 * MUL, 2 * MUL), (2 * MUL) ** (-0.5)), 'b_g1': jnp.zeros((2 * MUL,), jnp.float32), 'W_g2': randn((2 * MUL, 2 * MUL), (2 * MUL) ** (-0.5)), 'b_g2': jnp.zeros((2 * MUL,), jnp.float32), 'W_f1': randn((EDGE_ATTR, HID), EDGE_ATTR ** (-0.5)), 'W_f2': randn((HID, 4 * MUL), HID ** (-0.5)), 'W_s1': randn((3 * MUL, HID), (3 * MUL) ** (-0.5)), 'W_s2': randn((HID, 4 * MUL), HID ** (-0.5)), 'W_o0': randn((MUL, MUL), MUL ** (-0.5)), 'b_o0': jnp.zeros((MUL,), jnp.float32), 'W_o1': randn((MUL, MUL), MUL ** (-0.5))}
        return inp
    _L2_gnn_all = _L2_gnn_setup()
    _L2_gnn_in = {k: v for k, v in _L2_gnn_all.items() if k in ('W_pre0', 'b_pre0', 'W_pre1', 'W_nd0', 'b_nd0', 'W_nd1', 'W_g1', 'b_g1', 'W_g2', 'b_g2', 'W_f1', 'W_f2', 'W_s1', 'W_s2', 'W_o0', 'b_o0', 'W_o1')}
    del _L2_gnn_all

    def _L3_gnn_setup():
        import jax, jax.numpy as jnp
        import numpy as np
        N = 6250
        IN_CH = 512
        OUT_CH = 512
        DEG = 32
        E = N * DEG
        key = jax.random.key(seed)
        kx, kwc, kwn, kb, ke = jax.random.split(key, 5)
        x = jax.random.normal(kx, (N, IN_CH), dtype=jnp.float32)
        bound = 1.0 / np.sqrt(IN_CH)
        wc = jax.random.uniform(kwc, (IN_CH, OUT_CH), minval=-bound, maxval=bound, dtype=jnp.float32)
        wn = jax.random.uniform(kwn, (IN_CH, OUT_CH), minval=-bound, maxval=bound, dtype=jnp.float32)
        bias = jax.random.uniform(kb, (OUT_CH,), minval=-bound, maxval=bound, dtype=jnp.float32)
        src = jnp.repeat(jnp.arange(N, dtype=jnp.int64), DEG)
        dst = jax.random.randint(ke, (E,), 0, N, dtype=jnp.int64)
        edge_index = jnp.stack([src, dst], axis=0)
        return {'x': x, 'wc': wc, 'wn': wn, 'bias': bias, 'edge_index': edge_index}
    _L3_gnn_all = _L3_gnn_setup()
    _L3_gnn_in = {k: v for k, v in _L3_gnn_all.items() if k in ('wc', 'wn', 'bias')}
    del _L3_gnn_all
    return {'x': x, 'src': src, 'dst': dst, 'edge_attr_32': edge_attr_32, 'edge_attr_4': edge_attr_4, 'edge_weight': edge_weight, 'L0_gnn_W_gcn': _L0_gnn_in['W_gcn'], 'L0_gnn_b_gcn': _L0_gnn_in['b_gcn'], 'L0_gnn_W_mlp': _L0_gnn_in['W_mlp'], 'L0_gnn_b_mlp': _L0_gnn_in['b_mlp'], 'L1_gnn_Ws': _L1_gnn_in['Ws'], 'L1_gnn_Wb': _L1_gnn_in['Wb'], 'L1_gnn_a_w': _L1_gnn_in['a_w'], 'L1_gnn_a_b': _L1_gnn_in['a_b'], 'L2_gnn_W_pre0': _L2_gnn_in['W_pre0'], 'L2_gnn_b_pre0': _L2_gnn_in['b_pre0'], 'L2_gnn_W_pre1': _L2_gnn_in['W_pre1'], 'L2_gnn_W_nd0': _L2_gnn_in['W_nd0'], 'L2_gnn_b_nd0': _L2_gnn_in['b_nd0'], 'L2_gnn_W_nd1': _L2_gnn_in['W_nd1'], 'L2_gnn_W_g1': _L2_gnn_in['W_g1'], 'L2_gnn_b_g1': _L2_gnn_in['b_g1'], 'L2_gnn_W_g2': _L2_gnn_in['W_g2'], 'L2_gnn_b_g2': _L2_gnn_in['b_g2'], 'L2_gnn_W_f1': _L2_gnn_in['W_f1'], 'L2_gnn_W_f2': _L2_gnn_in['W_f2'], 'L2_gnn_W_s1': _L2_gnn_in['W_s1'], 'L2_gnn_W_s2': _L2_gnn_in['W_s2'], 'L2_gnn_W_o0': _L2_gnn_in['W_o0'], 'L2_gnn_b_o0': _L2_gnn_in['b_o0'], 'L2_gnn_W_o1': _L2_gnn_in['W_o1'], 'L3_gnn_wc': _L3_gnn_in['wc'], 'L3_gnn_wn': _L3_gnn_in['wn'], 'L3_gnn_bias': _L3_gnn_in['bias']}

def reference(x, src, dst, edge_attr_32, edge_attr_4, edge_weight, L0_gnn_W_gcn, L0_gnn_b_gcn, L0_gnn_W_mlp, L0_gnn_b_mlp, L1_gnn_Ws, L1_gnn_Wb, L1_gnn_a_w, L1_gnn_a_b, L2_gnn_W_pre0, L2_gnn_b_pre0, L2_gnn_W_pre1, L2_gnn_W_nd0, L2_gnn_b_nd0, L2_gnn_W_nd1, L2_gnn_W_g1, L2_gnn_b_g1, L2_gnn_W_g2, L2_gnn_b_g2, L2_gnn_W_f1, L2_gnn_W_f2, L2_gnn_W_s1, L2_gnn_W_s2, L2_gnn_W_o0, L2_gnn_b_o0, L2_gnn_W_o1, L3_gnn_wc, L3_gnn_wn, L3_gnn_bias):
    import jax
    import jax.numpy as jnp

    def _L0_gnn_ref(x, edge_weights, W_gcn, b_gcn, W_mlp, b_mlp, edge_index):
        import jax, jax.numpy as jnp
        import numpy as np
        N_NODES = 1024
        D_MODEL = 512
        N_LAYERS = 2
        N_EDGES = 32768
        LEAKY_SLOPE = 0.01

        def _normalized_adj(edge_index, edge_weights, num_nodes):
            A = jnp.zeros((num_nodes, num_nodes), dtype=edge_weights.dtype)
            A = A.at[edge_index[0], edge_index[1]].add(edge_weights)
            deg = jnp.sum(A, axis=1)
            dinv = jnp.where(deg > 0, deg ** (-0.5), 0.0)
            return dinv[:, None] * A * dinv[None, :]
        N = x.shape[0]
        A_norm = _normalized_adj(edge_index, edge_weights, N)
        h = x
        for l in range(W_gcn.shape[0]):
            h = A_norm @ h
            h = h @ W_gcn[l] + b_gcn[l]
            h = jax.nn.leaky_relu(h @ W_mlp[l] + b_mlp[l], negative_slope=LEAKY_SLOPE)
        return h

    def _L1_gnn_ref(x, edge_index, Ws, Wb, a_w, a_b):
        import jax, jax.numpy as jnp
        import numpy as np
        N, E, H, D_IN, D_PRIME = (6250, 100000, 8, 512, 64)

        def _segment_softmax(scores, seg, num_segments):
            smax = jax.ops.segment_max(scores, seg, num_segments=num_segments)
            ex = jnp.exp(scores - smax[seg])
            denom = jax.ops.segment_sum(ex, seg, num_segments=num_segments)
            return ex / denom[seg]
        v_src, v_tgt = (edge_index[0], edge_index[1])
        n = x.shape[0]
        outs = []
        for h in range(Ws.shape[0]):
            Wx = x @ Ws[h] + Wb[h]
            d = Wx.shape[-1]
            s = Wx[v_tgt] @ a_w[h, :d] + Wx[v_src] @ a_w[h, d:] + a_b[h]
            s = jax.nn.leaky_relu(s, negative_slope=0.2)
            alpha = _segment_softmax(s, v_tgt, n)
            outs.append(jax.ops.segment_sum(alpha[:, None] * Wx[v_src], v_tgt, num_segments=n))
        return jnp.stack(outs, axis=1).reshape(n, -1)

    def _L2_gnn_ref(x, edge_sh, edge_attr, edge_index, W_pre0, b_pre0, W_pre1, W_nd0, b_nd0, W_nd1, W_g1, b_g1, W_g2, b_g2, W_f1, W_f2, W_s1, W_s2, W_o0, b_o0, W_o1):
        import jax, jax.numpy as jnp
        import numpy as np
        import math
        N, E = (2500, 25000)
        MUL = 128
        D = MUL + 3 * MUL
        EDGE_ATTR = 32
        HID = 32
        LOG2 = math.log(2.0)

        def ssp(x):
            return jax.nn.softplus(x) - LOG2

        def split_irreps(x):
            return (x[:, :MUL], x[:, MUL:].reshape(x.shape[0], MUL, 3))

        def merge_irreps(x0, x1):
            return jnp.concatenate([x0, x1.reshape(x1.shape[0], MUL * 3)], axis=-1)

        def irrep_linear(x, W0, b0, W1):
            x0, x1 = split_irreps(x)
            y0 = x0 @ W0 + b0
            y1 = jnp.einsum('nuc,uv->nvc', x1, W1)
            return merge_irreps(y0, y1)
        edge_dst, edge_src = (edge_index[0], edge_index[1])
        old_x = x
        pre = irrep_linear(x, W_pre0, b_pre0, W_pre1)
        p0, p1 = split_irreps(pre)
        pd0 = p0[edge_dst]
        ip1 = jnp.einsum('eum,eum->eu', p1[edge_dst], p1[edge_src]) / 3.0
        s0 = jnp.concatenate([pd0, pd0, ip1], axis=-1)
        x0, x1 = split_irreps(x)
        n1 = jnp.sqrt(jnp.sum(x1 * x1, axis=-1) / 3.0)
        g = jax.nn.silu(jnp.concatenate([x0, n1], -1) @ W_g1 + b_g1) @ W_g2 + b_g2
        xg = merge_irreps(g[:, :MUL], x1 * g[:, MUL:, None])
        x = irrep_linear(xg, W_nd0, b_nd0, W_nd1)
        self_x = x
        w = ssp(edge_attr @ W_f1) @ W_f2 * (ssp(s0 @ W_s1) @ W_s2)
        w1, w2, w3, w4 = jnp.split(w, 4, axis=-1)
        x0e, x1e = split_irreps(x[edge_src])
        sh0, sh1 = (edge_sh[:, 0], edge_sh[:, 1:4])
        out0 = w1 * x0e * sh0[:, None] + w4 * (jnp.einsum('eum,em->eu', x1e, sh1) / jnp.sqrt(3.0))
        out1 = w2[:, :, None] * x0e[:, :, None] * sh1[:, None, :] + w3[:, :, None] * x1e * sh0[:, None, None]
        edge_feat = merge_irreps(out0, out1)
        out = jax.ops.segment_sum(edge_feat, edge_dst, num_segments=old_x.shape[0])
        out = out + self_x
        out = irrep_linear(out, W_o0, b_o0, W_o1)
        return out + old_x

    def _L3_gnn_ref(x, wc, wn, bias, edge_index):
        import jax, jax.numpy as jnp
        import numpy as np
        N = 6250
        IN_CH = 512
        OUT_CH = 512
        DEG = 32
        E = N * DEG
        alpha = x @ wc
        beta = x @ wn
        src, dst = (edge_index[0], edge_index[1])
        sums = jax.ops.segment_sum(beta[dst], src, num_segments=x.shape[0])
        counts = jax.ops.segment_sum(jnp.ones_like(src, dtype=beta.dtype), src, num_segments=x.shape[0])
        gamma = sums / counts[:, None]
        return alpha + gamma + bias
    edge_index = jnp.stack([src, dst])
    x = _layernorm(x + _L0_gnn_ref(x, edge_weight, L0_gnn_W_gcn, L0_gnn_b_gcn, L0_gnn_W_mlp, L0_gnn_b_mlp, edge_index), axis=-1)
    x = _layernorm(x + _L1_gnn_ref(x, edge_index, L1_gnn_Ws, L1_gnn_Wb, L1_gnn_a_w, L1_gnn_a_b), axis=-1)
    x = _layernorm(x + _L2_gnn_ref(x, edge_attr_4, edge_attr_32, edge_index, L2_gnn_W_pre0, L2_gnn_b_pre0, L2_gnn_W_pre1, L2_gnn_W_nd0, L2_gnn_b_nd0, L2_gnn_W_nd1, L2_gnn_W_g1, L2_gnn_b_g1, L2_gnn_W_g2, L2_gnn_b_g2, L2_gnn_W_f1, L2_gnn_W_f2, L2_gnn_W_s1, L2_gnn_W_s2, L2_gnn_W_o0, L2_gnn_b_o0, L2_gnn_W_o1), axis=-1)
    x = _layernorm(x + _L3_gnn_ref(x, L3_gnn_wc, L3_gnn_wn, L3_gnn_bias, edge_index), axis=-1)
    return x

_drawn_inputs = setup_inputs


def setup_inputs(seed=0):
    import zlib

    import numpy as np

    out = dict(_drawn_inputs(seed))
    spreads = {'L0_gnn_b_gcn': (0.0, 0.1),
     'L0_gnn_b_mlp': (0.0, 0.1),
     'L2_gnn_b_pre0': (0.0, 0.407),
     'L2_gnn_b_nd0': (0.0, 0.1),
     'L2_gnn_b_g1': (0.0, 0.1),
     'L2_gnn_b_g2': (0.0, 0.1),
     'L2_gnn_b_o0': (0.0, 0.304)}
    factors = {'edge_weight': 8.0, 'L0_gnn_W_gcn': 3.272, 'L1_gnn_a_b': 8.0, 'L3_gnn_bias': 2.744}
    for name, (base, spread) in spreads.items():
        noise = np.random.default_rng([zlib.crc32(name.encode()), seed]).standard_normal(out[name].shape)
        drawn = base * np.exp(spread * noise) if base else spread * noise
        out[name] = jnp.asarray(drawn.astype(out[name].dtype))
    for name, factor in factors.items():
        out[name] = (out[name] * factor).astype(out[name].dtype)
    return out
```

```python
from contextlib import ExitStack

import concourse.bass as bass
from concourse import mybir

F32 = mybir.dt.float32
BF16 = mybir.dt.bfloat16
I32 = mybir.dt.int32
I16 = mybir.dt.int16
ALU = mybir.AluOpType
ACT = mybir.ActivationFunctionType
AX = mybir.AxisListType.X

P = 128
N = 1024
NB = N // P
D = 512
FB = D // P
E = 17408
TE = E // P
SUP = 256
TPS = SUP // P
S = E // SUP + NB
T = S * TPS
GT = 8
REC = 39
R_SH, R_W, R_I, R_J = 32, 36, 37, 38
HEADS, DH = 8, 64
MUL = 128
BIG = 1e30
EPS = 1e-5


class Core:
    pass


def sbuf(c, name, shape, dtype=F32, stack=None):
    return (stack or c.stack).enter_context(c.nc.sbuf_tensor(name, shape, dtype))


def psum(c, name, shape, stack, dtype=F32):
    return stack.enter_context(c.nc.psum_tensor(name, shape, dtype))


def semaphore(c, name):
    got = c.semaphores.enter_context(c.nc.semaphore(name))
    c.used.append(got)
    return got


def clear_semaphores(c):
    with c.nc.Block() as block:
        @block.sync
        def _(sp):
            for one in c.used:
                sp.sem_clear(one)
    c.semaphores.close()
    c.used = []


def chained(engine, finished):
    count, before, mark, size = [0], [0], [0], [0]

    def chain(instruction):
        instruction.then_inc(finished, 1)
        count[0] += 1
        engine.wait_ge(finished, before[0] + count[0])

    def turn(i, per):
        before[0], mark[0], size[0] = i * per, count[0], per

    def close(turns):
        assert count[0] - mark[0] == size[0], (count[0] - mark[0], size[0])
        before[0], count[0] = 0, mark[0] + turns * size[0]

    return chain, turn, close


def constants(c):
    nc = c.nc
    c.iota_node = sbuf(c, "iota_node", [P, N], I16)
    c.iota_row = sbuf(c, "iota_row", [P, P], BF16)
    c.iota_tile = sbuf(c, "iota_tile", [P, T], BF16)
    c.iota_sup = sbuf(c, "iota_sup", [P, S], F32)
    c.ident = sbuf(c, "ident", [P, P])
    c.before = sbuf(c, "before", [P, P])
    c.ones = sbuf(c, "ones", [P, P])
    made = semaphore(c, "constants_made")

    with nc.Block() as block:
        @block.gpsimd
        def _(pool):
            chain, _, _ = chained(pool, made)
            chain(nc.gpsimd.iota(c.iota_node[:], [[1, N]], base=0, channel_multiplier=0))
            chain(nc.gpsimd.iota(c.iota_row[:], [[1, P]], base=0, channel_multiplier=0,
                                 allow_small_or_imprecise_dtypes=True))
            chain(nc.gpsimd.iota(c.iota_tile[:], [[1, T]], base=0, channel_multiplier=0,
                                 allow_small_or_imprecise_dtypes=True))
            chain(nc.gpsimd.iota(c.iota_sup[:], [[1, S]], base=0, channel_multiplier=0,
                                 allow_small_or_imprecise_dtypes=True))
            chain(nc.gpsimd.memset(c.ones[:], 1.0))
            chain(nc.gpsimd.memset(c.ident[:], 0.0))
            chain(nc.gpsimd.affine_select(out=c.ident[:], in_=c.ident[:], compare_op=ALU.not_equal, fill=1.0,
                                          base=0, pattern=[[-1, P]], channel_multiplier=1))
            chain(nc.gpsimd.memset(c.before[:], 0.0))
            chain(nc.gpsimd.affine_select(out=c.before[:], in_=c.before[:], compare_op=ALU.is_ge, fill=1.0,
                                          base=0, pattern=[[-1, P]], channel_multiplier=1))


def order_edges(c):
    nc = c.nc
    c.rows = nc.dram_tensor("records", [1 + E, REC], F32, kind="Internal").ap()
    c.row_of_place = sbuf(c, "row_of_place", [P, T], I32)
    c.block_of_sup = sbuf(c, "block_of_sup", [P, S], F32)
    c.block_reg = sbuf(c, "block_reg", [P, S], I32)
    loaded, loaded_attr, step, placed, attrs_in = (semaphore(c, n) for n in (
        "edges_loaded", "attributes_loaded", "order_step", "edges_placed", "attributes_copied"))
    rows_out, sums_ready, hot_ready, hot_used, perm_ready = (semaphore(c, n) for n in (
        "records_out", "prefix_ready", "places_hot", "places_hot_used", "rows_ready"))
    totals_ready, zero_made, row_numbers = semaphore(c, "totals_ready"), semaphore(c, "zero_made"), semaphore(c, "row_numbers")
    with ExitStack() as stack:
        sb = lambda name, shape, dtype=F32: sbuf(c, name, shape, dtype, stack)
        ends = sb("ends", [P, 2, TE], I32)
        attr32 = sb("attr32", [P, TE, 32])
        attr4 = sb("attr4", [P, TE, 4])
        weight = sb("weight", [P, TE])
        record = sb("record", [P, TE, REC])
        dummy = sb("empty_record", [1, REC])
        blk = sb("blk", [P, TE], I32)
        blk_f = sb("blk_f", [P, TE])
        in_block = sb("in_block", [P, NB, TE])
        upto = sb("upto", [P, NB, TE])
        onesrow = sb("onesrow", [P, TE])
        totals = sb("totals", [P, NB])
        first = sb("first", [P, NB])
        sups = sb("sups", [P, NB])
        sups_i = sb("sups_i", [P, NB], I32)
        sup_end = sb("sup_end", [P, NB])
        place = sb("place", [P, TE])
        term = sb("term", [P, TE])
        place_i = sb("place_i", [P, TE], I32)
        tmp_i = sb("tmp_i", [P, TE], I32)
        high = sb("high", [P, TE])
        low = sb("low", [P, TE])
        row_i = sb("row_i", [P, TE], I32)
        row_high = sb("row_high", [P, TE])
        row_low = sb("row_low", [P, TE])
        hot_low = sb("hot_low", [P, 2, GT, P], BF16)
        hot_row = sb("hot_row", [P, 2, GT, 2, T], BF16)
        zero = sb("zero", [P, 2 * T], BF16)
        row_f = sb("row_f", [P, T])
        sup_ge = sb("sup_ge", [P, S])
        counts_ps = psum(c, "counts_ps", [P, 2 * NB], stack)
        perm_ps = psum(c, "perm_ps", [P, 2 * T], stack)

        with nc.Block() as block:
            @block.sync
            def _(sp):
                sp.dma_start(ends[:, 0, :], c.ins["src"].rearrange("(p t) -> p t", p=P)).then_inc(loaded, 16)
                sp.dma_start(ends[:, 1, :], c.ins["dst"].rearrange("(p t) -> p t", p=P)).then_inc(loaded, 16)
                sp.dma_start(weight[:], c.ins["edge_weight"].rearrange("(p t) -> p t", p=P)).then_inc(loaded_attr, 16)
                sp.dma_start(attr4[:], c.ins["edge_attr_4"].rearrange("(p t) a -> p t a", p=P)).then_inc(loaded_attr, 16)
                sp.dma_start(attr32[:], c.ins["edge_attr_32"].rearrange("(p t) a -> p t a", p=P)).then_inc(loaded_attr, 16)
                sp.wait_ge(attrs_in, 5)
                sp.dma_start(c.rows[1:, :].rearrange("(p t) r -> p (t r)", p=P),
                             record[:].rearrange("p t r -> p (t r)")).then_inc(rows_out, 16)
                sp.dma_start(c.rows[0:1, :], dummy[:]).then_inc(rows_out, 16)
                sp.wait_ge(rows_out, 32)

            @block.scalar
            def _(act):
                act.wait_ge(loaded, 32)
                nc.scalar.copy(record[:, :, R_I:R_I + 2], ends[:].rearrange("p e t -> p t e")).then_inc(attrs_in, 1)
                act.wait_ge(loaded_attr, 48)
                nc.scalar.copy(record[:, :, 0:32], attr32[:]).then_inc(attrs_in, 1)
                nc.scalar.copy(record[:, :, R_SH:R_SH + 4], attr4[:]).then_inc(attrs_in, 1)
                nc.scalar.copy(record[:, :, R_W], weight[:]).then_inc(attrs_in, 1)

            @block.gpsimd
            def _(pool):
                nc.gpsimd.iota(row_i[:], [[1, TE]], base=1, channel_multiplier=TE).then_inc(row_numbers, 1)
                pool.wait_ge(zero_made, 1)
                nc.gpsimd.memset(dummy[0:1, R_I:R_I + 1], -1.0).then_inc(attrs_in, 1)

            @block.vector
            def _(dve):
                nc.vector.memset(dummy[:], 0.0).then_inc(zero_made, 1)
                nc.vector.memset(zero[:], 0.0).then_inc(zero_made, 1)
                chain, _, _ = chained(dve, step)
                chain(nc.vector.memset(onesrow[:], 1.0))
                dve.wait_ge(loaded, 32)
                chain(nc.vector.tensor_single_scalar(blk[:], ends[:, 0, :], 7, op=ALU.arith_shift_right))
                chain(nc.vector.tensor_copy(blk_f[:], blk[:]))
                for b in range(NB):
                    last = nc.vector.tensor_scalar(in_block[:, b, :], blk_f[:], float(b), None, ALU.is_equal)
                chain(last)
                for b in range(NB):
                    last = nc.vector.tensor_tensor_scan(upto[:, b, :], onesrow[:], in_block[:, b, :], 0.0,
                                                        ALU.mult, ALU.add)
                chain(last)
                nc.vector.tensor_copy(totals[:], upto[:, :, TE - 1]).then_inc(totals_ready, 1)
                dve.wait_ge(sums_ready, 1)
                chain(nc.vector.tensor_scalar(sups[:], counts_ps[:, NB:2 * NB], float(SUP - 1), None, ALU.add))
                chain(nc.vector.tensor_copy(sups_i[:], sups[:]))
                chain(nc.vector.tensor_single_scalar(sups_i[:], sups_i[:], SUP.bit_length() - 1,
                                                     op=ALU.arith_shift_right))
                chain(nc.vector.tensor_copy(sups[:], sups_i[:]))
                chain(nc.vector.tensor_tensor_scan(sup_end[:], onesrow[:, 0:NB], sups[:], 0.0, ALU.mult, ALU.add))
                chain(nc.vector.tensor_tensor(first[:], sup_end[:], sups[:], ALU.subtract))
                chain(nc.vector.tensor_scalar(first[:], first[:], float(SUP), -1.0, ALU.mult, ALU.add))
                chain(nc.vector.tensor_tensor(first[:], first[:], counts_ps[:, 0:NB], ALU.add))
                for b in range(NB):
                    chain(nc.vector.scalar_tensor_tensor(term[:] if b else place[:], upto[:, b, :], first[:, b:b + 1],
                                                         in_block[:, b, :], ALU.add, ALU.mult))
                    if b:
                        chain(nc.vector.tensor_tensor(place[:], place[:], term[:], ALU.add))
                chain(nc.vector.tensor_copy(place_i[:], place[:]))
                chain(nc.vector.tensor_single_scalar(tmp_i[:], place_i[:], 7, op=ALU.arith_shift_right))
                chain(nc.vector.tensor_copy(high[:], tmp_i[:]))
                chain(nc.vector.tensor_single_scalar(tmp_i[:], place_i[:], P - 1, op=ALU.bitwise_and))
                chain(nc.vector.tensor_copy(low[:], tmp_i[:]))
                dve.wait_ge(row_numbers, 1)
                chain(nc.vector.tensor_single_scalar(tmp_i[:], row_i[:], 7, op=ALU.arith_shift_right))
                chain(nc.vector.tensor_copy(row_high[:], tmp_i[:]))
                chain(nc.vector.tensor_single_scalar(tmp_i[:], row_i[:], P - 1, op=ALU.bitwise_and))
                chain(nc.vector.tensor_copy(row_low[:], tmp_i[:]))
                with dve.Fori(0, TE // GT) as i:
                    half = i % 2
                    dve.wait_ge(hot_used, i + 1)
                    for g in range(GT):
                        t = i * GT + g
                        nc.vector.tensor_scalar(hot_low[:, bass.ds(half, 1), g, :], c.iota_row[:],
                                                low[:, bass.ds(t, 1)], None, ALU.is_equal)
                        nc.vector.tensor_scalar(hot_row[:, bass.ds(half, 1), g, 0, :], c.iota_tile[:],
                                                high[:, bass.ds(t, 1)], row_high[:, bass.ds(t, 1)],
                                                ALU.is_equal, ALU.mult)
                        last = nc.vector.tensor_scalar(hot_row[:, bass.ds(half, 1), g, 1, :], c.iota_tile[:],
                                                       high[:, bass.ds(t, 1)], row_low[:, bass.ds(t, 1)],
                                                       ALU.is_equal, ALU.mult)
                    last.then_inc(hot_ready, 1)
                dve.wait_ge(perm_ready, 1)
                chain(nc.vector.tensor_copy(row_f[:], perm_ps[:, T:2 * T]))
                chain(nc.vector.scalar_tensor_tensor(row_f[:], perm_ps[:, 0:T], float(P), row_f[:],
                                                     ALU.mult, ALU.add))
                chain(nc.vector.tensor_copy(c.row_of_place[:], row_f[:]))
                chain(nc.vector.tensor_scalar(c.block_of_sup[:], c.iota_sup[:], sup_end[:, 0:1], None, ALU.is_ge))
                for b in range(1, NB - 1):
                    chain(nc.vector.tensor_scalar(sup_ge[:], c.iota_sup[:], sup_end[:, b:b + 1], None, ALU.is_ge))
                    chain(nc.vector.tensor_tensor(c.block_of_sup[:], c.block_of_sup[:], sup_ge[:], ALU.add))
                chain(nc.vector.tensor_copy(c.block_reg[:], c.block_of_sup[:]))

            @block.tensor
            def _(pe):
                pe.wait_ge(totals_ready, 1)
                nc.tensor.matmul(counts_ps[:, 0:NB], c.before[:], totals[:], start=True, stop=True)
                nc.tensor.matmul(counts_ps[:, NB:2 * NB], c.ones[:], totals[:], start=True, stop=True) \
                    .then_inc(sums_ready, 1)
                pe.wait_ge(zero_made, 2)
                nc.tensor.matmul(perm_ps[:], zero[:, 0:P], zero[:], start=True, stop=False).then_inc(hot_used, 2)
                with pe.Fori(0, TE // GT) as i:
                    pe.wait_ge(hot_ready, i + 1)
                    half = i % 2
                    for g in range(GT):
                        last = nc.tensor.matmul(perm_ps[:], hot_low[:, bass.ds(half, 1), g, :],
                                                hot_row[:, bass.ds(half, 1), g, :, :], start=False, stop=False)
                    last.then_inc(hot_used, 1)
                nc.tensor.matmul(perm_ps[:], zero[:, 0:P], zero[:], start=False, stop=True).then_inc(perm_ready, 1)


def build_adjacency(c):
    nc = c.nc
    turns = T // GT
    sups = GT // TPS
    c.recs = sbuf(c, "recs", [P, T, REC])
    c.i_local = sbuf(c, "i_local", [P, T])
    c.num_t = sbuf(c, "num_t", [P, NB, N])
    cleared, row_copied, copied, step, onehots, parts, built, added = (semaphore(c, n) for n in (
        "matrices_cleared", "row_number_copied", "record_copied", "adjacency_step", "onehots_ready",
        "weighted_ready", "block_built", "block_added"))
    slot_free, row_seen = semaphore(c, "record_slot_free"), semaphore(c, "row_number_seen")
    arrived = [semaphore(c, f"record_arrived_{g}") for g in range(GT)]
    stack = c.gcn_stack
    c.adj_t = sbuf(c, "adj_t", [P, NB, N], F32, stack)
    with ExitStack() as stack:
        sb = lambda name, shape, dtype=F32: sbuf(c, name, shape, dtype, stack)
        slots = sb("record_slots", [P, GT, REC])
        row_slots = sb("row_slots", [P, GT], I32)
        w_part = sb("w_part", [P, 3, 2, GT])
        w_rest = sb("w_rest", [P, GT])
        hot_j = sb("hot_j", [P, GT, N], BF16)
        hot_i = sb("hot_i", [P, GT, 4, P], BF16)
        built_ps = [psum(c, f"built_ps{b}", [P, NB, 2, P], stack) for b in range(2)]

        with nc.Block() as block:
            @block.gpsimd
            def _(pool):
                nc.gpsimd.memset(c.adj_t[:], 0.0).then_inc(cleared, 1)
                nc.gpsimd.memset(c.num_t[:], 0.0).then_inc(cleared, 1)
                with pool.Fori(0, turns) as i:
                    for g in range(GT):
                        pool.wait_ge(slot_free, i * GT + (g + 1))
                        nc.gpsimd.tensor_copy(row_slots[:, g:g + 1], c.row_of_place[:, bass.ds(i * GT + g, 1)]) \
                            .then_inc(row_copied, 1)
                        pool.wait_ge(row_copied, i * GT + (g + 1))
                        pool.sem_inc(row_seen, 1)
                        nc.gpsimd.indirect_dma_start(
                            slots[:, g, :], None, c.rows[:, :],
                            bass.IndirectOffsetOnAxis(ap=row_slots[:, g:g + 1], axis=0)).then_inc(arrived[g], 16)

            @block.scalar
            def _(act):
                def copy_records(i):
                    for g in range(GT):
                        act.wait_ge(arrived[g], i * 16 + 16)
                        nc.scalar.copy(c.recs[:, bass.ds(i * GT + g, 1), :], slots[:, g:g + 1, :]) \
                            .then_inc(copied, 1)
                        act.wait_ge(copied, i * GT + (g + 1))
                        act.sem_inc(slot_free, 1)

                def weigh(i):
                    for s in range(sups):
                        act.wait_ge(onehots, i * sups + (s + 1))
                        for t in range(TPS * s, TPS * s + TPS):
                            for part, at in enumerate((0, 2, 3)):
                                last = nc.scalar.activation(hot_i[:, t, at, :], hot_i[:, t, 1, :], ACT.Copy,
                                                            scale=w_part[:, part, 0, t:t + 1])
                        last.then_inc(parts, 1)

                act.sem_inc(slot_free, GT)
                copy_records(0)
                with act.Fori(0, turns - 1) as i:
                    copy_records(i + 1)
                    weigh(i)
                weigh(turns - 1)

            @block.vector
            def _(dve):
                chain, turn, close = chained(dve, step)

                def split_weights(i):
                    dve.wait_ge(copied, i * GT + GT)
                    rec = c.recs[:, bass.ds(i * GT, GT), :]
                    w1, w2, w3 = (w_part[:, n, 0, :] for n in range(3))
                    chain(nc.vector.tensor_single_scalar(w1.bitcast(I32), rec[:, :, R_W].bitcast(I32), -65536,
                                                         op=ALU.bitwise_and))
                    chain(nc.vector.tensor_tensor(w_rest[:], rec[:, :, R_W], w1, ALU.subtract))
                    chain(nc.vector.tensor_single_scalar(w2.bitcast(I32), w_rest[:].bitcast(I32), -65536,
                                                         op=ALU.bitwise_and))
                    chain(nc.vector.tensor_tensor(w3, w_rest[:], w2, ALU.subtract))
                    chain(nc.vector.scalar_tensor_tensor(
                        c.i_local[:, bass.ds(i * GT, GT)].rearrange("p (s k) -> p s k", k=TPS),
                        c.block_of_sup[:, bass.ds(i * sups, sups)].unsqueeze(2).to_broadcast([P, sups, TPS]),
                        -float(P), rec[:, :, R_I].rearrange("p (s k) -> p s k", k=TPS), ALU.mult, ALU.add))

                def one_hot(i, s):
                    t0 = TPS * s
                    nc.vector.tensor_tensor(
                        hot_i[:, t0:t0 + TPS, 1, :], c.iota_row[:].unsqueeze(1).to_broadcast([P, TPS, P]),
                        c.i_local[:, bass.ds(i * GT + t0, TPS)].unsqueeze(2).to_broadcast([P, TPS, P]), ALU.is_equal)
                    for t in range(t0, t0 + TPS):
                        last = nc.vector.tensor_scalar(hot_j[:, t, :], c.iota_node[:],
                                                       c.recs[:, bass.ds(i * GT + t, 1), R_J], None, ALU.is_equal)
                    last.then_inc(onehots, 1)

                def add_block(i, s):
                    k = dve.value_load(c.block_reg[0:1, bass.ds(i * sups + s, 1)], min_val=0, max_val=NB - 1)
                    dve.wait_ge(built, i * sups + (s + 1))
                    for n, m in enumerate((c.adj_t, c.num_t)):
                        to = m[:, :, bass.ds(k * P, P)]
                        ins = nc.vector.tensor_tensor(to, to, built_ps[s % 2][:, :, n, :], ALU.add)
                        chain(ins)
                    dve.sem_inc(added, 1)

                dve.wait_ge(cleared, 2)
                dve.sem_inc(added, 2)
                split_weights(0)
                for s in range(sups):
                    one_hot(0, s)
                with dve.Fori(0, turns - 1) as i:
                    turn(i, 5 + 2 * sups)
                    add_block(i, 0)
                    dve.wait_ge(parts, i * sups + sups)
                    split_weights(i + 1)
                    one_hot(i + 1, 0)
                    for s in range(1, sups):
                        add_block(i, s)
                        one_hot(i + 1, s)
                close(turns - 1)
                for s in range(sups):
                    add_block(turns - 1, s)

            @block.tensor
            def _(pe):
                with pe.Fori(0, turns) as i:
                    for s in range(sups):
                        pe.wait_ge(onehots, i * sups + (s + 1))
                        pe.wait_ge(parts, i * sups + (s + 1))
                        pe.wait_ge(added, i * sups + (s + 1))
                        for b in range(NB):
                            to = built_ps[s % 2]
                            for k in range(TPS):
                                t = TPS * s + k
                                hj = hot_j[:, t, b * P:(b + 1) * P]
                                nc.tensor.matmul(to[:, b, :, :], hj, hot_i[:, t, 0:2, :], start=(k == 0), stop=False)
                                nc.tensor.matmul(to[:, b, 0, :], hj, hot_i[:, t, 2, :], start=False, stop=False)
                                last = nc.tensor.matmul(to[:, b, 0, :], hj, hot_i[:, t, 3, :], start=False,
                                                        stop=(k == TPS - 1))
                        last.then_inc(built, 1)


def layer_norm(c, name, stack):
    nc = c.nc
    stats = sbuf(c, f"stats_{name}", [P, NB, 6], F32, stack)
    moments = sbuf(c, f"moments_{name}", [P, NB, 2], F32, stack)
    spread = sbuf(c, f"spread_{name}", [P, NB], F32, stack)
    measured, variance_ready, root_ready = (
        semaphore(c, f"{what}_{name}") for what in ("blocks_measured", "variance_ready", "roots_ready"))

    def measure(b, y):
        nc.vector.bn_stats(stats[:, b, :], y).then_inc(measured, 1)

    def root(act):
        act.wait_ge(variance_ready, 2)
        nc.scalar.activation(spread[:], spread[:], ACT.Sqrt).then_inc(root_ready, 1)

    def scale(dve, chain, y, out):
        dve.wait_ge(measured, NB)
        for b in range(NB):
            last = nc.vector.bn_aggr(moments[:, b, :], stats[:, b, :])
        last.then_inc(variance_ready, 1)
        dve.wait_ge(variance_ready, 1)
        nc.vector.tensor_scalar(spread[:], moments[:, :, 1], EPS, None, ALU.add).then_inc(variance_ready, 1)
        dve.wait_ge(root_ready, 1)
        chain(nc.vector.reciprocal(spread[:], spread[:]))
        for b in range(NB):
            last = nc.vector.tensor_scalar(out(b), y(b), moments[:, b, 0:1], spread[:, b:b + 1],
                                           ALU.subtract, ALU.mult)
        chain(last)

    return measure, root, scale, measured


def gcn(c):
    nc = c.nc
    layers = 2
    loaded, deg_ready, safe_ready, root_ready, scaled, agg_ready, agg_out, lin_ready, lin_out, mlp_ready, h_ready, \
        step, lin_free = (semaphore(c, n) for n in (
            "gcn_loaded", "degree_ready", "degree_safe", "degree_root", "gcn_scaled", "gcn_sums_ready",
            "gcn_sums_out", "gcn_linear_ready", "gcn_linear_out", "gcn_mlp_ready", "gcn_h_ready", "gcn_step",
            "gcn_mlp_free"))
    with ExitStack() as stack:
        sb = lambda name, shape, dtype=F32: sbuf(c, name, shape, dtype, stack)
        w_gcn = sb("w_gcn", [P, layers, FB, D])
        w_mlp = sb("w_mlp", [P, layers, FB, D])
        b_gcn = sb("b_gcn", [P, layers, FB])
        b_mlp = sb("b_mlp", [P, layers, D])
        h = sb("h", [P, 4, D])
        hs = sb("hs", [P, NB, D])
        root_b = sb("root_b", [P, N])
        root_p = sb("root_p", [P, NB])
        there_p = sb("there_p", [P, NB])
        agg = sb("agg", [P, FB, N])
        lin = sb("lin", [P, FB, N])
        there_b = agg[:, 0, :]
        measure, root, scale, measured = layer_norm(c, "gcn", stack)
        ps = [psum(c, f"gcn_ps{b}", [P, D], stack) for b in range(4)]
        deg_b = psum(c, "deg_b", [P, N], stack)
        deg_p = psum(c, "deg_p", [P, NB], stack)

        with nc.Block() as block:
            @block.sync
            def _(sp):
                sp.dma_start(c.x[:], c.ins["x"].rearrange("(b p) d -> p b d", p=P)).then_inc(loaded, 16)
                for l in range(layers):
                    sp.dma_start(w_gcn[:, l, :, :], c.ins["L0_gnn_W_gcn"][l].rearrange("(f p) o -> p f o", p=P)) \
                        .then_inc(loaded, 16)
                    sp.dma_start(w_mlp[:, l, :, :], c.ins["L0_gnn_W_mlp"][l].rearrange("(f p) o -> p f o", p=P)) \
                        .then_inc(loaded, 16)
                    sp.dma_start(b_gcn[:, l, :], c.ins["L0_gnn_b_gcn"][l].rearrange("(f p) -> p f", p=P), allow_slow_non_contiguous=True) \
                        .then_inc(loaded, 16)
                    sp.dma_start(b_mlp[:, l, :], c.ins["L0_gnn_b_mlp"][l].partition_broadcast(P)).then_inc(loaded, 16)
            all_loaded = 16 * (1 + 4 * layers)

            @block.tensor
            def _(pe):
                for half in range(2):
                    for b in range(NB):
                        nc.tensor.matmul(deg_b[:, half * D:half * D + D], c.ones[:],
                                         c.adj_t[:, b, half * D:half * D + D], start=(b == 0), stop=(b == NB - 1))
                for i in range(NB):
                    for b in range(NB):
                        last = nc.tensor.matmul(deg_p[:, i:i + 1], c.adj_t[:, b, i * P:i * P + P], c.ones[:, 0:1],
                                                start=(b == 0), stop=(b == NB - 1))
                last.then_inc(deg_ready, 1)
                for l in range(layers):
                    n = l * 2 * FB
                    for f in range(FB):
                        for half in range(2):
                            u = 2 * f + half
                            if u >= 4:
                                pe.wait_ge(agg_out, n + u - 3)
                            for b in range(NB):
                                pe.wait_ge(scaled, l * NB + b + 1)
                                last = nc.tensor.matmul(ps[u % 4][:], hs[:, b, f * P:f * P + P],
                                                        c.adj_t[:, b, half * D:half * D + D],
                                                        start=(b == 0), stop=(b == NB - 1))
                            last.then_inc(agg_ready, 1)
                    for half in range(2):
                        for f in range(FB):
                            u = half * FB + f
                            if u < 4:
                                pe.wait_ge(agg_out, n + 2 * FB)
                            else:
                                pe.wait_ge(lin_out, n + u - 3)
                            for k in range(FB):
                                last = nc.tensor.matmul(ps[u % 4][:], w_gcn[:, l, k, f * P:f * P + P],
                                                        agg[:, k, half * D:half * D + D],
                                                        start=(k == 0), stop=(k == FB - 1))
                            last.then_inc(lin_ready, 1)
                    for b in range(NB):
                        pe.wait_ge(lin_out, n + 2 * FB)
                        if b >= 4:
                            pe.wait_ge(lin_free, l * NB + b - 3)
                        for k in range(FB):
                            last = nc.tensor.matmul(ps[b % 4][:], lin[:, k, b * P:b * P + P], w_mlp[:, l, k, :],
                                                    start=(k == 0), stop=(k == FB - 1))
                        last.then_inc(mlp_ready, 1)
                    if l + 1 < layers:
                        pe.wait_ge(lin_free, l * NB + NB)

            @block.scalar
            def _(act):
                act.wait_ge(safe_ready, 2)
                nc.scalar.activation(root_b[:], root_b[:], ACT.Sqrt).then_inc(root_ready, 1)
                nc.scalar.activation(root_p[:], root_p[:], ACT.Sqrt).then_inc(root_ready, 1)
                act.wait_ge(loaded, all_loaded)
                for l in range(layers):
                    for half in range(2):
                        for f in range(FB):
                            u = half * FB + f
                            act.wait_ge(lin_ready, l * 2 * FB + u + 1)
                            if u == 0 and l:
                                act.wait_ge(mlp_ready, l * NB)
                            nc.scalar.activation(lin[:, f, half * D:half * D + D], ps[u % 4][:], ACT.Identity,
                                                 bias=b_gcn[:, l, f:f + 1]).then_inc(lin_out, 1)
                root(act)

            @block.vector
            def _(dve):
                chain, _, _ = chained(dve, step)
                dve.wait_ge(deg_ready, 1)
                for deg, there, root in ((deg_b, there_b, root_b), (deg_p, there_p[:], root_p)):
                    chain(nc.vector.tensor_scalar(there, deg[:], 0.0, None, ALU.is_gt))
                    chain(nc.vector.tensor_scalar(root[:], deg[:], 1e-30, None, ALU.max))
                    nc.vector.reciprocal(root[:], root[:]).then_inc(safe_ready, 1)
                dve.wait_ge(root_ready, 2)
                chain(nc.vector.tensor_tensor(root_b[:], root_b[:], there_b, ALU.mult))
                chain(nc.vector.tensor_tensor(root_p[:], root_p[:], there_p[:], ALU.mult))
                dve.wait_ge(loaded, all_loaded)
                for b in range(NB):
                    nc.vector.tensor_scalar(hs[:, b, :], c.x[:, b, :], root_p[:, b:b + 1], None, ALU.mult) \
                        .then_inc(scaled, 1)
                for l in range(layers):
                    for f in range(FB):
                        for half in range(2):
                            u = 2 * f + half
                            dve.wait_ge(agg_ready, l * 2 * FB + u + 1)
                            nc.vector.tensor_tensor(agg[:, f, half * D:half * D + D], ps[u % 4][:],
                                                    root_b[:, half * D:half * D + D], ALU.mult).then_inc(agg_out, 1)
                    for b in range(NB):
                        dve.wait_ge(mlp_ready, l * NB + b + 1)
                        nc.vector.tensor_tensor(h[:, b % 4, :], ps[b % 4][:], b_mlp[:, l, :], ALU.add) \
                            .then_inc(lin_free, 1)
                        dve.wait_ge(lin_free, l * NB + b + 1)
                        chain(nc.vector.scalar_tensor_tensor(h[:, b % 4, :], h[:, b % 4, :], 0.01, h[:, b % 4, :],
                                                             ALU.mult, ALU.max))
                        if l + 1 < layers:
                            nc.vector.tensor_scalar(hs[:, b, :], h[:, b % 4, :], root_p[:, b:b + 1], None, ALU.mult) \
                                .then_inc(scaled, 1)
                        else:
                            chain(nc.vector.tensor_tensor(c.x[:, b, :], c.x[:, b, :], h[:, b % 4, :], ALU.add))
                            measure(b, c.x[:, b, :])
                scale(dve, chain, lambda b: c.x[:, b, :], lambda b: c.x[:, b, :])


def gat(c):
    nc = c.nc
    AHEAD = 2
    SLOTS = 4
    PAIR = 2 * NB
    ON_POOL = (1, 4, 7)
    ON_DVE = tuple(b for b in range(NB) if b not in ON_POOL)
    SCORED0 = NB + SLOTS
    (loaded, copied, turned, turned_out, wx_ready, wx_out, prod_ready, reduced, set_up, lnready, cnt_ready, cnt_out,
     mask_t_made, diag_s, s_bcast, maxed, scores_done, step, diag_ready, bc_ready, bc_out, low_ready, scored,
     masked_dve, masked_pool, probs_ready, probs_used, heads_out, zero_made, pool_step, neg_ready, log_in,
     log_ready) = (semaphore(c, "gat_" + n) for n in (
         "loaded", "copied", "turned", "turned_out", "wx_ready", "wx_out", "products_ready", "reduced", "set_up",
         "logs_added", "counts_turned", "counts_out", "mask_t_made", "diag_s", "s_broadcast", "maxed",
         "scores_done", "step", "diag_ready", "broadcast", "broadcast_out", "low_slope", "scored", "masked_dve",
         "masked_pool", "probs_ready", "probs_used", "heads_out", "zero_made", "pool_step", "nonedges",
         "log_in", "log_ready"))
    with ExitStack() as outer:
        sbo = lambda name, shape, dtype=F32: sbuf(c, name, shape, dtype, outer)
        wx = sbo("wx", [P, NB, HEADS, DH + 1])
        s_i = sbo("s_i", [P, HEADS, NB])
        s_low = sbo("s_low", [P, HEADS, NB])
        t_j = sbo("t_j", [P, HEADS, NB])
        top = sbo("top", [P, HEADS, NB])
        arg = sbo("arg", [P, 2, HEADS, NB])
        a_b = sbo("a_b", [P, HEADS])
        log_num = sbo("log_num", [P, NB, N])
        zero = sbo("zero_gat", [P, 4 * (DH + 1)], BF16)
        measure, root, scale, measured = layer_norm(c, "gat", outer)

        with ExitStack() as stack, nc.Block() as block:
            sb = lambda name, shape, dtype=F32: sbuf(c, name, shape, dtype, stack)
            w_s = sb("w_s", [P, FB, HEADS, DH])
            w_b = sb("w_b", [P, D])
            a_w = sb("a_w", [P, HEADS, 2 * DH])
            x_t = sb("x_t", [P, FB, N])
            prod = sb("prod", [P, 2, 2, D])
            mask_t = sb("mask_t", [P, NB, N])
            diag = sb("diag", [P, 4, 4, P])
            junk = x_t[:, 0, :]
            atleast = x_t[:, 1, :].rearrange("p (u d) -> p u d", u=2)
            ps = [psum(c, f"gat_ps{b}", [P, 4, P], stack) for b in range(4)]
            s_ps = [psum(c, f"s_ps{b}", [P, N], stack) for b in range(2)]

            @block.sync
            def _(sp):
                for h in range(HEADS):
                    sp.dma_start(w_s[:, :, h, :], c.ins["L1_gnn_Ws"][h].rearrange("(f p) d -> p f d", p=P)) \
                        .then_inc(loaded, 16)
                sp.dma_start(w_b[:], c.ins["L1_gnn_Wb"].rearrange("h d -> (h d)").partition_broadcast(P)) \
                    .then_inc(loaded, 16)
                sp.dma_start(a_w[:], c.ins["L1_gnn_a_w"].partition_broadcast(P)).then_inc(loaded, 16)
                sp.dma_start(a_b[:], c.ins["L1_gnn_a_b"].partition_broadcast(P)).then_inc(loaded, 16)
            all_loaded = 16 * (HEADS + 3)

            @block.tensor
            def _(pe):
                for b in range(NB):
                    if b >= 4:
                        pe.wait_ge(turned_out, b - 3)
                    for f in range(FB):
                        last = nc.tensor.transpose(ps[b % 4][:, f, :], c.x[:, b, f * P:f * P + P], c.ident[:])
                    last.then_inc(turned, 1)
                pe.wait_ge(turned_out, NB)
                pe.wait_ge(loaded, all_loaded)
                for b in range(NB):
                    if b >= 4:
                        pe.wait_ge(wx_out, b - 3)
                    for f in range(FB):
                        last = nc.tensor.matmul(ps[b % 4][:], x_t[:, f, b * P:b * P + P], w_s[:, f, :, :],
                                                start=(f == 0), stop=(f == FB - 1))
                    last.then_inc(wx_ready, 1)
                pe.wait_ge(wx_out, NB)
                for u in range(2 * NB):
                    if u >= 4:
                        pe.wait_ge(cnt_out, 2 * (u - 3))
                    i, half = u // 2, u % 2
                    for j in range(4):
                        last = nc.tensor.transpose(ps[u % 4][:, j, :], c.num_t[:, 4 * half + j, i * P:i * P + P],
                                                   c.ident[:])
                    last.then_inc(cnt_ready, 1)
                for h in range(HEADS):
                    if h >= 2:
                        pe.wait_ge(maxed, NB * (h - 1))
                    for half in range(2):
                        u = 2 * h + half
                        pe.wait_ge(diag_s, u + 1)
                        nc.tensor.matmul(s_ps[h % 2][:, half * D:half * D + D], c.ones[:], diag[:, u % 4, :, :],
                                         start=True, stop=True).then_inc(s_bcast, 1)

            @block.scalar
            def _(act):
                for b in range(NB):
                    act.wait_ge(turned, b + 1)
                    nc.scalar.copy(x_t[:, :, b * P:b * P + P], ps[b % 4][:]).then_inc(turned_out, 1)
                for u in range(2 * NB):
                    i, half = u // 2, u % 2
                    act.wait_ge(cnt_out, 2 * u + 2)
                    nc.scalar.activation(atleast[:, u % 2, :], atleast[:, u % 2, :], ACT.Ln).then_inc(log_ready, 1)

            @block.gpsimd
            def _(pool):
                nc.gpsimd.memset(wx[:, :, :, DH:DH + 1], 1.0).then_inc(set_up, 1)
                nc.gpsimd.memset(zero[:], 0.0).then_inc(set_up, 1)
                for b in range(NB):
                    nc.gpsimd.tensor_scalar(mask_t[:, b, :], c.num_t[:, b, :], 0.5, -BIG, ALU.is_lt, ALU.mult) \
                        .then_inc(mask_t_made, 1)
                pool.wait_ge(loaded, all_loaded)
                for b in range(NB):
                    pool.wait_ge(wx_out, b + 1)
                    if b >= 2:
                        pool.wait_ge(reduced, 2 * (b - 1))
                    for n in range(2):
                        nc.gpsimd.tensor_tensor(prod[:, b % 2, n, :].rearrange("p (h d) -> p h d", d=DH),
                                                wx[:, b, :, 0:DH], a_w[:, :, n * DH:n * DH + DH], ALU.mult) \
                            .then_inc(prod_ready, 1)
                pool.wait_ge(reduced, 2 * NB)
                def s_diagonals(units):
                    for u in units:
                        h, half = u // 2, u % 2
                        if u >= 4:
                            pool.wait_ge(s_bcast, u - 3)
                        nc.gpsimd.tensor_tensor(diag[:, u % 4, :, :], c.ident[:].unsqueeze(1).to_broadcast([P, 4, P]),
                                                s_i[:, h, 4 * half:4 * half + 4].unsqueeze(2).to_broadcast([P, 4, P]),
                                                ALU.mult).then_inc(diag_s, 1)

                s_diagonals(range(4))
                for u in range(2 * NB):
                    i, half = u // 2, u % 2
                    pool.wait_ge(log_ready, u + 1)
                    nc.gpsimd.tensor_tensor(log_num[:, i, half * D:half * D + D],
                                            log_num[:, i, half * D:half * D + D], atleast[:, u % 2, :],
                                            ALU.add).then_inc(lnready, 1)
                s_diagonals(range(4, 2 * HEADS))

            @block.vector
            def _(dve):
                chain, _, _ = chained(dve, step)
                dve.wait_ge(loaded, all_loaded)
                dve.wait_ge(set_up, 1)

                def reduce(b):
                    for n, term in enumerate((t_j, s_i)):
                        dve.wait_ge(prod_ready, 2 * b + n + 1)
                        nc.vector.tensor_reduce(term[:, :, b], prod[:, b % 2, n, :].rearrange("p (h d) -> p h d", d=DH),
                                                AX, ALU.add).then_inc(reduced, 1)

                for b in range(NB):
                    dve.wait_ge(wx_ready, b + 1)
                    nc.vector.tensor_tensor(wx[:, b, :, 0:DH], ps[b % 4][:].rearrange("p a (g d) -> p (a g) d", d=DH),
                                            w_b[:].rearrange("p (h d) -> p h d", d=DH), ALU.add).then_inc(wx_out, 1)
                    if b:
                        reduce(b - 1)
                reduce(NB - 1)
                for u in range(2 * NB):
                    i, half = u // 2, u % 2
                    dve.wait_ge(cnt_ready, u + 1)
                    if u >= 2:
                        dve.wait_ge(lnready, u - 1)
                    got = ps[u % 4][:].rearrange("p a b -> p (a b)")
                    nc.vector.tensor_scalar(log_num[:, i, half * D:half * D + D], got, 0.5, -BIG, ALU.is_lt,
                                            ALU.mult).then_inc(cnt_out, 1)
                    nc.vector.tensor_scalar(atleast[:, u % 2, :], got, 1.0, None, ALU.max).then_inc(cnt_out, 1)
                dve.wait_ge(mask_t_made, NB)
                for h in range(HEADS):
                    dve.wait_ge(s_bcast, 2 * h + 2)
                    for b in range(NB):
                        dve.wait_ge(maxed, h * NB + b) if h + b else None
                        nc.vector.tensor_tensor_reduce(out=junk, in0=s_ps[h % 2][:], in1=mask_t[:, b, :], scale=1.0,
                                                       scalar=-3e38, op0=ALU.add, op1=ALU.max,
                                                       accum_out=top[:, h, b:b + 1]).then_inc(maxed, 1)
                dve.wait_ge(maxed, HEADS * NB)
                chain(nc.vector.tensor_tensor(t_j[:], t_j[:], a_b[:].unsqueeze(2).to_broadcast([P, HEADS, NB]),
                                              ALU.add))
                chain(nc.vector.tensor_tensor(top[:], top[:], t_j[:], ALU.add))
                chain(nc.vector.scalar_tensor_tensor(top[:], top[:], 0.2, top[:], ALU.mult, ALU.max))
                chain(nc.vector.tensor_tensor(arg[:, 0, :, :], t_j[:], top[:], ALU.subtract))
                chain(nc.vector.scalar_tensor_tensor(arg[:, 1, :, :], t_j[:], 0.2, top[:], ALU.mult, ALU.subtract))
                chain(nc.vector.tensor_scalar(s_low[:], s_i[:], 0.2, None, ALU.mult))

        with ExitStack() as stack, nc.Block() as block:
            sb = lambda name, shape, dtype=F32: sbuf(c, name, shape, dtype, stack)
            diag = sb("diag2", [P, 4, 4, P])
            args = sb("args", [P, 2, 2, N])
            low = sb("low_slope", [P, SLOTS, N])
            score = sb("score", [P, SLOTS, N])
            prob = sb("prob", [P, SLOTS, N])
            head = sb("head", [P, NB, DH])
            den = sb("den", [P, 2, NB])
            bc_ps = [psum(c, f"bc_ps{b}", [P, D], stack) for b in range(2)]
            pv_ps = [psum(c, f"pv_ps{b}", [P, 2, D], stack) for b in range(2)]
            turns = HEADS // 2

            @block.gpsimd
            def _(pool):
                def diagonals(i, h):
                    for u in range(4):
                        pool.wait_ge(bc_ready, i * 8 + (4 * h + u + 1))
                        nc.gpsimd.tensor_tensor(
                            diag[:, u, :, :], c.ident[:].unsqueeze(1).to_broadcast([P, 4, P]),
                            arg[:, u // 2, bass.ds(i * 2 + h, 1), 4 * (u % 2):4 * (u % 2) + 4]
                            .rearrange("p o b -> p (o b)").unsqueeze(2).to_broadcast([P, 4, P]), ALU.mult) \
                            .then_inc(diag_ready, 1)

                def pair(i, ends=False):
                    for h in range(2):
                        if not (ends and h):
                            diagonals(i, h + 1)
                        for b in ON_POOL:
                            n = NB * h + b
                            pool.wait_ge(scored, i * PAIR + (SCORED0 + n + 1))
                            nc.gpsimd.tensor_tensor(score[:, b % SLOTS, :], score[:, b % SLOTS, :], log_num[:, b, :],
                                                    ALU.add).then_inc(masked_pool, 1)

                diagonals(0, 0)
                with pool.Fori(0, turns - 1) as i:
                    pair(i)
                pair(turns - 1, True)

            @block.tensor
            def _(pe):
                pe.sem_inc(bc_ready, 4)

                def broadcast(i, h, u):
                    pe.wait_ge(diag_ready, i * 8 + (4 * h + u + 1))
                    pe.wait_ge(bc_out, i * 8 + (4 * h + u + 1))
                    nc.tensor.matmul(bc_ps[u % 2][:], c.ones[:], diag[:, u, :, :], start=True, stop=True) \
                        .then_inc(bc_ready, 1)

                def pair(i, ends=False):
                    for h in range(2):
                        pe.wait_ge(heads_out, i * 2 + (h + 1))
                        for bank in range(2):
                            nc.tensor.matmul(pv_ps[h][:, bank, 0:4 * (DH + 1)], zero[:, 0:P], zero[:],
                                             start=True, stop=False)
                        for b in range(NB):
                            pe.wait_ge(probs_ready, i * PAIR + (NB * h + b + SLOTS + 1))
                            for j in range(NB):
                                at = (j % 4) * (DH + 1)
                                last = nc.tensor.matmul(pv_ps[h][:, j // 4, at:at + DH + 1],
                                                        prob[:, b % SLOTS, j * P:j * P + P],
                                                        wx[:, b, bass.ds(i * 2 + h, 1), :],
                                                        start=False, stop=(b == NB - 1 and j % 4 == 3))
                            last.then_inc(probs_used, 1)
                            if b < 4 and not (ends and h):
                                broadcast(i, h + 1, b)

                for u in range(4):
                    broadcast(0, 0, u)
                with pe.Fori(0, turns - 1) as i:
                    pair(i)
                pair(turns - 1, True)

            @block.scalar
            def _(act):
                def take(i, h, u):
                    act.wait_ge(bc_ready, i * 8 + (4 * h + u + 5))
                    act.wait_ge(scored, i * PAIR + (NB * h + SLOTS))
                    nc.scalar.copy(args[:, h % 2, u // 2, (u % 2) * D:(u % 2) * D + D], bc_ps[u % 2][:]) \
                        .then_inc(bc_out, 1)

                def low_slope(i, n):
                    h, b = n // NB, n % NB
                    act.wait_ge(bc_out, i * 8 + (4 * h + 6))
                    act.wait_ge(scored, i * PAIR + (n + 1 + SCORED0 - SLOTS))
                    nc.scalar.activation(low[:, b % SLOTS, :], args[:, h % 2, 1, :], ACT.Identity,
                                         bias=s_low[:, bass.ds(i * 2 + h, 1), b]).then_inc(low_ready, 1)

                def exponential(i, n):
                    h, b = n // NB, n % NB
                    if b in ON_POOL:
                        act.wait_ge(masked_pool, i * (2 * len(ON_POOL)) + (len(ON_POOL) * h + ON_POOL.index(b) + 1))
                    else:
                        act.wait_ge(masked_dve, i * (2 * len(ON_DVE)) + (len(ON_DVE) * h + ON_DVE.index(b) + 1))
                    act.wait_ge(probs_used, i * PAIR + (n + 1))
                    nc.scalar.activation(prob[:, b % SLOTS, :], score[:, b % SLOTS, :], ACT.Exp) \
                        .then_inc(probs_ready, 1)

                def pair(i, ends=False):
                    for n in range(PAIR):
                        h, b = n // NB, n % NB
                        if 1 <= b <= 4 and not (ends and h):
                            take(i, h + 1, b - 1)
                        if not (ends and n + AHEAD >= PAIR):
                            low_slope(i, n + AHEAD)
                        exponential(i, n)

                act.sem_inc(bc_out, 2)
                act.sem_inc(probs_ready, SLOTS)
                act.sem_inc(probs_used, SLOTS)
                for u in range(4):
                    take(0, 0, u)
                for n in range(AHEAD):
                    low_slope(0, n)
                with act.Fori(0, turns - 1) as i:
                    pair(i)
                pair(turns - 1, True)
                root(act)

            @block.vector
            def _(dve):
                chain, turn, close = chained(dve, pool_step)
                dve.sem_inc(scored, SCORED0)
                dve.sem_inc(heads_out, 2)

                def make_score(i, n):
                    h, b = n // NB, n % NB
                    dve.wait_ge(low_ready, i * PAIR + (n + 1))
                    dve.wait_ge(probs_ready, i * PAIR + (n + 1))
                    nc.vector.scalar_tensor_tensor(score[:, b % SLOTS, :], args[:, h, 0, :],
                                                   s_i[:, bass.ds(i * 2 + h, 1), b], low[:, b % SLOTS, :],
                                                   ALU.add, ALU.max).then_inc(scored, 1)

                def mask(i, n):
                    b = n % NB
                    dve.wait_ge(scored, i * PAIR + (SCORED0 + n + 1))
                    nc.vector.tensor_tensor(score[:, b % SLOTS, :], score[:, b % SLOTS, :], log_num[:, b, :],
                                            ALU.add).then_inc(masked_dve, 1)

                def divide(i, h):
                    got = pv_ps[h][:, :, 0:4 * (DH + 1)].rearrange("p k (j d) -> p k j d", d=DH + 1)
                    d = den[:, h, :].rearrange("p (k j) -> p k j", j=4)
                    chain(nc.vector.tensor_scalar(d, got[:, :, :, DH], 1e-30, None, ALU.max))
                    chain(nc.vector.reciprocal(d, d))
                    nc.vector.tensor_tensor(head[:].rearrange("p (k j) d -> p k j d", j=4), got[:, :, :, 0:DH],
                                            d.unsqueeze(3).to_broadcast([P, 2, 4, DH]), ALU.mult) \
                        .then_inc(heads_out, 1)
                    dve.wait_ge(heads_out, i * 2 + (h + 3))
                    to = c.x[:, :, bass.ds(i * (2 * DH) + h * DH, DH)]
                    chain(nc.vector.tensor_tensor(to, to, head[:], ALU.add))

                def pair(i, before=None):
                    for n in range(PAIR):
                        make_score(i, n)
                        if n % NB and (n - 1) % NB in ON_DVE:
                            mask(i, n - 1)
                        if n == NB + 2:
                            dve.wait_ge(probs_used, i * PAIR + (NB + SLOTS))
                            divide(i, 0)
                        if n % NB == NB - 1 and NB - 1 in ON_DVE:
                            mask(i, n)
                    dve.wait_ge(probs_used, i * PAIR + (PAIR + SLOTS))
                    divide(i, 1)

                with dve.Fori(0, turns) as i:
                    turn(i, 6)
                    pair(i)
                close(turns)
                for b in range(NB):
                    measure(b, c.x[:, b, :])
                scale(dve, chain, lambda b: c.x[:, b, :], lambda b: c.x[:, b, :])


HID = 32
Q_AT, P1_AT, X_AT = 0, HID, HID + 3 * MUL
ROW = X_AT + D
FAR = ROW - P1_AT
LAGS = 4


def staged(engine, stages):
    for u in range(LAGS):
        for lag, stage in stages:
            if u >= lag:
                stage(u - lag, (u - lag) % 4, (u - lag) // 4)
    with engine.Fori(0, (S - LAGS) // 4) as i:
        for k in range(4):
            for lag, stage in stages:
                ahead = LAGS + k - lag
                stage(i * 4 + ahead, ahead % 4, i + ahead // 4)
    for u in range(S, S + LAGS):
        for lag, stage in stages:
            if u - lag < S:
                stage(u - lag, (u - lag) % 4, (u - lag) // 4)


def interaction(c):
    nc = c.nc
    with ExitStack() as stack:
        c.far = nc.dram_tensor("far_rows", [N, FAR], F32, kind="Internal").ap()
        c.table = sbuf(c, "table", [P, NB, ROW], F32, stack)
        c.w_o = sbuf(c, "w_o", [P, 2, MUL], F32, stack)
        c.b_o = sbuf(c, "b_o", [P, MUL], F32, stack)
        c.w_s1 = sbuf(c, "w_s1", [P, 3, HID], F32, stack)
        c.w_f1 = sbuf(c, "w_f1", [HID, HID], F32, stack)
        c.w_2 = sbuf(c, "w_2", [2 * HID, 4 * MUL], F32, stack)
        interaction_nodes(c)
        c.sums = sbuf(c, "sums", [P, NB, D], F32, stack)
        interaction_edges(c)
        interaction_out(c)


def interaction_nodes(c):
    nc = c.nc
    (loaded, turned, turned_out, step, square_ready, norm_ready, g1_ready, g1_out, act_ready, hid_ready, g2_ready,
     g_ready, xg_ready, p0_ready, p0_out, near_ready, near_out, self_ready, table_ready, stored, exp_ready) = (
        semaphore(c, "node_" + n) for n in (
            "loaded", "turned", "turned_out", "step", "square_ready", "norm_ready", "g1_ready", "g1_out",
            "neg_bias", "hidden_ready", "g2_ready", "g_ready", "gated", "p0_ready", "p0_out", "near_ready",
            "near_out", "self_ready", "table_ready", "stored", "exp_ready"))
    with ExitStack() as stack, nc.Block() as block:
        sb = lambda name, shape, dtype=F32: sbuf(c, name, shape, dtype, stack)
        w_pre = sb("w_pre", [P, 2, MUL])
        w_nd = sb("w_nd", [P, 2, MUL])
        w_g = sb("w_g", [P, 2, 2, 2 * MUL])
        b_g = sb("b_g", [P, 2, 2])
        b_g_neg = sb("b_g_neg", [P, 2])
        b_pre = sb("b_pre", [P, 1])
        b_nd = sb("b_nd", [P, MUL])
        x_t = sb("x_t4", [P, 4, N])
        length = sb("length", [P, N])
        hidden = sb("hidden", [P, 2, N])
        gate = sb("gate", [P, 2, N])
        expo = sb("expo", [P, 2, D])
        p0_t = sb("p0_t", [P, N])
        ps = [psum(c, f"node_ps{b}", [P, D], stack) for b in range(8)]
        cols = dict(allow_slow_non_contiguous=True)

        @block.sync
        def _(sp):
            loads = [(w_pre[:, 0, :], "W_pre0"), (w_pre[:, 1, :], "W_pre1"), (w_nd[:, 0, :], "W_nd0"),
                     (w_nd[:, 1, :], "W_nd1"), (c.w_o[:, 0, :], "W_o0"), (c.w_o[:, 1, :], "W_o1"),
                     (c.w_f1[:], "W_f1"), (c.w_2[0:HID, :], "W_f2"), (c.w_2[HID:2 * HID, :], "W_s2")]
            for to, name in loads:
                sp.dma_start(to, c.ins["L2_gnn_" + name]).then_inc(loaded, 16)
            sp.dma_start(c.w_s1[:], c.ins["L2_gnn_W_s1"].rearrange("(a p) h -> p a h", p=P)).then_inc(loaded, 16)
            for n, name in enumerate(("g1", "g2")):
                sp.dma_start(w_g[:, n, :, :], c.ins["L2_gnn_W_" + name].rearrange("(a p) h -> p a h", p=P)) \
                    .then_inc(loaded, 16)
                sp.dma_start(b_g[:, n, :], c.ins["L2_gnn_b_" + name].rearrange("(a p) -> p a", p=P), **cols) \
                    .then_inc(loaded, 16)
            sp.dma_start(b_pre[:], c.ins["L2_gnn_b_pre0"].rearrange("(a p) -> p a", p=P), **cols) \
                .then_inc(loaded, 16)
            sp.dma_start(b_nd[:], c.ins["L2_gnn_b_nd0"].partition_broadcast(P)).then_inc(loaded, 16)
            sp.dma_start(c.b_o[:], c.ins["L2_gnn_b_o0"].partition_broadcast(P)).then_inc(loaded, 16)
            sp.wait_ge(near_out, NB)
            sp.wait_ge(table_ready, NB)
            sp.dma_start(c.far.rearrange("(b p) r -> p b r", p=P), c.table[:, :, P1_AT:ROW]).then_inc(stored, 16)
            sp.wait_ge(stored, 16)
        all_loaded = 16 * 17

        @block.tensor
        def _(pe):
            for b in range(NB):
                if b >= 4:
                    pe.wait_ge(turned_out, b - 3)
                to = ps[b % 4][:].rearrange("p (f n) -> p f n", f=4)
                nc.tensor.transpose(to[:, 0, :], c.x[:, b, 0:MUL], c.ident[:])
                vectors = c.x[:, b, MUL:D].rearrange("p (u m) -> p m u", m=3)
                for m in range(3):
                    last = nc.tensor.transpose(to[:, 1 + m, :], vectors[:, m, :], c.ident[:])
                last.then_inc(turned, 1)
            pe.wait_ge(turned_out, NB)
            pe.wait_ge(loaded, all_loaded)
            for half in range(2):
                nc.tensor.matmul(ps[4 + half][:], w_pre[:, 0, :], x_t[:, 0, half * D:half * D + D],
                                 start=True, stop=True).then_inc(p0_ready, 1)
            pe.wait_ge(norm_ready, 1)
            for o in range(2):
                for half in range(2):
                    cut = slice(half * D, half * D + D)
                    nc.tensor.matmul(ps[2 * o + half][:], w_g[:, 0, 0, o * P:o * P + P], x_t[:, 0, cut],
                                     start=True, stop=False)
                    nc.tensor.matmul(ps[2 * o + half][:], w_g[:, 0, 1, o * P:o * P + P], length[:, cut],
                                     start=False, stop=True).then_inc(g1_ready, 1)
            pe.wait_ge(p0_out, 2)
            for b in range(NB):
                if b >= 4:
                    pe.wait_ge(near_out, b - 3)
                to, cut = ps[4 + b % 4], slice(b * P, b * P + P)
                nc.tensor.matmul(to[:, Q_AT:Q_AT + HID], p0_t[:, cut], c.w_s1[:, 0, :], start=True, stop=False)
                nc.tensor.matmul(to[:, Q_AT:Q_AT + HID], p0_t[:, cut], c.w_s1[:, 1, :], start=False, stop=True)
                for m in range(3):
                    last = nc.tensor.matmul(to[:, P1_AT + m * MUL:P1_AT + (m + 1) * MUL], x_t[:, 1 + m, cut],
                                            w_pre[:, 1, :], start=True, stop=True)
                last.then_inc(near_ready, 1)
            pe.wait_ge(hid_ready, 4)
            for o in range(2):
                for half in range(2):
                    for k in range(2):
                        last = nc.tensor.matmul(ps[2 * o + half][:], w_g[:, 1, k, o * P:o * P + P],
                                                hidden[:, k, half * D:half * D + D], start=(k == 0), stop=(k == 1))
                    last.then_inc(g2_ready, 1)
            pe.wait_ge(g_ready, 4)
            pe.wait_ge(xg_ready, 3)
            for b in range(NB):
                if b >= 4:
                    pe.wait_ge(table_ready, b - 3)
                to, cut = ps[b % 4], slice(b * P, b * P + P)
                nc.tensor.matmul(to[:, 0:MUL], gate[:, 0, cut], w_nd[:, 0, :], start=True, stop=True)
                for m in range(3):
                    last = nc.tensor.matmul(to[:, (1 + m) * MUL:(2 + m) * MUL], x_t[:, 1 + m, cut], w_nd[:, 1, :],
                                            start=True, stop=True)
                last.then_inc(self_ready, 1)

        @block.scalar
        def _(act):
            for b in range(NB):
                act.wait_ge(turned, b + 1)
                nc.scalar.copy(x_t[:, :, b * P:b * P + P], ps[b % 4][:].rearrange("p (f n) -> p f n", f=4)) \
                    .then_inc(turned_out, 1)
            act.wait_ge(loaded, all_loaded)
            for half in range(2):
                act.wait_ge(p0_ready, half + 1)
                nc.scalar.activation(p0_t[:, half * D:half * D + D], ps[4 + half][:], ACT.Identity,
                                     bias=b_pre[:, 0:1]).then_inc(p0_out, 1)
            act.wait_ge(square_ready, 1)
            nc.scalar.activation(length[:], length[:], ACT.Sqrt, scale=1.0 / 3.0).then_inc(norm_ready, 1)
            act.wait_ge(act_ready, 1)
            for o in range(2):
                for half in range(2):
                    u = 2 * o + half
                    act.wait_ge(g1_ready, u + 1)
                    if u >= 2:
                        act.wait_ge(hid_ready, u - 1)
                    nc.scalar.activation(expo[:, half, :], ps[u][:], ACT.Exp, bias=b_g_neg[:, o:o + 1],
                                         scale=-1.0).then_inc(exp_ready, 1)
            for b in range(NB):
                act.wait_ge(near_ready, b + 1)
                nc.scalar.copy(c.table[:, b, 0:X_AT], ps[4 + b % 4][:, 0:X_AT]).then_inc(near_out, 1)
            for o in range(2):
                for half in range(2):
                    u = 2 * o + half
                    act.wait_ge(g2_ready, u + 1)
                    nc.scalar.activation(gate[:, o, half * D:half * D + D], ps[u][:], ACT.Identity,
                                         bias=b_g[:, 1, o:o + 1]).then_inc(g_ready, 1)

        @block.vector
        def _(dve):
            chain, _, _ = chained(dve, step)
            dve.wait_ge(loaded, all_loaded)
            nc.vector.tensor_scalar(b_g_neg[:], b_g[:, 0, :], -1.0, None, ALU.mult).then_inc(act_ready, 1)
            chain(nc.vector.tensor_scalar(c.w_2[0:HID, 3 * MUL:], c.w_2[0:HID, 3 * MUL:], 3.0 ** -0.5, None,
                                          ALU.mult))
            dve.wait_ge(turned_out, NB)
            chain(nc.vector.tensor_tensor(length[:], x_t[:, 1, :], x_t[:, 1, :], ALU.mult))
            square = hidden[:, 0, :]
            for m in (2, 3):
                chain(nc.vector.tensor_tensor(square, x_t[:, m, :], x_t[:, m, :], ALU.mult))
                last = nc.vector.tensor_tensor(length[:], length[:], square, ALU.add)
                if m == 2:
                    chain(last)
            last.then_inc(square_ready, 1)
            for o in range(2):
                for half in range(2):
                    u = 2 * o + half
                    dve.wait_ge(exp_ready, u + 1)
                    e = expo[:, half, :]
                    chain(nc.vector.tensor_scalar(e, e, 1.0, None, ALU.add))
                    chain(nc.vector.reciprocal(e, e))
                    nc.vector.scalar_tensor_tensor(hidden[:, o, half * D:half * D + D], ps[u][:],
                                                   b_g[:, 0, o:o + 1], e, ALU.add, ALU.mult).then_inc(hid_ready, 1)
            dve.wait_ge(near_ready, NB)
            dve.wait_ge(g_ready, 4)
            for m in range(3):
                nc.vector.tensor_tensor(x_t[:, 1 + m, :], x_t[:, 1 + m, :], gate[:, 1, :], ALU.mult) \
                    .then_inc(xg_ready, 1)
            for b in range(NB):
                dve.wait_ge(self_ready, b + 1)
                chain(nc.vector.tensor_tensor(c.table[:, b, X_AT:X_AT + MUL], ps[b % 4][:, 0:MUL], b_nd[:], ALU.add))
                nc.vector.tensor_copy(c.table[:, b, X_AT + MUL:ROW], ps[b % 4][:, MUL:D]).then_inc(table_ready, 1)


def interaction_edges(c):
    nc = c.nc
    FIRST = dict(turned_out=1, attr_out=1, near=2, prod=1, q_out=1, ip=4, ip_turned=2, ip_out=1, hid=4, shifted=1,
                 filt_s=4, f_out=2, weights=2, thirds=4, msgs=4, sums=4, added=1,
                 attr_turned=4)
    (hot_ready, turned, turned_out, attr_turned, attr_out, near, prod_ready, q_out, ip_ready, ip_turned, ip_out,
     hid_ready, soft_ready, soft_shifted, filt_f, filt_s, f_out, weights_ready, thirds_ready, msgs_ready,
     sums_ready, sums_added, step, index_copied, index_seen, index_made, sums_cleared, attr_ready,
     soft_step) = (
         semaphore(c, "edge_" + n) for n in (
             "onehot_ready", "turned", "turned_out", "attributes_turned", "attributes_out", "near_ready",
             "product_ready", "near_scalar_out", "inner_ready", "inner_turned", "inner_out", "hidden_ready",
             "softplus_ready", "softplus_shifted", "filter_f", "filter_s", "filter_f_out", "weights_ready",
             "thirds_ready", "messages_ready", "sums_ready", "sums_added", "step", "index_copied", "index_seen",
             "indices_made", "sums_cleared", "attributes_ready", "softplus_step"))
    arrived = [semaphore(c, f"far_row_arrived_{g}") for g in range(4 * TPS)]
    STEPS = 5
    with ExitStack() as stack, nc.Block() as block:
        sb = lambda name, shape, dtype=F32: sbuf(c, name, shape, dtype, stack)
        far_node = sb("far_node", [P, T], I32)
        index = sb("far_index", [P, 4 * TPS], I32)
        far = sb("far", [P, 4, TPS, FAR])
        hot = sb("hot", [P, 4, TPS, P])
        attr = sb("attr", [P, 4, TPS, 32])
        half = sb("half", [P, 1])
        attr_t = sb("attr_t", [HID, 4, TPS * P])
        hot_t = sb("hot_t", [P, 2, TPS, P])
        prod = sb("prod_i", [P, 2, TPS, 3, MUL])
        q = sb("q", [P, 2, TPS, HID])
        inner = sb("inner", [P, 2, TPS, MUL])
        inner_t = sb("inner_t", [P, 2, TPS * P])
        soft = sb("soft", [2 * HID, 2, TPS * P])
        filt = sb("filt", [P, 2, TPS, 4, MUL])
        weight = sb("weight_e", [P, 2, TPS, 4, MUL])
        msg = sb("msg", [P, 2, TPS, 4, MUL])
        firsts = sb("firsts", [P, TPS, 2, MUL])
        dot = sb("dot", [P, TPS, MUL])
        near_ps = psum(c, "near_ps", [P, TPS, D], stack)
        turn_ps = psum(c, "turn_ps", [P, 2, TPS * P], stack)
        hid_ps = psum(c, "hid_ps", [P, 2, TPS * P], stack)
        f_ps = psum(c, "f_ps", [P, D], stack)
        s_ps = psum(c, "s_ps", [P, TPS, D], stack)
        sum_ps = psum(c, "sum_ps", [P, D], stack)

        @block.gpsimd
        def _(pool):
            pool.sem_inc(ip_ready, FIRST["ip"])
            pool.sem_inc(thirds_ready, FIRST["thirds"])

            def gather(u, r, turn):
                pool.wait_ge(msgs_ready, u + 1)
                pool.wait_ge(thirds_ready, u + 1)
                for k in range(TPS):
                    g = TPS * r + k
                    nc.gpsimd.tensor_copy(index[:, g:g + 1], far_node[:, bass.ds(u * TPS + k, 1)]) \
                        .then_inc(index_copied, 1)
                    pool.wait_ge(index_copied, u * TPS + (k + 1))
                    pool.sem_inc(index_seen, 1)
                    nc.gpsimd.indirect_dma_start(far[:, r, k, :], None, c.far[:, :],
                                                 bass.IndirectOffsetOnAxis(ap=index[:, g:g + 1], axis=0)) \
                        .then_inc(arrived[g], 16)

            def add_inner(u, r, turn):
                b = r % 2
                pool.wait_ge(prod_ready, u + 1 + FIRST["prod"])
                pool.wait_ge(ip_turned, u + 1)
                nc.gpsimd.tensor_tensor(inner[:, b, :, :], prod[:, b, :, 0, :], prod[:, b, :, 1, :], ALU.add) \
                    .then_inc(ip_ready, 1)
                pool.wait_ge(ip_ready, u * 2 + 1 + FIRST["ip"])
                nc.gpsimd.tensor_tensor(inner[:, b, :, :], inner[:, b, :, :], prod[:, b, :, 2, :], ALU.add) \
                    .then_inc(ip_ready, 1)

            def thirds(u, r, turn):
                b = r % 2
                pool.wait_ge(weights_ready, u + 1 + FIRST["weights"])
                pool.wait_ge(sums_ready, u + 3)
                nc.gpsimd.tensor_tensor(
                    msg[:, b, :, 1:4, :], far[:, r, :, 4 * MUL:].rearrange("p k (m v) -> p k m v", m=3),
                    weight[:, b, :, 2:3, :].to_broadcast([P, TPS, 3, MUL]), ALU.mult).then_inc(thirds_ready, 1)

            def take_attributes(u, r, turn):
                pool.wait_ge(attr_turned, u + 1)
                nc.gpsimd.tensor_copy(attr[:, r, :, :], c.recs[:, bass.ds(u * TPS, TPS), 0:32]) \
                    .then_inc(attr_ready, 1)

            pool.wait_ge(index_made, 1)
            staged(pool, [(0, take_attributes), (4, thirds), (0, gather), (2, add_inner)])

        @block.tensor
        def _(pe):
            for semaphore, name in ((attr_turned, "attr_turned"), (near, "near"), (ip_turned, "ip_turned"), (hid_ready, "hid"),
                                    (filt_s, "filt_s"), (sums_ready, "sums")):
                pe.sem_inc(semaphore, FIRST[name])

            def turn_round(u, r, turn):
                pe.wait_ge(hot_ready, u + 1)
                pe.wait_ge(attr_out, u + 1)
                for k in range(TPS):
                    last = nc.tensor.transpose(turn_ps[:, 0, k * P:k * P + P], hot[:, r, k, :], c.ident[:])
                pe.wait_ge(attr_ready, u + 1)
                for k in range(TPS):
                    last = nc.tensor.transpose(turn_ps[0:HID, 1, k * P:k * P + P], attr[:, r, k, :], c.ident[:])
                last.then_inc(attr_turned, 1)

            def gather_near(u, r, turn):
                block_of = pe.value_load(c.block_reg[0:1, bass.ds(u, 1)], min_val=0, max_val=NB - 1)
                pe.wait_ge(turned_out, u + 1 + FIRST["turned_out"])
                pe.wait_ge(prod_ready, u + 1)
                pe.wait_ge(q_out, u + 1)
                for k in range(TPS):
                    last = nc.tensor.matmul(near_ps[:, k, 0:X_AT], hot_t[:, r % 2, k, :],
                                            c.table[:, bass.ds(block_of, 1), 0:X_AT], start=True, stop=True)
                last.then_inc(near, 1)

            def turn_inner(u, r, turn):
                pe.wait_ge(ip_ready, u * 2 + 2 + FIRST["ip"])
                pe.wait_ge(soft_shifted, u + 1)
                for k in range(TPS):
                    last = nc.tensor.transpose(hid_ps[:, 0, k * P:k * P + P], inner[:, r % 2, k, :], c.ident[:])
                last.then_inc(ip_turned, 1)

            def hidden(u, r, turn):
                b = r % 2
                pe.wait_ge(attr_out, u + 1 + FIRST["attr_out"])
                pe.wait_ge(ip_out, u + 1 + FIRST["ip_out"])
                pe.wait_ge(q_out, u + 1 + FIRST["q_out"])
                nc.tensor.matmul(hid_ps[HID:2 * HID, 1, :], c.w_s1[:, 2, :], inner_t[:, b, :], start=True, stop=False)
                for k in range(TPS):
                    nc.tensor.matmul(hid_ps[HID:2 * HID, 1, k * P:k * P + P], q[:, b, k, :], c.ident[:],
                                     start=False, stop=(k == TPS - 1))
                nc.tensor.matmul(hid_ps[0:HID, 1, :], c.w_f1[:], attr_t[:, r, :], start=True, stop=True) \
                    .then_inc(hid_ready, 1)

            def filters(u, r, turn):
                b = r % 2
                pe.wait_ge(soft_shifted, u + 1 + FIRST["shifted"])
                pe.wait_ge(weights_ready, u + 2)
                for k in range(TPS):
                    cut = slice(k * P, k * P + P)
                    pe.wait_ge(f_out, u * (2 * TPS) + (2 * k + FIRST["f_out"]))
                    nc.tensor.matmul(f_ps[:], soft[0:HID, b, cut], c.w_2[0:HID, :], start=True, stop=True) \
                        .then_inc(filt_f, 1)
                    nc.tensor.matmul(s_ps[:, k, :], soft[HID:2 * HID, b, cut], c.w_2[HID:2 * HID, :],
                                     start=True, stop=True).then_inc(filt_s, 1)

            def add_up(u, r, turn):
                pe.wait_ge(msgs_ready, u + 1 + FIRST["msgs"])
                pe.wait_ge(sums_added, u + 1)
                for k in range(TPS):
                    last = nc.tensor.matmul(sum_ps[:], hot[:, r, k, :], msg[:, r % 2, k, :, :], start=(k == 0),
                                            stop=(k == TPS - 1))
                last.then_inc(sums_ready, 1)

            staged(pe, [(4, add_up), (0, turn_round), (2, turn_inner), (1, gather_near), (3, filters), (2, hidden)])

        @block.scalar
        def _(act):
            for semaphore, name in ((turned_out, "turned_out"), (attr_out, "attr_out"), (q_out, "q_out"),
                                    (ip_out, "ip_out"), (f_out, "f_out")):
                act.sem_inc(semaphore, FIRST[name])

            act.wait_ge(sums_cleared, 2)

            def take_turned(u, r, turn):
                b = r % 2
                act.wait_ge(attr_turned, u + 1 + FIRST["attr_turned"])
                act.wait_ge(near, u + 1)
                nc.scalar.copy(hot_t[:, b, :, :], turn_ps[:, 0, :].rearrange("p (k e) -> p k e", k=TPS)) \
                    .then_inc(turned_out, 1)
                act.wait_ge(hid_ready, u + 1)
                nc.scalar.copy(attr_t[:, r, :], turn_ps[0:HID, 1, :]).then_inc(attr_out, 1)

            def take_near(u, r, turn):
                act.wait_ge(prod_ready, u + 1 + FIRST["prod"])
                act.wait_ge(hid_ready, u + 3)
                nc.scalar.copy(q[:, r % 2, :, :], near_ps[:, :, Q_AT:Q_AT + HID]).then_inc(q_out, 1)

            def take_inner(u, r, turn):
                b = r % 2
                act.wait_ge(ip_turned, u + 1 + FIRST["ip_turned"])
                nc.scalar.mul(inner_t[:, b, :], hid_ps[:, 0, :], 1.0 / 3.0).then_inc(ip_out, 1)

            def take_hidden(u, r, turn):
                b = r % 2
                act.wait_ge(hid_ready, u + 1 + FIRST["hid"])
                act.wait_ge(filt_s, u * TPS + 2)
                to = soft[:, b, :]
                nc.scalar.activation(to, hid_ps[0:2 * HID, 1, :], ACT.Abs).then_inc(soft_step, 1)
                act.wait_ge(soft_step, u * 2 + 1)
                nc.scalar.activation(to, to, ACT.Exp, scale=-1.0).then_inc(soft_step, 1)
                act.wait_ge(soft_step, u * 2 + 2)
                nc.scalar.activation(to, to, ACT.Ln, scale=0.5, bias=half[0:2 * HID, 0:1]).then_inc(soft_ready, 1)

            def take_filter(u, r, turn):
                b = r % 2
                act.wait_ge(weights_ready, u + 1)
                for k in range(TPS):
                    act.wait_ge(filt_f, u * TPS + (k + 1))
                    got = f_ps[:].rearrange("p (a o v) -> p o a v", a=2, o=2)
                    to = filt[:, b, k, :, :].rearrange("p (a o) v -> p o a v", a=2)
                    sh0 = c.recs[:, bass.ds(u * TPS + k, 1), R_SH]
                    nc.scalar.activation(to[:, 0, :, :], got[:, 0, :, :], ACT.Copy, scale=sh0).then_inc(f_out, 1)
                    nc.scalar.copy(to[:, 1, :, :], got[:, 1, :, :]).then_inc(f_out, 1)

            staged(act, [(0, take_turned), (1, take_near), (2, take_inner), (3, take_filter), (2, take_hidden)])

        @block.vector
        def _(dve):
            nc.vector.tensor_copy(far_node[:], c.recs[:, :, R_J]).then_inc(index_made, 1)
            nc.vector.memset(c.sums[:], 0.0).then_inc(sums_cleared, 1)
            nc.vector.memset(half[:], 0.5).then_inc(sums_cleared, 1)
            dve.wait_ge(sums_cleared, 2)
            for semaphore, name in ((prod_ready, "prod"), (weights_ready, "weights"), (msgs_ready, "msgs"),
                                    (soft_shifted, "shifted"),
                                    (sums_added, "added")):
                dve.sem_inc(semaphore, FIRST[name])

            def one_hot(u, r, turn):
                dve.wait_ge(sums_ready, u + 1)
                for k in range(TPS):
                    last = nc.vector.tensor_scalar(hot[:, r, k, :], c.iota_row[:],
                                                   c.i_local[:, bass.ds(u * TPS + k, 1)], None, ALU.is_equal)
                last.then_inc(hot_ready, 1)

            def product(u, r, turn):
                dve.wait_ge(near, u + 1 + FIRST["near"])
                for k in range(TPS):
                    dve.wait_ge(arrived[TPS * r + k], turn * 16 + 16)
                dve.wait_ge(ip_ready, u * 2 + 2)
                nc.vector.tensor_tensor(prod[:, r % 2, :, :, :].rearrange("p k m v -> p k (m v)"),
                                        near_ps[:, :, P1_AT:X_AT], far[:, r, :, 0:3 * MUL], ALU.mult) \
                    .then_inc(prod_ready, 1)

            def shift(u, r, turn):
                dve.wait_ge(soft_ready, u + 1)
                nc.vector.scalar_tensor_tensor(soft[:, r % 2, :], hid_ps[0:2 * HID, 1, :], 0.0, soft[:, r % 2, :],
                                               ALU.max, ALU.add).then_inc(soft_shifted, 1)

            def messages(u, r, turn):
                b = r % 2
                sh = lambda k, m: c.recs[:, bass.ds(u * TPS + k, 1), R_SH + 1 + m]
                vector = lambda k, m: far[:, r, k, (4 + m) * MUL:(5 + m) * MUL]
                steps = [0]

                def stepped(instruction):
                    instruction.then_inc(step, 1)
                    steps[0] += 1
                    dve.wait_ge(step, u * STEPS + steps[0])

                dve.wait_ge(f_out, u * (2 * TPS) + (2 * TPS + FIRST["f_out"]))
                dve.wait_ge(filt_s, u * TPS + (TPS + FIRST["filt_s"]))
                dve.wait_ge(thirds_ready, u + 3)
                nc.vector.tensor_tensor(weight[:, b, :, :, :].rearrange("p k a v -> p k (a v)"),
                                        filt[:, b, :, :, :].rearrange("p k a v -> p k (a v)"), s_ps[:],
                                        ALU.mult).then_inc(weights_ready, 1)
                for m in range(3):
                    for k in range(TPS):
                        if m == 0:
                            last = nc.vector.tensor_scalar(dot[:, k, :], vector(k, m), sh(k, m), None, ALU.mult)
                        else:
                            last = nc.vector.scalar_tensor_tensor(dot[:, k, :], vector(k, m), sh(k, m),
                                                                  dot[:, k, :], ALU.mult, ALU.add)
                    if m == 2:
                        dve.wait_ge(weights_ready, u + 1 + FIRST["weights"])
                    stepped(last)
                nc.vector.tensor_tensor(dot[:], dot[:], weight[:, b, :, 3, :], ALU.mult)
                stepped(nc.vector.tensor_tensor(
                    firsts[:], far[:, r, :, 3 * MUL:4 * MUL].unsqueeze(2).to_broadcast([P, TPS, 2, MUL]),
                    weight[:, b, :, 0:2, :], ALU.mult))
                dve.wait_ge(thirds_ready, u + 1 + FIRST["thirds"])
                nc.vector.tensor_tensor(msg[:, b, :, 0, :], firsts[:, :, 0, :], dot[:], ALU.add)
                for k in range(TPS):
                    for m in range(3):
                        last = nc.vector.scalar_tensor_tensor(msg[:, b, k, 1 + m, :], firsts[:, k, 1, :], sh(k, m),
                                                              msg[:, b, k, 1 + m, :], ALU.mult, ALU.add)
                stepped(last)
                dve.sem_inc(msgs_ready, 1)

            def take_sums(u, r, turn):
                block_of = dve.value_load(c.block_reg[0:1, bass.ds(u, 1)], min_val=0, max_val=NB - 1)
                dve.wait_ge(sums_ready, u + 1 + FIRST["sums"])
                dve.wait_ge(sums_added, u + 1)
                to = c.sums[:, bass.ds(block_of, 1), :]
                nc.vector.tensor_tensor(to, to, sum_ps[:].unsqueeze(1), ALU.add).then_inc(sums_added, 1)

            staged(dve, [(0, one_hot), (1, product), (3, messages), (2, shift), (4, take_sums)])


def interaction_out(c):
    nc = c.nc
    own_added, turned, turned_out, out_ready, step = (semaphore(c, "inter_out_" + n) for n in (
        "own_added", "turned", "turned_out", "ready", "step"))
    with ExitStack() as stack, nc.Block() as block:
        sums_t = sbuf(c, "sums_t", [P, 4, N], F32, stack)
        scalars = sbuf(c, "scalars", [P, 2, MUL], F32, stack)
        measure, root, scale, measured = layer_norm(c, "interaction", stack)
        ps = [psum(c, f"inter_ps{b}", [P, D], stack) for b in range(4)]
        ps_out = [psum(c, f"inter_out_ps{b}", [P, D], stack) for b in range(4)]

        @block.vector
        def _(dve):
            chain, _, _ = chained(dve, step)
            for b in range(NB):
                nc.vector.tensor_tensor(c.sums[:, b, :], c.sums[:, b, :], c.table[:, b, X_AT:ROW], ALU.add) \
                    .then_inc(own_added, 1)
            for b in range(NB):
                dve.wait_ge(out_ready, b + 1)
                got = ps_out[b % 4]
                chain(nc.vector.tensor_tensor(scalars[:, b % 2, :], got[:, 0:MUL], c.b_o[:], ALU.add))
                vectors = c.x[:, b, MUL:D].rearrange("p (u m) -> p m u", m=3)
                nc.vector.scalar_tensor_tensor(vectors, vectors, 2.0, got[:, MUL:D].rearrange("p (m u) -> p m u", m=3),
                                               ALU.mult, ALU.add)
                chain(nc.vector.scalar_tensor_tensor(c.x[:, b, 0:MUL], c.x[:, b, 0:MUL], 2.0, scalars[:, b % 2, :],
                                                     ALU.mult, ALU.add))
                measure(b, c.x[:, b, :])
            scale(dve, chain, lambda b: c.x[:, b, :], lambda b: c.x[:, b, :])

        @block.scalar
        def _(act):
            for b in range(NB):
                act.wait_ge(turned, b + 1)
                nc.scalar.copy(sums_t[:, :, b * P:b * P + P], ps[b % 4][:].rearrange("p (f n) -> p f n", f=4)) \
                    .then_inc(turned_out, 1)
            root(act)

        @block.tensor
        def _(pe):
            for b in range(NB):
                pe.wait_ge(own_added, b + 1)
                if b >= 4:
                    pe.wait_ge(turned_out, b - 3)
                for f in range(4):
                    last = nc.tensor.transpose(ps[b % 4][:, f * P:f * P + P], c.sums[:, b, f * P:f * P + P],
                                               c.ident[:])
                last.then_inc(turned, 1)
            for b in range(NB):
                pe.wait_ge(turned_out, b + 1)
                if b >= 4:
                    pe.wait_ge(measured, b - 3)
                for f in range(4):
                    last = nc.tensor.matmul(ps_out[b % 4][:, f * P:f * P + P], sums_t[:, f, b * P:b * P + P],
                                            c.w_o[:, min(f, 1), :], start=True, stop=True)
                last.then_inc(out_ready, 1)


def graph_conv(c):
    nc = c.nc
    loaded, turned, turned_out, count_ready, beta_ready, beta_out, sum_ready, sum_out, own_ready, step, stored = (
        semaphore(c, "conv_" + n) for n in ("loaded", "turned", "turned_out", "counts_ready", "neighbour_ready",
                                     "neighbour_out", "sums_ready", "sums_out", "own_ready", "step", "stored"))
    with ExitStack() as stack, nc.Block() as block:
        sb = lambda name, shape, dtype=F32: sbuf(c, name, shape, dtype, stack)
        w_c = sb("w_c", [P, FB, D])
        w_n = sb("w_n", [P, FB, D])
        bias = sb("bias", [P, D])
        x_t = sb("x_t_conv", [P, FB, N])
        beta = sb("beta", [P, NB, D])
        inverse = sb("inverse", [P, NB])
        measure, root, scale, measured = layer_norm(c, "conv", stack)
        ps = [psum(c, f"conv_ps{b}", [P, D], stack) for b in range(4)]
        sum_ps = [psum(c, f"conv_sum_ps{b}", [P, D], stack) for b in range(2)]
        count_ps = psum(c, "count_ps", [P, NB], stack)

        @block.sync
        def _(sp):
            for to, name in ((w_n, "L3_gnn_wn"), (w_c, "L3_gnn_wc")):
                sp.dma_start(to[:], c.ins[name].rearrange("(f p) o -> p f o", p=P)).then_inc(loaded, 16)
            sp.dma_start(bias[:], c.ins["L3_gnn_bias"].partition_broadcast(P)).then_inc(loaded, 16)
            out = c.out.rearrange("(b p) d -> p b d", p=P)
            sp.wait_ge(step, 3 + 2 * NB)
            sp.dma_start(out, c.x[:]).then_inc(stored, 16)
            sp.wait_ge(stored, 16)

        @block.tensor
        def _(pe):
            for b in range(NB):
                if b >= 4:
                    pe.wait_ge(turned_out, b - 3)
                for f in range(FB):
                    last = nc.tensor.transpose(ps[b % 4][:, f * P:f * P + P], c.x[:, b, f * P:f * P + P], c.ident[:])
                last.then_inc(turned, 1)
            for i in range(NB):
                for b in range(NB):
                    last = nc.tensor.matmul(count_ps[:, i:i + 1], c.num_t[:, b, i * P:i * P + P], c.ones[:, 0:1],
                                            start=(b == 0), stop=(b == NB - 1))
            last.then_inc(count_ready, 1)
            pe.wait_ge(loaded, 48)
            pe.wait_ge(turned_out, NB)
            for b in range(NB):
                if b >= 4:
                    pe.wait_ge(beta_out, b - 3)
                for k in range(FB):
                    last = nc.tensor.matmul(ps[b % 4][:], x_t[:, k, b * P:b * P + P], w_n[:, k, :], start=(k == 0),
                                            stop=(k == FB - 1))
                last.then_inc(beta_ready, 1)
            pe.wait_ge(beta_out, NB)
            for i in range(NB):
                if i >= 2:
                    pe.wait_ge(sum_out, i - 1)
                for b in range(NB):
                    last = nc.tensor.matmul(sum_ps[i % 2][:], c.num_t[:, b, i * P:i * P + P], beta[:, b, :],
                                            start=(b == 0), stop=(b == NB - 1))
                last.then_inc(sum_ready, 1)
                if i >= 4:
                    pe.wait_ge(measured, i - 3)
                for k in range(FB):
                    last = nc.tensor.matmul(ps[i % 4][:], x_t[:, k, i * P:i * P + P], w_c[:, k, :], start=(k == 0),
                                            stop=(k == FB - 1))
                last.then_inc(own_ready, 1)

        @block.scalar
        def _(act):
            for b in range(NB):
                act.wait_ge(turned, b + 1)
                nc.scalar.copy(x_t[:, :, b * P:b * P + P], ps[b % 4][:].rearrange("p (f n) -> p f n", f=FB)) \
                    .then_inc(turned_out, 1)
            for b in range(NB):
                act.wait_ge(beta_ready, b + 1)
                nc.scalar.copy(beta[:, b, :], ps[b % 4][:]).then_inc(beta_out, 1)
            root(act)

        @block.vector
        def _(dve):
            chain, _, _ = chained(dve, step)
            dve.wait_ge(count_ready, 1)
            chain(nc.vector.reciprocal(inverse[:], count_ps[:]))
            dve.wait_ge(loaded, 48)
            dve.wait_ge(turned, NB)
            for b in range(NB):
                y = c.x[:, b, :]
                chain(nc.vector.tensor_tensor(y, y, bias[:], ALU.add))
                dve.wait_ge(sum_ready, b + 1)
                nc.vector.scalar_tensor_tensor(y, sum_ps[b % 2][:], inverse[:, b:b + 1], y, ALU.mult, ALU.add) \
                    .then_inc(sum_out, 1)
                dve.wait_ge(sum_out, b + 1)
                dve.wait_ge(own_ready, b + 1)
                chain(nc.vector.tensor_tensor(y, y, ps[b % 4][:], ALU.add))
                measure(b, y)
            scale(dve, chain, lambda b: c.x[:, b, :], lambda b: c.x[:, b, :])


def build_program(nc, ins, out):
    with ExitStack() as stack:
        c = Core()
        c.nc, c.stack, c.semaphores, c.used = nc, stack, ExitStack(), []
        c.ins, c.out = ins, out
        constants(c)
        order_edges(c)
        clear_semaphores(c)
        c.x = sbuf(c, "x_sb", [P, NB, D])
        with ExitStack() as c.gcn_stack:
            build_adjacency(c)
            clear_semaphores(c)
            gcn(c)
            clear_semaphores(c)
        gat(c)
        clear_semaphores(c)
        interaction(c)
        clear_semaphores(c)
        graph_conv(c)



_INS = ['x', 'src', 'dst', 'edge_attr_32', 'edge_attr_4', 'edge_weight', 'L0_gnn_W_gcn', 'L0_gnn_b_gcn',
        'L0_gnn_W_mlp', 'L0_gnn_b_mlp', 'L1_gnn_Ws', 'L1_gnn_Wb', 'L1_gnn_a_w', 'L1_gnn_a_b', 'L2_gnn_W_pre0',
        'L2_gnn_b_pre0', 'L2_gnn_W_pre1', 'L2_gnn_W_nd0', 'L2_gnn_b_nd0', 'L2_gnn_W_nd1', 'L2_gnn_W_g1',
        'L2_gnn_b_g1', 'L2_gnn_W_g2', 'L2_gnn_b_g2', 'L2_gnn_W_f1', 'L2_gnn_W_f2', 'L2_gnn_W_s1', 'L2_gnn_W_s2',
        'L2_gnn_W_o0', 'L2_gnn_b_o0', 'L2_gnn_W_o1', 'L3_gnn_wc', 'L3_gnn_wn', 'L3_gnn_bias']


def kernel(**inputs):
    import numpy as _np
    import concourse.bacc as _bacc
    from concourse import mybir as _mybir
    from concourse.bass_utils import run_bass_kernel_spmd as _run

    nc = _bacc.Bacc("TRN2", target_bir_lowering=False, num_devices=1)
    arrays, aps = {}, {}
    for name in _INS:
        a = _np.ascontiguousarray(inputs[name])
        arrays[f"in_{name}"] = a
        aps[name] = nc.dram_tensor(f"in_{name}", a.shape, _mybir.dt.from_np(a.dtype), kind="ExternalInput").ap()
    out = nc.dram_tensor("out", (N, D), F32, kind="ExternalOutput").ap()
    build_program(nc, aps, out)
    r = _run(nc, [arrays], core_ids=[0])
    return r.results[0]["out"]
```

```python
from contextlib import ExitStack

import concourse.bass as bass
from concourse import mybir

F32 = mybir.dt.float32
BF16 = mybir.dt.bfloat16
I32 = mybir.dt.int32
I16 = mybir.dt.int16
ALU = mybir.AluOpType
ACT = mybir.ActivationFunctionType
AX = mybir.AxisListType.X

P = 128
N = 1024
NB = N // P
D = 512
FB = D // P
E = 17408
TE = E // P
SUP = 256
TPS = SUP // P
S = E // SUP + NB
T = S * TPS
GT = 8
REC = 39
R_SH, R_W, R_I, R_J = 32, 36, 37, 38
HEADS, DH = 8, 64
MUL = 128
BIG = 1e30
EPS = 1e-5


class Core:
    pass


def sbuf(c, name, shape, dtype=F32, stack=None):
    return (stack or c.stack).enter_context(c.nc.sbuf_tensor(name, shape, dtype))


def psum(c, name, shape, stack, dtype=F32):
    return stack.enter_context(c.nc.psum_tensor(name, shape, dtype))


def semaphore(c, name):
    got = c.semaphores.enter_context(c.nc.semaphore(name))
    c.used.append(got)
    return got


def clear_semaphores(c):
    with c.nc.Block() as block:
        @block.sync
        def _(sp):
            for one in c.used:
                sp.sem_clear(one)
    c.semaphores.close()
    c.used = []


def chained(engine, finished):
    count, before, mark, size = [0], [0], [0], [0]

    def chain(instruction):
        instruction.then_inc(finished, 1)
        count[0] += 1
        engine.wait_ge(finished, before[0] + count[0])

    def turn(i, per):
        before[0], mark[0], size[0] = i * per, count[0], per

    def close(turns):
        assert count[0] - mark[0] == size[0], (count[0] - mark[0], size[0])
        before[0], count[0] = 0, mark[0] + turns * size[0]

    return chain, turn, close


def constants(c):
    nc = c.nc
    c.iota_node = sbuf(c, "iota_node", [P, N], I16)
    c.iota_row = sbuf(c, "iota_row", [P, P], BF16)
    c.iota_tile = sbuf(c, "iota_tile", [P, T], BF16)
    c.iota_sup = sbuf(c, "iota_sup", [P, S], F32)
    c.iota_col = sbuf(c, "iota_col", [P, 1])
    c.ident = sbuf(c, "ident", [P, P])
    c.before = sbuf(c, "before", [P, P])
    c.ones = sbuf(c, "ones", [P, P])
    made = semaphore(c, "constants_made")

    with nc.Block() as block:
        @block.gpsimd
        def _(pool):
            chain, _, _ = chained(pool, made)
            chain(nc.gpsimd.iota(c.iota_node[:], [[1, N]], base=0, channel_multiplier=0))
            chain(nc.gpsimd.iota(c.iota_row[:], [[1, P]], base=0, channel_multiplier=0,
                                 allow_small_or_imprecise_dtypes=True))
            chain(nc.gpsimd.iota(c.iota_tile[:], [[1, T]], base=0, channel_multiplier=0,
                                 allow_small_or_imprecise_dtypes=True))
            chain(nc.gpsimd.iota(c.iota_sup[:], [[1, S]], base=0, channel_multiplier=0,
                                 allow_small_or_imprecise_dtypes=True))
            chain(nc.gpsimd.iota(c.iota_col[:], [[0, 1]], base=0, channel_multiplier=1,
                                 allow_small_or_imprecise_dtypes=True))
            chain(nc.gpsimd.memset(c.ones[:], 1.0))
            chain(nc.gpsimd.memset(c.ident[:], 0.0))
            chain(nc.gpsimd.affine_select(out=c.ident[:], in_=c.ident[:], compare_op=ALU.not_equal, fill=1.0,
                                          base=0, pattern=[[-1, P]], channel_multiplier=1))
            chain(nc.gpsimd.memset(c.before[:], 0.0))
            chain(nc.gpsimd.affine_select(out=c.before[:], in_=c.before[:], compare_op=ALU.is_ge, fill=1.0,
                                          base=0, pattern=[[-1, P]], channel_multiplier=1))


def order_edges(c):
    nc = c.nc
    c.rows = nc.dram_tensor("records", [1 + E, REC], F32, kind="Internal").ap()
    c.row_of_place = sbuf(c, "row_of_place", [P, T], I32)
    c.block_of_sup = sbuf(c, "block_of_sup", [P, S], F32)
    c.block_reg = sbuf(c, "block_reg", [P, S], I32)
    loaded, loaded_attr, step, placed, attrs_in = (semaphore(c, n) for n in (
        "edges_loaded", "attributes_loaded", "order_step", "edges_placed", "attributes_copied"))
    rows_out, sums_ready, hot_ready, hot_used, perm_ready = (semaphore(c, n) for n in (
        "records_out", "prefix_ready", "places_hot", "places_hot_used", "rows_ready"))
    totals_ready, zero_made, row_numbers = semaphore(c, "totals_ready"), semaphore(c, "zero_made"), semaphore(c, "row_numbers")
    with ExitStack() as stack:
        sb = lambda name, shape, dtype=F32: sbuf(c, name, shape, dtype, stack)
        ends = sb("ends", [P, 2, TE], I32)
        attr32 = sb("attr32", [P, TE, 32])
        attr4 = sb("attr4", [P, TE, 4])
        weight = sb("weight", [P, TE])
        record = sb("record", [P, TE, REC])
        dummy = sb("empty_record", [1, REC])
        blk = sb("blk", [P, TE], I32)
        blk_f = sb("blk_f", [P, TE])
        in_block = sb("in_block", [P, NB, TE])
        upto = sb("upto", [P, NB, TE])
        onesrow = sb("onesrow", [P, TE])
        totals = sb("totals", [P, NB])
        first = sb("first", [P, NB])
        sups = sb("sups", [P, NB])
        sups_i = sb("sups_i", [P, NB], I32)
        sup_end = sb("sup_end", [P, NB])
        place = sb("place", [P, TE])
        term = sb("term", [P, TE])
        place_i = sb("place_i", [P, TE], I32)
        tmp_i = sb("tmp_i", [P, TE], I32)
        high = sb("high", [P, TE])
        low = sb("low", [P, TE])
        row_i = sb("row_i", [P, TE], I32)
        row_high = sb("row_high", [P, TE])
        row_low = sb("row_low", [P, TE])
        hot_low = sb("hot_low", [P, 2, GT, P], BF16)
        hot_row = sb("hot_row", [P, 2, GT, 2, T], BF16)
        zero = sb("zero", [P, 2 * T], BF16)
        row_f = sb("row_f", [P, T])
        sup_ge = sb("sup_ge", [P, S])
        counts_ps = psum(c, "counts_ps", [P, 2 * NB], stack)
        perm_ps = psum(c, "perm_ps", [P, 2 * T], stack)

        with nc.Block() as block:
            @block.sync
            def _(sp):
                sp.dma_start(ends[:, 0, :], c.ins["src"].rearrange("(p t) -> p t", p=P)).then_inc(loaded, 16)
                sp.dma_start(ends[:, 1, :], c.ins["dst"].rearrange("(p t) -> p t", p=P)).then_inc(loaded, 16)
                sp.dma_start(weight[:], c.ins["edge_weight"].rearrange("(p t) -> p t", p=P)).then_inc(loaded_attr, 16)
                sp.dma_start(attr4[:], c.ins["edge_attr_4"].rearrange("(p t) a -> p t a", p=P)).then_inc(loaded_attr, 16)
                sp.dma_start(attr32[:], c.ins["edge_attr_32"].rearrange("(p t) a -> p t a", p=P)).then_inc(loaded_attr, 16)
                sp.wait_ge(attrs_in, 5)
                sp.dma_start(c.rows[1:, :].rearrange("(p t) r -> p (t r)", p=P),
                             record[:].rearrange("p t r -> p (t r)")).then_inc(rows_out, 16)
                sp.dma_start(c.rows[0:1, :], dummy[:]).then_inc(rows_out, 16)
                sp.wait_ge(rows_out, 32)

            @block.scalar
            def _(act):
                act.wait_ge(loaded, 32)
                nc.scalar.copy(record[:, :, R_I:R_I + 2], ends[:].rearrange("p e t -> p t e")).then_inc(attrs_in, 1)
                act.wait_ge(loaded_attr, 48)
                nc.scalar.copy(record[:, :, 0:32], attr32[:]).then_inc(attrs_in, 1)
                nc.scalar.copy(record[:, :, R_SH:R_SH + 4], attr4[:]).then_inc(attrs_in, 1)
                nc.scalar.copy(record[:, :, R_W], weight[:]).then_inc(attrs_in, 1)

            @block.gpsimd
            def _(pool):
                nc.gpsimd.iota(row_i[:], [[1, TE]], base=1, channel_multiplier=TE).then_inc(row_numbers, 1)
                pool.wait_ge(zero_made, 1)
                nc.gpsimd.memset(dummy[0:1, R_I:R_I + 1], -1.0).then_inc(attrs_in, 1)

            @block.vector
            def _(dve):
                nc.vector.memset(dummy[:], 0.0).then_inc(zero_made, 1)
                nc.vector.memset(zero[:], 0.0).then_inc(zero_made, 1)
                chain, _, _ = chained(dve, step)
                chain(nc.vector.memset(onesrow[:], 1.0))
                dve.wait_ge(loaded, 32)
                chain(nc.vector.tensor_single_scalar(blk[:], ends[:, 0, :], 7, op=ALU.arith_shift_right))
                chain(nc.vector.tensor_copy(blk_f[:], blk[:]))
                for b in range(NB):
                    last = nc.vector.tensor_scalar(in_block[:, b, :], blk_f[:], float(b), None, ALU.is_equal)
                chain(last)
                for b in range(NB):
                    last = nc.vector.tensor_tensor_scan(upto[:, b, :], onesrow[:], in_block[:, b, :], 0.0,
                                                        ALU.mult, ALU.add)
                chain(last)
                nc.vector.tensor_copy(totals[:], upto[:, :, TE - 1]).then_inc(totals_ready, 1)
                dve.wait_ge(sums_ready, 1)
                chain(nc.vector.tensor_scalar(sups[:], counts_ps[:, NB:2 * NB], float(SUP - 1), None, ALU.add))
                chain(nc.vector.tensor_copy(sups_i[:], sups[:]))
                chain(nc.vector.tensor_single_scalar(sups_i[:], sups_i[:], SUP.bit_length() - 1,
                                                     op=ALU.arith_shift_right))
                chain(nc.vector.tensor_copy(sups[:], sups_i[:]))
                chain(nc.vector.tensor_tensor_scan(sup_end[:], onesrow[:, 0:NB], sups[:], 0.0, ALU.mult, ALU.add))
                chain(nc.vector.tensor_tensor(first[:], sup_end[:], sups[:], ALU.subtract))
                chain(nc.vector.tensor_scalar(first[:], first[:], float(SUP), -1.0, ALU.mult, ALU.add))
                chain(nc.vector.tensor_tensor(first[:], first[:], counts_ps[:, 0:NB], ALU.add))
                for b in range(NB):
                    chain(nc.vector.scalar_tensor_tensor(term[:] if b else place[:], upto[:, b, :], first[:, b:b + 1],
                                                         in_block[:, b, :], ALU.add, ALU.mult))
                    if b:
                        chain(nc.vector.tensor_tensor(place[:], place[:], term[:], ALU.add))
                chain(nc.vector.tensor_copy(place_i[:], place[:]))
                chain(nc.vector.tensor_single_scalar(tmp_i[:], place_i[:], 7, op=ALU.arith_shift_right))
                chain(nc.vector.tensor_copy(high[:], tmp_i[:]))
                chain(nc.vector.tensor_single_scalar(tmp_i[:], place_i[:], P - 1, op=ALU.bitwise_and))
                chain(nc.vector.tensor_copy(low[:], tmp_i[:]))
                dve.wait_ge(row_numbers, 1)
                chain(nc.vector.tensor_single_scalar(tmp_i[:], row_i[:], 7, op=ALU.arith_shift_right))
                chain(nc.vector.tensor_copy(row_high[:], tmp_i[:]))
                chain(nc.vector.tensor_single_scalar(tmp_i[:], row_i[:], P - 1, op=ALU.bitwise_and))
                chain(nc.vector.tensor_copy(row_low[:], tmp_i[:]))
                with dve.Fori(0, TE // GT) as i:
                    half = i % 2
                    dve.wait_ge(hot_used, i + 1)
                    for g in range(GT):
                        t = i * GT + g
                        nc.vector.tensor_scalar(hot_low[:, bass.ds(half, 1), g, :], c.iota_row[:],
                                                low[:, bass.ds(t, 1)], None, ALU.is_equal)
                        nc.vector.tensor_scalar(hot_row[:, bass.ds(half, 1), g, 0, :], c.iota_tile[:],
                                                high[:, bass.ds(t, 1)], row_high[:, bass.ds(t, 1)],
                                                ALU.is_equal, ALU.mult)
                        last = nc.vector.tensor_scalar(hot_row[:, bass.ds(half, 1), g, 1, :], c.iota_tile[:],
                                                       high[:, bass.ds(t, 1)], row_low[:, bass.ds(t, 1)],
                                                       ALU.is_equal, ALU.mult)
                    last.then_inc(hot_ready, 1)
                dve.wait_ge(perm_ready, 1)
                chain(nc.vector.tensor_copy(row_f[:], perm_ps[:, T:2 * T]))
                chain(nc.vector.scalar_tensor_tensor(row_f[:], perm_ps[:, 0:T], float(P), row_f[:],
                                                     ALU.mult, ALU.add))
                chain(nc.vector.tensor_copy(c.row_of_place[:], row_f[:]))
                chain(nc.vector.tensor_scalar(c.block_of_sup[:], c.iota_sup[:], sup_end[:, 0:1], None, ALU.is_ge))
                for b in range(1, NB - 1):
                    chain(nc.vector.tensor_scalar(sup_ge[:], c.iota_sup[:], sup_end[:, b:b + 1], None, ALU.is_ge))
                    chain(nc.vector.tensor_tensor(c.block_of_sup[:], c.block_of_sup[:], sup_ge[:], ALU.add))
                chain(nc.vector.tensor_copy(c.block_reg[:], c.block_of_sup[:]))

            @block.tensor
            def _(pe):
                pe.wait_ge(totals_ready, 1)
                nc.tensor.matmul(counts_ps[:, 0:NB], c.before[:], totals[:], start=True, stop=True)
                nc.tensor.matmul(counts_ps[:, NB:2 * NB], c.ones[:], totals[:], start=True, stop=True) \
                    .then_inc(sums_ready, 1)
                pe.wait_ge(zero_made, 2)
                nc.tensor.matmul(perm_ps[:], zero[:, 0:P], zero[:], start=True, stop=False).then_inc(hot_used, 2)
                with pe.Fori(0, TE // GT) as i:
                    pe.wait_ge(hot_ready, i + 1)
                    half = i % 2
                    for g in range(GT):
                        last = nc.tensor.matmul(perm_ps[:], hot_low[:, bass.ds(half, 1), g, :],
                                                hot_row[:, bass.ds(half, 1), g, :, :], start=False, stop=False)
                    last.then_inc(hot_used, 1)
                nc.tensor.matmul(perm_ps[:], zero[:, 0:P], zero[:], start=False, stop=True).then_inc(perm_ready, 1)


def build_adjacency(c):
    nc = c.nc
    turns = T // GT
    sups = GT // TPS
    c.recs = sbuf(c, "recs", [P, T, REC])
    c.i_local = sbuf(c, "i_local", [P, T])
    c.num_t = sbuf(c, "num_t", [P, NB, N])
    cleared, row_copied, copied, step, onehots, parts, built, added = (semaphore(c, n) for n in (
        "matrices_cleared", "row_number_copied", "record_copied", "adjacency_step", "onehots_ready",
        "weighted_ready", "block_built", "block_added"))
    slot_free, row_seen = semaphore(c, "record_slot_free"), semaphore(c, "row_number_seen")
    arrived = c.gathered[0:GT]
    stack = c.gcn_stack
    c.adj_t = sbuf(c, "adj_t", [P, NB, N], F32, stack)
    with ExitStack() as stack:
        sb = lambda name, shape, dtype=F32: sbuf(c, name, shape, dtype, stack)
        slots = sb("record_slots", [P, GT, REC])
        row_slots = sb("row_slots", [P, GT], I32)
        w_part = sb("w_part", [P, 3, 2, GT])
        w_rest = sb("w_rest", [P, GT])
        hot_j = sb("hot_j", [P, GT, N], BF16)
        hot_i = sb("hot_i", [P, GT, 4, P], BF16)
        built_ps = [psum(c, f"built_ps{b}", [P, NB, 2, P], stack) for b in range(2)]

        with nc.Block() as block:
            @block.gpsimd
            def _(pool):
                nc.gpsimd.memset(c.adj_t[:], 0.0).then_inc(cleared, 1)
                nc.gpsimd.memset(c.num_t[:], 0.0).then_inc(cleared, 1)
                with pool.Fori(0, turns) as i:
                    for g in range(GT):
                        pool.wait_ge(slot_free, i * GT + (g + 1))
                        nc.gpsimd.tensor_copy(row_slots[:, g:g + 1], c.row_of_place[:, bass.ds(i * GT + g, 1)]) \
                            .then_inc(row_copied, 1)
                        pool.wait_ge(row_copied, i * GT + (g + 1))
                        pool.sem_inc(row_seen, 1)
                        nc.gpsimd.indirect_dma_start(
                            slots[:, g, :], None, c.rows[:, :],
                            bass.IndirectOffsetOnAxis(ap=row_slots[:, g:g + 1], axis=0)).then_inc(arrived[g], 16)

            @block.scalar
            def _(act):
                def copy_records(i):
                    for g in range(GT):
                        act.wait_ge(arrived[g], i * 16 + 16)
                        nc.scalar.copy(c.recs[:, bass.ds(i * GT + g, 1), :], slots[:, g:g + 1, :]) \
                            .then_inc(copied, 1)
                        act.wait_ge(copied, i * GT + (g + 1))
                        act.sem_inc(slot_free, 1)

                def weigh(i):
                    for s in range(sups):
                        act.wait_ge(onehots, i * sups + (s + 1))
                        for t in range(TPS * s, TPS * s + TPS):
                            for part, at in enumerate((0, 2, 3)):
                                last = nc.scalar.activation(hot_i[:, t, at, :], hot_i[:, t, 1, :], ACT.Copy,
                                                            scale=w_part[:, part, 0, t:t + 1])
                        last.then_inc(parts, 1)

                act.sem_inc(slot_free, GT)
                copy_records(0)
                with act.Fori(0, turns - 1) as i:
                    copy_records(i + 1)
                    weigh(i)
                weigh(turns - 1)

            @block.vector
            def _(dve):
                chain, turn, close = chained(dve, step)

                def split_weights(i):
                    dve.wait_ge(copied, i * GT + GT)
                    rec = c.recs[:, bass.ds(i * GT, GT), :]
                    w1, w2, w3 = (w_part[:, n, 0, :] for n in range(3))
                    chain(nc.vector.tensor_single_scalar(w1.bitcast(I32), rec[:, :, R_W].bitcast(I32), -65536,
                                                         op=ALU.bitwise_and))
                    chain(nc.vector.tensor_tensor(w_rest[:], rec[:, :, R_W], w1, ALU.subtract))
                    chain(nc.vector.tensor_single_scalar(w2.bitcast(I32), w_rest[:].bitcast(I32), -65536,
                                                         op=ALU.bitwise_and))
                    chain(nc.vector.tensor_tensor(w3, w_rest[:], w2, ALU.subtract))
                    chain(nc.vector.scalar_tensor_tensor(
                        c.i_local[:, bass.ds(i * GT, GT)].rearrange("p (s k) -> p s k", k=TPS),
                        c.block_of_sup[:, bass.ds(i * sups, sups)].unsqueeze(2).to_broadcast([P, sups, TPS]),
                        -float(P), rec[:, :, R_I].rearrange("p (s k) -> p s k", k=TPS), ALU.mult, ALU.add))

                def one_hot(i, s):
                    t0 = TPS * s
                    nc.vector.tensor_tensor(
                        hot_i[:, t0:t0 + TPS, 1, :], c.iota_row[:].unsqueeze(1).to_broadcast([P, TPS, P]),
                        c.i_local[:, bass.ds(i * GT + t0, TPS)].unsqueeze(2).to_broadcast([P, TPS, P]), ALU.is_equal)
                    for t in range(t0, t0 + TPS):
                        last = nc.vector.tensor_scalar(hot_j[:, t, :], c.iota_node[:],
                                                       c.recs[:, bass.ds(i * GT + t, 1), R_J], None, ALU.is_equal)
                    last.then_inc(onehots, 1)

                def add_block(i, s):
                    k = dve.value_load(c.block_reg[0:1, bass.ds(i * sups + s, 1)], min_val=0, max_val=NB - 1)
                    dve.wait_ge(built, i * sups + (s + 1))
                    for n, m in enumerate((c.adj_t, c.num_t)):
                        to = m[:, :, bass.ds(k * P, P)]
                        ins = nc.vector.tensor_tensor(to, to, built_ps[s % 2][:, :, n, :], ALU.add)
                        chain(ins)
                    dve.sem_inc(added, 1)

                dve.wait_ge(cleared, 2)
                dve.sem_inc(added, 2)
                split_weights(0)
                for s in range(sups):
                    one_hot(0, s)
                with dve.Fori(0, turns - 1) as i:
                    turn(i, 5 + 2 * sups)
                    add_block(i, 0)
                    dve.wait_ge(parts, i * sups + sups)
                    split_weights(i + 1)
                    one_hot(i + 1, 0)
                    for s in range(1, sups):
                        add_block(i, s)
                        one_hot(i + 1, s)
                close(turns - 1)
                for s in range(sups):
                    add_block(turns - 1, s)

            @block.tensor
            def _(pe):
                with pe.Fori(0, turns) as i:
                    for s in range(sups):
                        pe.wait_ge(onehots, i * sups + (s + 1))
                        pe.wait_ge(parts, i * sups + (s + 1))
                        pe.wait_ge(added, i * sups + (s + 1))
                        for b in range(NB):
                            to = built_ps[s % 2]
                            for k in range(TPS):
                                t = TPS * s + k
                                hj = hot_j[:, t, b * P:(b + 1) * P]
                                nc.tensor.matmul(to[:, b, :, :], hj, hot_i[:, t, 0:2, :], start=(k == 0), stop=False)
                                nc.tensor.matmul(to[:, b, 0, :], hj, hot_i[:, t, 2, :], start=False, stop=False)
                                last = nc.tensor.matmul(to[:, b, 0, :], hj, hot_i[:, t, 3, :], start=False,
                                                        stop=(k == TPS - 1))
                        last.then_inc(built, 1)


def layer_norm(c, name, stack):
    nc = c.nc
    stats = sbuf(c, f"stats_{name}", [P, NB, 6], F32, stack)
    moments = sbuf(c, f"moments_{name}", [P, NB, 2], F32, stack)
    spread = sbuf(c, f"spread_{name}", [P, NB], F32, stack)
    measured, variance_ready, root_ready = (
        semaphore(c, f"{what}_{name}") for what in ("blocks_measured", "variance_ready", "roots_ready"))

    def measure(b, y):
        nc.vector.bn_stats(stats[:, b, :], y).then_inc(measured, 1)

    def root(act):
        act.wait_ge(variance_ready, 2)
        nc.scalar.activation(spread[:], spread[:], ACT.Sqrt).then_inc(root_ready, 1)

    def scale(dve, chain, y, out):
        dve.wait_ge(measured, NB)
        for b in range(NB):
            last = nc.vector.bn_aggr(moments[:, b, :], stats[:, b, :])
        last.then_inc(variance_ready, 1)
        dve.wait_ge(variance_ready, 1)
        nc.vector.tensor_scalar(spread[:], moments[:, :, 1], EPS, None, ALU.add).then_inc(variance_ready, 1)
        dve.wait_ge(root_ready, 1)
        chain(nc.vector.reciprocal(spread[:], spread[:]))
        for b in range(NB):
            last = nc.vector.tensor_scalar(out(b), y(b), moments[:, b, 0:1], spread[:, b:b + 1],
                                           ALU.subtract, ALU.mult)
        chain(last)

    return measure, root, scale, measured


def gcn(c):
    nc = c.nc
    layers = 2
    loaded, deg_ready, safe_ready, root_ready, scaled, agg_ready, agg_out, lin_ready, lin_out, mlp_ready, h_ready, \
        step, lin_free = (semaphore(c, n) for n in (
            "gcn_loaded", "degree_ready", "degree_safe", "degree_root", "gcn_scaled", "gcn_sums_ready",
            "gcn_sums_out", "gcn_linear_ready", "gcn_linear_out", "gcn_mlp_ready", "gcn_h_ready", "gcn_step",
            "gcn_mlp_free"))
    with ExitStack() as stack:
        sb = lambda name, shape, dtype=F32: sbuf(c, name, shape, dtype, stack)
        w_gcn = sb("w_gcn", [P, layers, FB, D])
        w_mlp = sb("w_mlp", [P, layers, FB, D])
        b_gcn = sb("b_gcn", [P, layers, FB])
        b_mlp = sb("b_mlp", [P, layers, D])
        h = sb("h", [P, 4, D])
        hs = sb("hs", [P, NB, D])
        root_b = sb("root_b", [P, N])
        root_p = sb("root_p", [P, NB])
        there_p = sb("there_p", [P, NB])
        agg = sb("agg", [P, FB, N])
        lin = sb("lin", [P, FB, N])
        there_b = agg[:, 0, :]
        measure, root, scale, measured = layer_norm(c, "gcn", stack)
        ps = [psum(c, f"gcn_ps{b}", [P, D], stack) for b in range(4)]
        deg_b = psum(c, "deg_b", [P, N], stack)
        deg_p = psum(c, "deg_p", [P, NB], stack)

        with nc.Block() as block:
            @block.sync
            def _(sp):
                sp.dma_start(c.x[:], c.ins["x"].rearrange("(b p) d -> p b d", p=P)).then_inc(loaded, 16)
                for l in range(layers):
                    sp.dma_start(w_gcn[:, l, :, :], c.ins["L0_gnn_W_gcn"][l].rearrange("(f p) o -> p f o", p=P)) \
                        .then_inc(loaded, 16)
                    sp.dma_start(w_mlp[:, l, :, :], c.ins["L0_gnn_W_mlp"][l].rearrange("(f p) o -> p f o", p=P)) \
                        .then_inc(loaded, 16)
                    sp.dma_start(b_gcn[:, l, :], c.ins["L0_gnn_b_gcn"][l].rearrange("(f p) -> p f", p=P), allow_slow_non_contiguous=True) \
                        .then_inc(loaded, 16)
                    sp.dma_start(b_mlp[:, l, :], c.ins["L0_gnn_b_mlp"][l].partition_broadcast(P)).then_inc(loaded, 16)
            all_loaded = 16 * (1 + 4 * layers)

            @block.tensor
            def _(pe):
                for half in range(2):
                    for b in range(NB):
                        nc.tensor.matmul(deg_b[:, half * D:half * D + D], c.ones[:],
                                         c.adj_t[:, b, half * D:half * D + D], start=(b == 0), stop=(b == NB - 1))
                for i in range(NB):
                    for b in range(NB):
                        last = nc.tensor.matmul(deg_p[:, i:i + 1], c.adj_t[:, b, i * P:i * P + P], c.ones[:, 0:1],
                                                start=(b == 0), stop=(b == NB - 1))
                last.then_inc(deg_ready, 1)
                for l in range(layers):
                    n = l * 2 * FB
                    for f in range(FB):
                        for half in range(2):
                            u = 2 * f + half
                            if u >= 4:
                                pe.wait_ge(agg_out, n + u - 3)
                            for b in range(NB):
                                pe.wait_ge(scaled, l * NB + b + 1)
                                last = nc.tensor.matmul(ps[u % 4][:], hs[:, b, f * P:f * P + P],
                                                        c.adj_t[:, b, half * D:half * D + D],
                                                        start=(b == 0), stop=(b == NB - 1))
                            last.then_inc(agg_ready, 1)
                    for half in range(2):
                        for f in range(FB):
                            u = half * FB + f
                            if u < 4:
                                pe.wait_ge(agg_out, n + 2 * FB)
                            else:
                                pe.wait_ge(lin_out, n + u - 3)
                            for k in range(FB):
                                last = nc.tensor.matmul(ps[u % 4][:], w_gcn[:, l, k, f * P:f * P + P],
                                                        agg[:, k, half * D:half * D + D],
                                                        start=(k == 0), stop=(k == FB - 1))
                            last.then_inc(lin_ready, 1)
                    for b in range(NB):
                        pe.wait_ge(lin_out, n + 2 * FB)
                        if b >= 4:
                            pe.wait_ge(lin_free, l * NB + b - 3)
                        for k in range(FB):
                            last = nc.tensor.matmul(ps[b % 4][:], lin[:, k, b * P:b * P + P], w_mlp[:, l, k, :],
                                                    start=(k == 0), stop=(k == FB - 1))
                        last.then_inc(mlp_ready, 1)
                    if l + 1 < layers:
                        pe.wait_ge(lin_free, l * NB + NB)

            @block.scalar
            def _(act):
                act.wait_ge(safe_ready, 2)
                nc.scalar.activation(root_b[:], root_b[:], ACT.Sqrt).then_inc(root_ready, 1)
                nc.scalar.activation(root_p[:], root_p[:], ACT.Sqrt).then_inc(root_ready, 1)
                act.wait_ge(loaded, all_loaded)
                for l in range(layers):
                    for half in range(2):
                        for f in range(FB):
                            u = half * FB + f
                            act.wait_ge(lin_ready, l * 2 * FB + u + 1)
                            if u == 0 and l:
                                act.wait_ge(mlp_ready, l * NB)
                            nc.scalar.activation(lin[:, f, half * D:half * D + D], ps[u % 4][:], ACT.Identity,
                                                 bias=b_gcn[:, l, f:f + 1]).then_inc(lin_out, 1)
                root(act)

            @block.vector
            def _(dve):
                chain, _, _ = chained(dve, step)
                dve.wait_ge(deg_ready, 1)
                for deg, there, root in ((deg_b, there_b, root_b), (deg_p, there_p[:], root_p)):
                    chain(nc.vector.tensor_scalar(there, deg[:], 0.0, None, ALU.is_gt))
                    chain(nc.vector.tensor_scalar(root[:], deg[:], 1e-30, None, ALU.max))
                    nc.vector.reciprocal(root[:], root[:]).then_inc(safe_ready, 1)
                dve.wait_ge(root_ready, 2)
                chain(nc.vector.tensor_tensor(root_b[:], root_b[:], there_b, ALU.mult))
                chain(nc.vector.tensor_tensor(root_p[:], root_p[:], there_p[:], ALU.mult))
                dve.wait_ge(loaded, all_loaded)
                for b in range(NB):
                    nc.vector.tensor_scalar(hs[:, b, :], c.x[:, b, :], root_p[:, b:b + 1], None, ALU.mult) \
                        .then_inc(scaled, 1)
                for l in range(layers):
                    for f in range(FB):
                        for half in range(2):
                            u = 2 * f + half
                            dve.wait_ge(agg_ready, l * 2 * FB + u + 1)
                            nc.vector.tensor_tensor(agg[:, f, half * D:half * D + D], ps[u % 4][:],
                                                    root_b[:, half * D:half * D + D], ALU.mult).then_inc(agg_out, 1)
                    for b in range(NB):
                        dve.wait_ge(mlp_ready, l * NB + b + 1)
                        nc.vector.tensor_tensor(h[:, b % 4, :], ps[b % 4][:], b_mlp[:, l, :], ALU.add) \
                            .then_inc(lin_free, 1)
                        dve.wait_ge(lin_free, l * NB + b + 1)
                        chain(nc.vector.scalar_tensor_tensor(h[:, b % 4, :], h[:, b % 4, :], 0.01, h[:, b % 4, :],
                                                             ALU.mult, ALU.max))
                        if l + 1 < layers:
                            nc.vector.tensor_scalar(hs[:, b, :], h[:, b % 4, :], root_p[:, b:b + 1], None, ALU.mult) \
                                .then_inc(scaled, 1)
                        else:
                            chain(nc.vector.tensor_tensor(c.x[:, b, :], c.x[:, b, :], h[:, b % 4, :], ALU.add))
                            measure(b, c.x[:, b, :])
                scale(dve, chain, lambda b: c.x[:, b, :], lambda b: c.x[:, b, :])


def gat(c):
    nc = c.nc
    AHEAD = 2
    SLOTS = 4
    PAIR = 2 * NB
    ON_POOL = (1, 4, 7)
    ON_DVE = tuple(b for b in range(NB) if b not in ON_POOL)
    SCORED0 = NB + SLOTS
    (loaded, copied, turned, turned_out, wx_ready, wx_out, prod_ready, reduced, set_up, lnready, cnt_ready, cnt_out,
     mask_t_made, diag_s, s_bcast, maxed, scores_done, step, diag_ready, bc_ready, bc_out, low_ready, scored,
     masked_dve, masked_pool, probs_ready, probs_used, heads_out, zero_made, pool_step, neg_ready, log_in,
     log_ready) = (semaphore(c, "gat_" + n) for n in (
         "loaded", "copied", "turned", "turned_out", "wx_ready", "wx_out", "products_ready", "reduced", "set_up",
         "logs_added", "counts_turned", "counts_out", "mask_t_made", "diag_s", "s_broadcast", "maxed",
         "scores_done", "step", "diag_ready", "broadcast", "broadcast_out", "low_slope", "scored", "masked_dve",
         "masked_pool", "probs_ready", "probs_used", "heads_out", "zero_made", "pool_step", "nonedges",
         "log_in", "log_ready"))
    with ExitStack() as outer:
        sbo = lambda name, shape, dtype=F32: sbuf(c, name, shape, dtype, outer)
        wx = sbo("wx", [P, NB, HEADS, DH + 1])
        s_i = sbo("s_i", [P, HEADS, NB])
        s_low = sbo("s_low", [P, HEADS, NB])
        t_j = sbo("t_j", [P, HEADS, NB])
        top = sbo("top", [P, HEADS, NB])
        arg = sbo("arg", [P, 2, HEADS, NB])
        a_b = sbo("a_b", [P, HEADS])
        log_num = sbo("log_num", [P, NB, N])
        zero = sbo("zero_gat", [P, 4 * (DH + 1)], BF16)
        measure, root, scale, measured = layer_norm(c, "gat", outer)

        with ExitStack() as stack, nc.Block() as block:
            sb = lambda name, shape, dtype=F32: sbuf(c, name, shape, dtype, stack)
            w_s = sb("w_s", [P, FB, HEADS, DH])
            w_b = sb("w_b", [P, D])
            a_w = sb("a_w", [P, HEADS, 2 * DH])
            x_t = sb("x_t", [P, FB, N])
            prod = sb("prod", [P, 2, 2, D])
            mask_t = sb("mask_t", [P, NB, N])
            diag = sb("diag", [P, 4, 4, P])
            junk = x_t[:, 0, :]
            atleast = x_t[:, 1, :].rearrange("p (u d) -> p u d", u=2)
            ps = [psum(c, f"gat_ps{b}", [P, 4, P], stack) for b in range(4)]
            s_ps = [psum(c, f"s_ps{b}", [P, N], stack) for b in range(2)]

            @block.sync
            def _(sp):
                for h in range(HEADS):
                    sp.dma_start(w_s[:, :, h, :], c.ins["L1_gnn_Ws"][h].rearrange("(f p) d -> p f d", p=P)) \
                        .then_inc(loaded, 16)
                sp.dma_start(w_b[:], c.ins["L1_gnn_Wb"].rearrange("h d -> (h d)").partition_broadcast(P)) \
                    .then_inc(loaded, 16)
                sp.dma_start(a_w[:], c.ins["L1_gnn_a_w"].partition_broadcast(P)).then_inc(loaded, 16)
                sp.dma_start(a_b[:], c.ins["L1_gnn_a_b"].partition_broadcast(P)).then_inc(loaded, 16)
            all_loaded = 16 * (HEADS + 3)

            @block.tensor
            def _(pe):
                for b in range(NB):
                    if b >= 4:
                        pe.wait_ge(turned_out, b - 3)
                    for f in range(FB):
                        last = nc.tensor.transpose(ps[b % 4][:, f, :], c.x[:, b, f * P:f * P + P], c.ident[:])
                    last.then_inc(turned, 1)
                pe.wait_ge(turned_out, NB)
                pe.wait_ge(loaded, all_loaded)
                for b in range(NB):
                    if b >= 4:
                        pe.wait_ge(wx_out, b - 3)
                    for f in range(FB):
                        last = nc.tensor.matmul(ps[b % 4][:], x_t[:, f, b * P:b * P + P], w_s[:, f, :, :],
                                                start=(f == 0), stop=(f == FB - 1))
                    last.then_inc(wx_ready, 1)
                pe.wait_ge(wx_out, NB)
                for u in range(2 * NB):
                    if u >= 4:
                        pe.wait_ge(cnt_out, 2 * (u - 3))
                    i, half = u // 2, u % 2
                    for j in range(4):
                        last = nc.tensor.transpose(ps[u % 4][:, j, :], c.num_t[:, 4 * half + j, i * P:i * P + P],
                                                   c.ident[:])
                    last.then_inc(cnt_ready, 1)
                for h in range(HEADS):
                    if h >= 2:
                        pe.wait_ge(maxed, NB * (h - 1))
                    for half in range(2):
                        u = 2 * h + half
                        pe.wait_ge(diag_s, u + 1)
                        nc.tensor.matmul(s_ps[h % 2][:, half * D:half * D + D], c.ones[:], diag[:, u % 4, :, :],
                                         start=True, stop=True).then_inc(s_bcast, 1)

            @block.scalar
            def _(act):
                for b in range(NB):
                    act.wait_ge(turned, b + 1)
                    nc.scalar.copy(x_t[:, :, b * P:b * P + P], ps[b % 4][:]).then_inc(turned_out, 1)
                for u in range(2 * NB):
                    i, half = u // 2, u % 2
                    act.wait_ge(cnt_out, 2 * u + 2)
                    nc.scalar.activation(atleast[:, u % 2, :], atleast[:, u % 2, :], ACT.Ln).then_inc(log_ready, 1)

            @block.gpsimd
            def _(pool):
                nc.gpsimd.memset(wx[:, :, :, DH:DH + 1], 1.0).then_inc(set_up, 1)
                nc.gpsimd.memset(zero[:], 0.0).then_inc(set_up, 1)
                for b in range(NB):
                    nc.gpsimd.tensor_scalar(mask_t[:, b, :], c.num_t[:, b, :], 0.5, -BIG, ALU.is_lt, ALU.mult) \
                        .then_inc(mask_t_made, 1)
                pool.wait_ge(loaded, all_loaded)
                for b in range(NB):
                    pool.wait_ge(wx_out, b + 1)
                    if b >= 2:
                        pool.wait_ge(reduced, 2 * (b - 1))
                    for n in range(2):
                        nc.gpsimd.tensor_tensor(prod[:, b % 2, n, :].rearrange("p (h d) -> p h d", d=DH),
                                                wx[:, b, :, 0:DH], a_w[:, :, n * DH:n * DH + DH], ALU.mult) \
                            .then_inc(prod_ready, 1)
                pool.wait_ge(reduced, 2 * NB)
                def s_diagonals(units):
                    for u in units:
                        h, half = u // 2, u % 2
                        if u >= 4:
                            pool.wait_ge(s_bcast, u - 3)
                        nc.gpsimd.tensor_tensor(diag[:, u % 4, :, :], c.ident[:].unsqueeze(1).to_broadcast([P, 4, P]),
                                                s_i[:, h, 4 * half:4 * half + 4].unsqueeze(2).to_broadcast([P, 4, P]),
                                                ALU.mult).then_inc(diag_s, 1)

                s_diagonals(range(4))
                for u in range(2 * NB):
                    i, half = u // 2, u % 2
                    pool.wait_ge(log_ready, u + 1)
                    nc.gpsimd.tensor_tensor(log_num[:, i, half * D:half * D + D],
                                            log_num[:, i, half * D:half * D + D], atleast[:, u % 2, :],
                                            ALU.add).then_inc(lnready, 1)
                s_diagonals(range(4, 2 * HEADS))

            @block.vector
            def _(dve):
                chain, _, _ = chained(dve, step)
                dve.wait_ge(loaded, all_loaded)
                dve.wait_ge(set_up, 1)

                def reduce(b):
                    for n, term in enumerate((t_j, s_i)):
                        dve.wait_ge(prod_ready, 2 * b + n + 1)
                        nc.vector.tensor_reduce(term[:, :, b], prod[:, b % 2, n, :].rearrange("p (h d) -> p h d", d=DH),
                                                AX, ALU.add).then_inc(reduced, 1)

                for b in range(NB):
                    dve.wait_ge(wx_ready, b + 1)
                    nc.vector.tensor_tensor(wx[:, b, :, 0:DH], ps[b % 4][:].rearrange("p a (g d) -> p (a g) d", d=DH),
                                            w_b[:].rearrange("p (h d) -> p h d", d=DH), ALU.add).then_inc(wx_out, 1)
                    if b:
                        reduce(b - 1)
                reduce(NB - 1)
                for u in range(2 * NB):
                    i, half = u // 2, u % 2
                    dve.wait_ge(cnt_ready, u + 1)
                    if u >= 2:
                        dve.wait_ge(lnready, u - 1)
                    got = ps[u % 4][:].rearrange("p a b -> p (a b)")
                    nc.vector.tensor_scalar(log_num[:, i, half * D:half * D + D], got, 0.5, -BIG, ALU.is_lt,
                                            ALU.mult).then_inc(cnt_out, 1)
                    nc.vector.tensor_scalar(atleast[:, u % 2, :], got, 1.0, None, ALU.max).then_inc(cnt_out, 1)
                dve.wait_ge(mask_t_made, NB)
                for h in range(HEADS):
                    dve.wait_ge(s_bcast, 2 * h + 2)
                    for b in range(NB):
                        dve.wait_ge(maxed, h * NB + b) if h + b else None
                        nc.vector.tensor_tensor_reduce(out=junk, in0=s_ps[h % 2][:], in1=mask_t[:, b, :], scale=1.0,
                                                       scalar=-3e38, op0=ALU.add, op1=ALU.max,
                                                       accum_out=top[:, h, b:b + 1]).then_inc(maxed, 1)
                dve.wait_ge(maxed, HEADS * NB)
                chain(nc.vector.tensor_tensor(t_j[:], t_j[:], a_b[:].unsqueeze(2).to_broadcast([P, HEADS, NB]),
                                              ALU.add))
                chain(nc.vector.tensor_tensor(top[:], top[:], t_j[:], ALU.add))
                chain(nc.vector.scalar_tensor_tensor(top[:], top[:], 0.2, top[:], ALU.mult, ALU.max))
                chain(nc.vector.tensor_tensor(arg[:, 0, :, :], t_j[:], top[:], ALU.subtract))
                chain(nc.vector.scalar_tensor_tensor(arg[:, 1, :, :], t_j[:], 0.2, top[:], ALU.mult, ALU.subtract))
                chain(nc.vector.tensor_scalar(s_low[:], s_i[:], 0.2, None, ALU.mult))

        with ExitStack() as stack, nc.Block() as block:
            sb = lambda name, shape, dtype=F32: sbuf(c, name, shape, dtype, stack)
            diag = sb("diag2", [P, 4, 4, P])
            args = sb("args", [P, 2, 2, N])
            low = sb("low_slope", [P, SLOTS, N])
            score = sb("score", [P, SLOTS, N])
            prob = sb("prob", [P, SLOTS, N])
            head = sb("head", [P, NB, DH])
            den = sb("den", [P, 2, NB])
            bc_ps = [psum(c, f"bc_ps{b}", [P, D], stack) for b in range(2)]
            pv_ps = [psum(c, f"pv_ps{b}", [P, 2, D], stack) for b in range(2)]
            turns = HEADS // 2

            @block.gpsimd
            def _(pool):
                def diagonals(i, h):
                    for u in range(4):
                        pool.wait_ge(bc_ready, i * 8 + (4 * h + u + 1))
                        nc.gpsimd.tensor_tensor(
                            diag[:, u, :, :], c.ident[:].unsqueeze(1).to_broadcast([P, 4, P]),
                            arg[:, u // 2, bass.ds(i * 2 + h, 1), 4 * (u % 2):4 * (u % 2) + 4]
                            .rearrange("p o b -> p (o b)").unsqueeze(2).to_broadcast([P, 4, P]), ALU.mult) \
                            .then_inc(diag_ready, 1)

                def pair(i, ends=False):
                    for h in range(2):
                        if not (ends and h):
                            diagonals(i, h + 1)
                        for b in ON_POOL:
                            n = NB * h + b
                            pool.wait_ge(scored, i * PAIR + (SCORED0 + n + 1))
                            nc.gpsimd.tensor_tensor(score[:, b % SLOTS, :], score[:, b % SLOTS, :], log_num[:, b, :],
                                                    ALU.add).then_inc(masked_pool, 1)

                diagonals(0, 0)
                with pool.Fori(0, turns - 1) as i:
                    pair(i)
                pair(turns - 1, True)

            @block.tensor
            def _(pe):
                pe.sem_inc(bc_ready, 4)

                def broadcast(i, h, u):
                    pe.wait_ge(diag_ready, i * 8 + (4 * h + u + 1))
                    pe.wait_ge(bc_out, i * 8 + (4 * h + u + 1))
                    nc.tensor.matmul(bc_ps[u % 2][:], c.ones[:], diag[:, u, :, :], start=True, stop=True) \
                        .then_inc(bc_ready, 1)

                def pair(i, ends=False):
                    for h in range(2):
                        pe.wait_ge(heads_out, i * 2 + (h + 1))
                        for bank in range(2):
                            nc.tensor.matmul(pv_ps[h][:, bank, 0:4 * (DH + 1)], zero[:, 0:P], zero[:],
                                             start=True, stop=False)
                        for b in range(NB):
                            pe.wait_ge(probs_ready, i * PAIR + (NB * h + b + SLOTS + 1))
                            for j in range(NB):
                                at = (j % 4) * (DH + 1)
                                last = nc.tensor.matmul(pv_ps[h][:, j // 4, at:at + DH + 1],
                                                        prob[:, b % SLOTS, j * P:j * P + P],
                                                        wx[:, b, bass.ds(i * 2 + h, 1), :],
                                                        start=False, stop=(b == NB - 1 and j % 4 == 3))
                            last.then_inc(probs_used, 1)
                            if b < 4 and not (ends and h):
                                broadcast(i, h + 1, b)

                for u in range(4):
                    broadcast(0, 0, u)
                with pe.Fori(0, turns - 1) as i:
                    pair(i)
                pair(turns - 1, True)

            @block.scalar
            def _(act):
                def take(i, h, u):
                    act.wait_ge(bc_ready, i * 8 + (4 * h + u + 5))
                    act.wait_ge(scored, i * PAIR + (NB * h + SLOTS))
                    nc.scalar.copy(args[:, h % 2, u // 2, (u % 2) * D:(u % 2) * D + D], bc_ps[u % 2][:]) \
                        .then_inc(bc_out, 1)

                def low_slope(i, n):
                    h, b = n // NB, n % NB
                    act.wait_ge(bc_out, i * 8 + (4 * h + 6))
                    act.wait_ge(scored, i * PAIR + (n + 1 + SCORED0 - SLOTS))
                    nc.scalar.activation(low[:, b % SLOTS, :], args[:, h % 2, 1, :], ACT.Identity,
                                         bias=s_low[:, bass.ds(i * 2 + h, 1), b]).then_inc(low_ready, 1)

                def exponential(i, n):
                    h, b = n // NB, n % NB
                    if b in ON_POOL:
                        act.wait_ge(masked_pool, i * (2 * len(ON_POOL)) + (len(ON_POOL) * h + ON_POOL.index(b) + 1))
                    else:
                        act.wait_ge(masked_dve, i * (2 * len(ON_DVE)) + (len(ON_DVE) * h + ON_DVE.index(b) + 1))
                    act.wait_ge(probs_used, i * PAIR + (n + 1))
                    nc.scalar.activation(prob[:, b % SLOTS, :], score[:, b % SLOTS, :], ACT.Exp) \
                        .then_inc(probs_ready, 1)

                def pair(i, ends=False):
                    for n in range(PAIR):
                        h, b = n // NB, n % NB
                        if 1 <= b <= 4 and not (ends and h):
                            take(i, h + 1, b - 1)
                        if not (ends and n + AHEAD >= PAIR):
                            low_slope(i, n + AHEAD)
                        exponential(i, n)

                act.sem_inc(bc_out, 2)
                act.sem_inc(probs_ready, SLOTS)
                act.sem_inc(probs_used, SLOTS)
                for u in range(4):
                    take(0, 0, u)
                for n in range(AHEAD):
                    low_slope(0, n)
                with act.Fori(0, turns - 1) as i:
                    pair(i)
                pair(turns - 1, True)
                root(act)

            @block.vector
            def _(dve):
                chain, turn, close = chained(dve, pool_step)
                dve.sem_inc(scored, SCORED0)
                dve.sem_inc(heads_out, 2)

                def make_score(i, n):
                    h, b = n // NB, n % NB
                    dve.wait_ge(low_ready, i * PAIR + (n + 1))
                    dve.wait_ge(probs_ready, i * PAIR + (n + 1))
                    nc.vector.scalar_tensor_tensor(score[:, b % SLOTS, :], args[:, h, 0, :],
                                                   s_i[:, bass.ds(i * 2 + h, 1), b], low[:, b % SLOTS, :],
                                                   ALU.add, ALU.max).then_inc(scored, 1)

                def mask(i, n):
                    b = n % NB
                    dve.wait_ge(scored, i * PAIR + (SCORED0 + n + 1))
                    nc.vector.tensor_tensor(score[:, b % SLOTS, :], score[:, b % SLOTS, :], log_num[:, b, :],
                                            ALU.add).then_inc(masked_dve, 1)

                def divide(i, h):
                    got = pv_ps[h][:, :, 0:4 * (DH + 1)].rearrange("p k (j d) -> p k j d", d=DH + 1)
                    d = den[:, h, :].rearrange("p (k j) -> p k j", j=4)
                    chain(nc.vector.tensor_scalar(d, got[:, :, :, DH], 1e-30, None, ALU.max))
                    chain(nc.vector.reciprocal(d, d))
                    nc.vector.tensor_tensor(head[:].rearrange("p (k j) d -> p k j d", j=4), got[:, :, :, 0:DH],
                                            d.unsqueeze(3).to_broadcast([P, 2, 4, DH]), ALU.mult) \
                        .then_inc(heads_out, 1)
                    dve.wait_ge(heads_out, i * 2 + (h + 3))
                    to = c.x[:, :, bass.ds(i * (2 * DH) + h * DH, DH)]
                    chain(nc.vector.tensor_tensor(to, to, head[:], ALU.add))

                def pair(i, before=None):
                    for n in range(PAIR):
                        make_score(i, n)
                        if n % NB and (n - 1) % NB in ON_DVE:
                            mask(i, n - 1)
                        if n == NB + 2:
                            dve.wait_ge(probs_used, i * PAIR + (NB + SLOTS))
                            divide(i, 0)
                        if n % NB == NB - 1 and NB - 1 in ON_DVE:
                            mask(i, n)
                    dve.wait_ge(probs_used, i * PAIR + (PAIR + SLOTS))
                    divide(i, 1)

                with dve.Fori(0, turns) as i:
                    turn(i, 6)
                    pair(i)
                close(turns)
                for b in range(NB):
                    measure(b, c.x[:, b, :])
                scale(dve, chain, lambda b: c.x[:, b, :], lambda b: c.x[:, b, :])


HID = 32
Q_AT, P1_AT, X_AT = 0, HID, HID + 3 * MUL
ROW = X_AT + D
FAR = ROW - P1_AT
LAGS = 5
UNROLL = 6
HEAD = 10


def staged(engine, stages):
    assert (S - HEAD) % UNROLL == 0 and HEAD >= LAGS
    for u in range(HEAD):
        for lag, stage in stages:
            if u >= lag:
                stage(u - lag, (u - lag) % UNROLL, (u - lag) // UNROLL)
    with engine.Fori(0, (S - HEAD) // UNROLL) as i:
        for k in range(UNROLL):
            for lag, stage in stages:
                ahead = HEAD + k - lag
                stage(i * UNROLL + ahead, ahead % UNROLL, i + ahead // UNROLL)
    for u in range(S, S + LAGS):
        for lag, stage in stages:
            if u - lag < S:
                stage(u - lag, (u - lag) % UNROLL, (u - lag) // UNROLL)


def interaction(c):
    nc = c.nc
    with ExitStack() as stack:
        c.far = nc.dram_tensor("far_rows", [N, FAR], F32, kind="Internal").ap()
        c.local_rows = nc.dram_tensor("local_rows", [T * P], F32, kind="Internal").ap()
        c.table = sbuf(c, "table", [P, NB, ROW], F32, stack)
        c.w_o = sbuf(c, "w_o", [P, 2, MUL], F32, stack)
        c.b_o = sbuf(c, "b_o", [P, MUL], F32, stack)
        c.w_s1 = sbuf(c, "w_s1", [P, 3, HID], F32, stack)
        c.w_f1 = sbuf(c, "w_f1", [HID, HID], F32, stack)
        c.w_2 = sbuf(c, "w_2", [2 * HID, 4 * MUL], F32, stack)
        interaction_nodes(c)
        c.sums = sbuf(c, "sums", [P, NB, D], F32, stack)
        interaction_edges(c)
        interaction_out(c)


def interaction_nodes(c):
    nc = c.nc
    (loaded, turned, turned_out, step, square_ready, norm_ready, g1_ready, g1_out, act_ready, hid_ready, g2_ready,
     g_ready, xg_ready, p0_ready, p0_out, near_ready, near_out, self_ready, table_ready, stored, exp_ready) = (
        semaphore(c, "node_" + n) for n in (
            "loaded", "turned", "turned_out", "step", "square_ready", "norm_ready", "g1_ready", "g1_out",
            "neg_bias", "hidden_ready", "g2_ready", "g_ready", "gated", "p0_ready", "p0_out", "near_ready",
            "near_out", "self_ready", "table_ready", "stored", "exp_ready"))
    places_turned, places_out = semaphore(c, "places_turned"), semaphore(c, "places_out")
    with ExitStack() as stack, nc.Block() as block:
        sb = lambda name, shape, dtype=F32: sbuf(c, name, shape, dtype, stack)
        tile_rows = sb("tile_rows", [P, 2, P])
        w_pre = sb("w_pre", [P, 2, MUL])
        w_nd = sb("w_nd", [P, 2, MUL])
        w_g = sb("w_g", [P, 2, 2, 2 * MUL])
        b_g = sb("b_g", [P, 2, 2])
        b_g_neg = sb("b_g_neg", [P, 2])
        b_pre = sb("b_pre", [P, 1])
        b_nd = sb("b_nd", [P, MUL])
        x_t = sb("x_t4", [P, 4, N])
        length = sb("length", [P, N])
        hidden = sb("hidden", [P, 2, N])
        gate = sb("gate", [P, 2, N])
        expo = sb("expo", [P, 2, D])
        p0_t = sb("p0_t", [P, N])
        ps = [psum(c, f"node_ps{b}", [P, D], stack) for b in range(8)]
        cols = dict(allow_slow_non_contiguous=True)

        @block.sync
        def _(sp):
            loads = [(w_pre[:, 0, :], "W_pre0"), (w_pre[:, 1, :], "W_pre1"), (w_nd[:, 0, :], "W_nd0"),
                     (w_nd[:, 1, :], "W_nd1"), (c.w_o[:, 0, :], "W_o0"), (c.w_o[:, 1, :], "W_o1"),
                     (c.w_f1[:], "W_f1"), (c.w_2[0:HID, :], "W_f2"), (c.w_2[HID:2 * HID, :], "W_s2")]
            for to, name in loads:
                sp.dma_start(to, c.ins["L2_gnn_" + name]).then_inc(loaded, 16)
            sp.dma_start(c.w_s1[:], c.ins["L2_gnn_W_s1"].rearrange("(a p) h -> p a h", p=P)).then_inc(loaded, 16)
            for n, name in enumerate(("g1", "g2")):
                sp.dma_start(w_g[:, n, :, :], c.ins["L2_gnn_W_" + name].rearrange("(a p) h -> p a h", p=P)) \
                    .then_inc(loaded, 16)
                sp.dma_start(b_g[:, n, :], c.ins["L2_gnn_b_" + name].rearrange("(a p) -> p a", p=P), **cols) \
                    .then_inc(loaded, 16)
            sp.dma_start(b_pre[:], c.ins["L2_gnn_b_pre0"].rearrange("(a p) -> p a", p=P), **cols) \
                .then_inc(loaded, 16)
            sp.dma_start(b_nd[:], c.ins["L2_gnn_b_nd0"].partition_broadcast(P)).then_inc(loaded, 16)
            sp.dma_start(c.b_o[:], c.ins["L2_gnn_b_o0"].partition_broadcast(P)).then_inc(loaded, 16)
            sp.wait_ge(places_out, 2)
            for n in range(2):
                t0, t1 = n * P, min(T, n * P + P)
                sp.dma_start(c.local_rows[t0 * P:t1 * P].rearrange("(t e) -> t e", e=P),
                             tile_rows[0:t1 - t0, n, :]).then_inc(stored, 16)
            sp.wait_ge(near_out, NB)
            sp.wait_ge(table_ready, NB)
            sp.dma_start(c.far.rearrange("(b p) r -> p b r", p=P), c.table[:, :, P1_AT:ROW]).then_inc(stored, 16)
            sp.wait_ge(stored, 48)
        all_loaded = 16 * 17

        @block.tensor
        def _(pe):
            for n in range(2):
                t0, t1 = n * P, min(T, n * P + P)
                nc.tensor.transpose(ps[6 + n][0:t1 - t0, 0:P], c.i_local[:, t0:t1], c.ident[:]) \
                    .then_inc(places_turned, 1)
            for b in range(NB):
                if b >= 4:
                    pe.wait_ge(turned_out, b - 3)
                to = ps[b % 4][:].rearrange("p (f n) -> p f n", f=4)
                nc.tensor.transpose(to[:, 0, :], c.x[:, b, 0:MUL], c.ident[:])
                vectors = c.x[:, b, MUL:D].rearrange("p (u m) -> p m u", m=3)
                for m in range(3):
                    last = nc.tensor.transpose(to[:, 1 + m, :], vectors[:, m, :], c.ident[:])
                last.then_inc(turned, 1)
            pe.wait_ge(turned_out, NB)
            pe.wait_ge(loaded, all_loaded)
            for half in range(2):
                nc.tensor.matmul(ps[4 + half][:], w_pre[:, 0, :], x_t[:, 0, half * D:half * D + D],
                                 start=True, stop=True).then_inc(p0_ready, 1)
            pe.wait_ge(norm_ready, 1)
            for o in range(2):
                for half in range(2):
                    cut = slice(half * D, half * D + D)
                    nc.tensor.matmul(ps[2 * o + half][:], w_g[:, 0, 0, o * P:o * P + P], x_t[:, 0, cut],
                                     start=True, stop=False)
                    nc.tensor.matmul(ps[2 * o + half][:], w_g[:, 0, 1, o * P:o * P + P], length[:, cut],
                                     start=False, stop=True).then_inc(g1_ready, 1)
            pe.wait_ge(p0_out, 2)
            pe.wait_ge(places_out, 2)
            for b in range(NB):
                if b >= 4:
                    pe.wait_ge(near_out, b - 3)
                to, cut = ps[4 + b % 4], slice(b * P, b * P + P)
                nc.tensor.matmul(to[:, Q_AT:Q_AT + HID], p0_t[:, cut], c.w_s1[:, 0, :], start=True, stop=False)
                nc.tensor.matmul(to[:, Q_AT:Q_AT + HID], p0_t[:, cut], c.w_s1[:, 1, :], start=False, stop=True)
                for m in range(3):
                    last = nc.tensor.matmul(to[:, P1_AT + m * MUL:P1_AT + (m + 1) * MUL], x_t[:, 1 + m, cut],
                                            w_pre[:, 1, :], start=True, stop=True)
                last.then_inc(near_ready, 1)
            pe.wait_ge(hid_ready, 4)
            for o in range(2):
                for half in range(2):
                    for k in range(2):
                        last = nc.tensor.matmul(ps[2 * o + half][:], w_g[:, 1, k, o * P:o * P + P],
                                                hidden[:, k, half * D:half * D + D], start=(k == 0), stop=(k == 1))
                    last.then_inc(g2_ready, 1)
            pe.wait_ge(g_ready, 4)
            pe.wait_ge(xg_ready, 3)
            for b in range(NB):
                if b >= 4:
                    pe.wait_ge(table_ready, b - 3)
                to, cut = ps[b % 4], slice(b * P, b * P + P)
                nc.tensor.matmul(to[:, 0:MUL], gate[:, 0, cut], w_nd[:, 0, :], start=True, stop=True)
                for m in range(3):
                    last = nc.tensor.matmul(to[:, (1 + m) * MUL:(2 + m) * MUL], x_t[:, 1 + m, cut], w_nd[:, 1, :],
                                            start=True, stop=True)
                last.then_inc(self_ready, 1)

        @block.scalar
        def _(act):
            for n in range(2):
                tiles = min(T, n * P + P) - n * P
                act.wait_ge(places_turned, n + 1)
                nc.scalar.copy(tile_rows[0:tiles, n, :], ps[6 + n][0:tiles, 0:P]).then_inc(places_out, 1)
            for b in range(NB):
                act.wait_ge(turned, b + 1)
                nc.scalar.copy(x_t[:, :, b * P:b * P + P], ps[b % 4][:].rearrange("p (f n) -> p f n", f=4)) \
                    .then_inc(turned_out, 1)
            act.wait_ge(loaded, all_loaded)
            for half in range(2):
                act.wait_ge(p0_ready, half + 1)
                nc.scalar.activation(p0_t[:, half * D:half * D + D], ps[4 + half][:], ACT.Identity,
                                     bias=b_pre[:, 0:1]).then_inc(p0_out, 1)
            act.wait_ge(square_ready, 1)
            nc.scalar.activation(length[:], length[:], ACT.Sqrt, scale=1.0 / 3.0).then_inc(norm_ready, 1)
            act.wait_ge(act_ready, 1)
            for o in range(2):
                for half in range(2):
                    u = 2 * o + half
                    act.wait_ge(g1_ready, u + 1)
                    if u >= 2:
                        act.wait_ge(hid_ready, u - 1)
                    nc.scalar.activation(expo[:, half, :], ps[u][:], ACT.Exp, bias=b_g_neg[:, o:o + 1],
                                         scale=-1.0).then_inc(exp_ready, 1)
            for b in range(NB):
                act.wait_ge(near_ready, b + 1)
                nc.scalar.copy(c.table[:, b, 0:X_AT], ps[4 + b % 4][:, 0:X_AT]).then_inc(near_out, 1)
            for o in range(2):
                for half in range(2):
                    u = 2 * o + half
                    act.wait_ge(g2_ready, u + 1)
                    nc.scalar.activation(gate[:, o, half * D:half * D + D], ps[u][:], ACT.Identity,
                                         bias=b_g[:, 1, o:o + 1]).then_inc(g_ready, 1)

        @block.vector
        def _(dve):
            chain, _, _ = chained(dve, step)
            dve.wait_ge(loaded, all_loaded)
            nc.vector.tensor_scalar(b_g_neg[:], b_g[:, 0, :], -1.0, None, ALU.mult).then_inc(act_ready, 1)
            chain(nc.vector.tensor_scalar(c.w_2[0:HID, 3 * MUL:], c.w_2[0:HID, 3 * MUL:], 3.0 ** -0.5, None,
                                          ALU.mult))
            dve.wait_ge(turned_out, NB)
            chain(nc.vector.tensor_tensor(length[:], x_t[:, 1, :], x_t[:, 1, :], ALU.mult))
            square = hidden[:, 0, :]
            for m in (2, 3):
                chain(nc.vector.tensor_tensor(square, x_t[:, m, :], x_t[:, m, :], ALU.mult))
                last = nc.vector.tensor_tensor(length[:], length[:], square, ALU.add)
                if m == 2:
                    chain(last)
            last.then_inc(square_ready, 1)
            for o in range(2):
                for half in range(2):
                    u = 2 * o + half
                    dve.wait_ge(exp_ready, u + 1)
                    e = expo[:, half, :]
                    chain(nc.vector.tensor_scalar(e, e, 1.0, None, ALU.add))
                    chain(nc.vector.reciprocal(e, e))
                    nc.vector.scalar_tensor_tensor(hidden[:, o, half * D:half * D + D], ps[u][:],
                                                   b_g[:, 0, o:o + 1], e, ALU.add, ALU.mult).then_inc(hid_ready, 1)
            dve.wait_ge(near_ready, NB)
            dve.wait_ge(g_ready, 4)
            for m in range(3):
                nc.vector.tensor_tensor(x_t[:, 1 + m, :], x_t[:, 1 + m, :], gate[:, 1, :], ALU.mult) \
                    .then_inc(xg_ready, 1)
            for b in range(NB):
                dve.wait_ge(self_ready, b + 1)
                chain(nc.vector.tensor_tensor(c.table[:, b, X_AT:X_AT + MUL], ps[b % 4][:, 0:MUL], b_nd[:], ALU.add))
                nc.vector.tensor_copy(c.table[:, b, X_AT + MUL:ROW], ps[b % 4][:, MUL:D]).then_inc(table_ready, 1)


def interaction_edges(c):
    nc = c.nc
    FIRST = dict(onehots_turned=3, near=3, products=1, inner=2, turned=2, turned_out=1, hidden=3, shifted=1,
                 filtered=2, filter_out=1, weights=2, dots=UNROLL, thirds=UNROLL, messages=UNROLL, sums=2, added=1)
    made = lambda name, u, per=1: u * per + (1 + FIRST[name]) * per
    free = lambda name, u, ring, per=1: u * per + (1 + FIRST[name] - ring) * per
    (hot_t_ready, near_ready, prod_ready, ip_ready, turned, turned_out, hid_ready, soft_shifted, filtered, filter_out,
     weights_ready, dots_ready, thirds_ready, msgs_ready, sums_ready, sums_added) = (semaphore(c, "edge_" + n) for n in FIRST)
    (hot_ready, soft_ready, soft_step, filt_f, step, index_copied, index_seen, index_made, sums_cleared, attr_ready,
     q_ready, fourth_ready) = (
         semaphore(c, "edge_" + n) for n in (
             "onehot_ready", "softplus_ready", "softplus_step", "attributes_filtered", "step", "index_copied",
             "index_seen", "indices_made", "sums_cleared", "attributes_ready", "near_scalars_ready", "fourth_ready"))
    arrived = c.gathered[GT:]
    places_arrived = [semaphore(c, f"places_arrived_{g}") for g in range(3)]
    STEPS = 3
    with ExitStack() as stack, nc.Block() as block:
        sb = lambda name, shape, dtype=F32: sbuf(c, name, shape, dtype, stack)
        far_node = sb("far_node", [P, T], I32)
        index = sb("far_index", [P, UNROLL * TPS], I32)
        half = sb("half", [P, 1])
        far = sb("far", [P, UNROLL, TPS, FAR])
        places = sb("places", [P, 3, SUP])
        hot_t = sb("hot_t", [P, 3, SUP])
        hot = sb("hot", [P, 2, TPS, P])
        attr = sb("attr", [P, 2, TPS, 32])
        attr_t = sb("attr_t", [HID, 2, SUP])
        q = sb("q", [P, 2, HID])
        inner = sb("inner", [P, 2, TPS, MUL])
        inner_t = sb("inner_t", [P, 2, SUP])
        soft = sb("soft", [2 * HID, 2, SUP])
        weight = sb("weight_e", [P, 2, TPS, 4, MUL])
        msg = sb("msg", [P, 2, TPS, 4, MUL])
        firsts = sb("firsts", [P, TPS, 2, MUL])
        dot = sb("dot", [P, TPS, MUL])
        near_ps = psum(c, "near_ps", [P, TPS, D], stack)
        turn_ps = psum(c, "turn_ps", [P, 2, SUP], stack)
        hid_ps = psum(c, "hid_ps", [P, 2 * SUP], stack)
        f_ps = psum(c, "f_ps", [P, D], stack)
        s_ps = psum(c, "s_ps", [P, TPS, D], stack)
        sum_ps = psum(c, "sum_ps", [P, D], stack)

        @block.sync
        def _(sp):
            def load_places(u, r, turn):
                sp.wait_ge(hot_t_ready, free("onehots_turned", u, 3))
                sp.dma_start(places[:, r % 3, :], c.local_rows[bass.ds(u * SUP, SUP)].partition_broadcast(P)) \
                    .then_inc(places_arrived[r % 3], 16)

            staged(sp, [(0, load_places)])

        @block.gpsimd
        def _(pool):
            pool.sem_inc(ip_ready, 2 * FIRST["inner"])
            pool.sem_inc(thirds_ready, FIRST["thirds"])

            def gather(u, r, turn):
                pool.wait_ge(msgs_ready, free("messages", u, UNROLL))
                pool.wait_ge(thirds_ready, free("thirds", u, UNROLL))
                for k in range(TPS):
                    g = TPS * r + k
                    nc.gpsimd.tensor_copy(index[:, g:g + 1], far_node[:, bass.ds(u * TPS + k, 1)]) \
                        .then_inc(index_copied, 1)
                    pool.wait_ge(index_copied, u * TPS + (k + 1))
                    pool.sem_inc(index_seen, 1)
                    nc.gpsimd.indirect_dma_start(far[:, r, k, :], None, c.far[:, :],
                                                 bass.IndirectOffsetOnAxis(ap=index[:, g:g + 1], axis=0)) \
                        .then_inc(arrived[g], 16)

            def take_fixed(u, r, turn):
                pool.wait_ge(turned, free("turned", u, 2))
                nc.gpsimd.tensor_copy(attr[:, r % 2, :, :], c.recs[:, bass.ds(u * TPS, TPS), 0:32]) \
                    .then_inc(attr_ready, 1)
                block_of = pool.value_load(c.block_reg[0:1, bass.ds(u, 1)], min_val=0, max_val=NB - 1)
                pool.wait_ge(hid_ready, free("hidden", u, 2))
                nc.gpsimd.tensor_copy(q[:, r % 2:r % 2 + 1, :], c.table[:, bass.ds(block_of, 1), Q_AT:Q_AT + HID]) \
                    .then_inc(q_ready, 1)

            def add_inner(u, r, turn):
                b = r % 2
                pool.wait_ge(prod_ready, made("products", u))
                pool.wait_ge(turned, free("turned", u, 2))
                nc.gpsimd.tensor_tensor(inner[:, b, :, :], far[:, r, :, 0:MUL], far[:, r, :, MUL:2 * MUL], ALU.add) \
                    .then_inc(ip_ready, 1)
                pool.wait_ge(ip_ready, u * 2 + (1 + 2 * FIRST["inner"]))
                nc.gpsimd.tensor_tensor(inner[:, b, :, :], inner[:, b, :, :], far[:, r, :, 2 * MUL:3 * MUL],
                                        ALU.add) \
                    .then_inc(ip_ready, 1)

            def thirds(u, r, turn):
                b = r % 2
                pool.wait_ge(weights_ready, made("weights", u))
                pool.wait_ge(sums_ready, free("sums", u, 2))
                nc.gpsimd.tensor_tensor(
                    msg[:, b, :, 1:4, :], far[:, r, :, 4 * MUL:].rearrange("p k (m v) -> p k m v", m=3),
                    weight[:, b, :, 2:3, :].to_broadcast([P, TPS, 3, MUL]), ALU.mult).then_inc(thirds_ready, 1)

            pool.wait_ge(index_made, 1)
            staged(pool, [(0, gather), (1, take_fixed), (1, add_inner), (3, thirds)])

        @block.tensor
        def _(pe):
            for semaphore, name in ((near_ready, "near"), (turned, "turned"), (hid_ready, "hidden"),
                                    (filtered, "filtered"), (sums_ready, "sums")):
                pe.sem_inc(semaphore, FIRST[name])

            def gather_near(u, r, turn):
                block_of = pe.value_load(c.block_reg[0:1, bass.ds(u, 1)], min_val=0, max_val=NB - 1)
                pe.wait_ge(hot_t_ready, made("onehots_turned", u))
                pe.wait_ge(prod_ready, free("products", u, 1))
                for k in range(TPS):
                    last = nc.tensor.matmul(near_ps[:, k, 0:3 * MUL], hot_t[:, r % 3, k * P:k * P + P],
                                            c.table[:, bass.ds(block_of, 1), P1_AT:X_AT], start=True, stop=True)
                last.then_inc(near_ready, 1)

            def turn_inner(u, r, turn):
                pe.wait_ge(attr_ready, u + 1)
                pe.wait_ge(ip_ready, made("inner", u, 2))
                pe.wait_ge(turned_out, free("turned_out", u, 1, 2))
                for k in range(TPS):
                    nc.tensor.transpose(turn_ps[:, 0, k * P:k * P + P], inner[:, r % 2, k, :], c.ident[:])
                for k in range(TPS):
                    last = nc.tensor.transpose(turn_ps[0:HID, 1, k * P:k * P + P], attr[:, r % 2, k, :], c.ident[:])
                last.then_inc(turned, 1)

            def hidden(u, r, turn):
                b = r % 2
                pe.wait_ge(turned_out, made("turned_out", u, 2))
                pe.wait_ge(q_ready, u + 1)
                pe.wait_ge(soft_shifted, free("shifted", u, 1))
                nc.tensor.matmul(hid_ps[HID:2 * HID, 0:SUP], c.w_s1[:, 2, :], inner_t[:, b, :], start=True, stop=False)
                nc.tensor.matmul(hid_ps[HID:2 * HID, 0:SUP], q[:, b, :], hot_t[:, r % 3, :], start=False, stop=True)
                nc.tensor.matmul(hid_ps[0:HID, 0:SUP], c.w_f1[:], attr_t[:, b, :], start=True, stop=True) \
                    .then_inc(hid_ready, 1)

            def filters(u, r, turn):
                b = r % 2
                pe.wait_ge(soft_shifted, made("shifted", u))
                pe.wait_ge(weights_ready, free("weights", u, 1))
                for k in range(TPS):
                    cut = slice(k * P, k * P + P)
                    pe.wait_ge(filter_out, u * (2 * TPS) + (2 * k + 2 * TPS * FIRST["filter_out"]))
                    nc.tensor.matmul(f_ps[:], soft[0:HID, b, cut], c.w_2[0:HID, :], start=True, stop=True) \
                        .then_inc(filt_f, 1)
                    last = nc.tensor.matmul(s_ps[:, k, :], soft[HID:2 * HID, b, cut], c.w_2[HID:2 * HID, :],
                                            start=True, stop=True)
                last.then_inc(filtered, 1)

            def add_up(u, r, turn):
                pe.wait_ge(hot_ready, u + 1)
                pe.wait_ge(msgs_ready, made("messages", u))
                pe.wait_ge(sums_added, free("added", u, 1))
                for k in range(TPS):
                    last = nc.tensor.matmul(sum_ps[:], hot[:, r % 2, k, :], msg[:, r % 2, k, :, :], start=(k == 0),
                                            stop=(k == TPS - 1))
                last.then_inc(sums_ready, 1)

            staged(pe, [(1, gather_near), (5, add_up), (2, turn_inner), (3, filters), (2, hidden)])

        @block.scalar
        def _(act):
            for semaphore, name in ((turned_out, "turned_out"), (filter_out, "filter_out")):
                act.sem_inc(semaphore, FIRST[name] * (2 if name == "turned_out" else 2 * TPS))

            act.wait_ge(sums_cleared, 2)
            nc.scalar.preload_act_table_set("natural_log_exp_and_others")

            def take_turned(u, r, turn):
                b = r % 2
                act.wait_ge(turned, made("turned", u))
                act.wait_ge(hid_ready, free("hidden", u, 2))
                nc.scalar.mul(inner_t[:, b, :], turn_ps[:, 0, :], 1.0 / 3.0).then_inc(turned_out, 1)
                nc.scalar.copy(attr_t[:, b, :], turn_ps[0:HID, 1, :]).then_inc(turned_out, 1)

            def take_hidden(u, r, turn):
                b = r % 2
                act.wait_ge(hid_ready, made("hidden", u))
                act.wait_ge(filtered, free("filtered", u, 2))
                to = soft[:, b, :]
                nc.scalar.activation(to, hid_ps[0:2 * HID, 0:SUP], ACT.Abs).then_inc(soft_step, 1)
                act.wait_ge(soft_step, u * 2 + 1)
                nc.scalar.activation(to, to, ACT.Exp, scale=-1.0).then_inc(soft_step, 1)
                act.wait_ge(soft_step, u * 2 + 2)
                nc.scalar.activation(to, to, ACT.Ln, scale=0.5, bias=half[0:2 * HID, 0:1]).then_inc(soft_ready, 1)

            def take_filter(u, r, turn):
                b = r % 2
                act.wait_ge(thirds_ready, free("thirds", u, 2))
                act.wait_ge(msgs_ready, free("messages", u, 2))
                for k in range(TPS):
                    act.wait_ge(filt_f, u * TPS + (k + 1))
                    got = f_ps[:].rearrange("p (a o v) -> p o a v", a=2, o=2)
                    to = weight[:, b, k, :, :].rearrange("p (a o) v -> p o a v", a=2)
                    sh0 = c.recs[:, bass.ds(u * TPS + k, 1), R_SH]
                    nc.scalar.activation(to[:, 0, :, :], got[:, 0, :, :], ACT.Copy, scale=sh0).then_inc(filter_out, 1)
                    nc.scalar.copy(to[:, 1, :, :], got[:, 1, :, :]).then_inc(filter_out, 1)

            def scale_vectors(u, r, turn):
                act.wait_ge(ip_ready, made("inner", u, 2))
                for k in range(TPS):
                    for m in range(3):
                        last = nc.scalar.activation(
                            far[:, r, k, m * MUL:(m + 1) * MUL], far[:, r, k, (4 + m) * MUL:(5 + m) * MUL], ACT.Copy,
                            scale=c.recs[:, bass.ds(u * TPS + k, 1), R_SH + 1 + m])
                last.then_inc(dots_ready, 1)

            act.sem_inc(dots_ready, FIRST["dots"])
            staged(act, [(3, scale_vectors), (2, take_turned), (3, take_filter), (2, take_hidden)])

        @block.vector
        def _(dve):
            nc.vector.tensor_copy(far_node[:], c.recs[:, :, R_J]).then_inc(index_made, 1)
            nc.vector.memset(c.sums[:], 0.0).then_inc(sums_cleared, 1)
            nc.vector.memset(half[:], 0.5).then_inc(sums_cleared, 1)
            dve.wait_ge(sums_cleared, 2)
            for semaphore, name in ((hot_t_ready, "onehots_turned"), (prod_ready, "products"),
                                    (soft_shifted, "shifted"), (weights_ready, "weights"),
                                    (msgs_ready, "messages"), (sums_added, "added")):
                dve.sem_inc(semaphore, FIRST[name])

            def one_hot_turned(u, r, turn):
                dve.wait_ge(places_arrived[r % 3], (turn * 2 + r // 3) * 16 + 16)
                dve.wait_ge(near_ready, free("near", u, 3))
                dve.wait_ge(hid_ready, free("hidden", u, 3))
                nc.vector.tensor_scalar(hot_t[:, r % 3, :], places[:, r % 3, :], c.iota_col[:, 0:1], None,
                                        ALU.is_equal).then_inc(hot_t_ready, 1)

            def one_hot(u, r, turn):
                dve.wait_ge(sums_ready, free("sums", u, 2))
                nc.vector.tensor_tensor(
                    hot[:, r % 2, :, :], c.iota_row[:].unsqueeze(1).to_broadcast([P, TPS, P]),
                    c.i_local[:, bass.ds(u * TPS, TPS)].unsqueeze(2).to_broadcast([P, TPS, P]), ALU.is_equal) \
                    .then_inc(hot_ready, 1)

            def product(u, r, turn):
                dve.wait_ge(near_ready, made("near", u))
                for k in range(TPS):
                    dve.wait_ge(arrived[TPS * r + k], turn * 16 + 16)
                nc.vector.tensor_tensor(far[:, r, :, 0:3 * MUL],
                                        near_ps[:, :, 0:3 * MUL], far[:, r, :, 0:3 * MUL], ALU.mult) \
                    .then_inc(prod_ready, 1)

            def shift(u, r, turn):
                dve.wait_ge(soft_ready, u + 1)
                nc.vector.scalar_tensor_tensor(soft[:, r % 2, :], hid_ps[0:2 * HID, 0:SUP], 0.0, soft[:, r % 2, :],
                                               ALU.max, ALU.add).then_inc(soft_shifted, 1)

            def weigh(u, r, turn):
                b = r % 2
                dve.wait_ge(filter_out, made("filter_out", u, 2 * TPS))
                dve.wait_ge(filtered, made("filtered", u))
                nc.vector.tensor_tensor(weight[:, b, :, :, :].rearrange("p k a v -> p k (a v)"),
                                        weight[:, b, :, :, :].rearrange("p k a v -> p k (a v)"), s_ps[:],
                                        ALU.mult).then_inc(weights_ready, 1)

            def messages(u, r, turn):
                b = r % 2
                scaled = lambda m: far[:, r, :, m * MUL:(m + 1) * MUL]
                dve.wait_ge(dots_ready, made("dots", u))
                nc.vector.tensor_tensor(dot[:], scaled(0), scaled(1), ALU.add).then_inc(step, 1)
                dve.wait_ge(weights_ready, made("weights", u))
                nc.vector.tensor_tensor(
                    firsts[:], far[:, r, :, 3 * MUL:4 * MUL].unsqueeze(2).to_broadcast([P, TPS, 2, MUL]),
                    weight[:, b, :, 0:2, :], ALU.mult).then_inc(step, 1)
                dve.wait_ge(step, u * STEPS + 1)
                nc.vector.tensor_tensor(dot[:], dot[:], scaled(2), ALU.add).then_inc(step, 1)
                dve.wait_ge(thirds_ready, made("thirds", u))
                dve.wait_ge(step, u * STEPS + 2)
                for k in range(TPS):
                    for m in range(3):
                        nc.vector.scalar_tensor_tensor(
                            msg[:, b, k, 1 + m, :], firsts[:, k, 1, :],
                            c.recs[:, bass.ds(u * TPS + k, 1), R_SH + 1 + m], msg[:, b, k, 1 + m, :], ALU.mult,
                            ALU.add)
                dve.wait_ge(step, u * STEPS + 3)
                nc.vector.tensor_tensor(dot[:], dot[:], weight[:, b, :, 3, :], ALU.mult).then_inc(fourth_ready, 1)
                dve.wait_ge(fourth_ready, u + 1)
                last = nc.vector.tensor_tensor(msg[:, b, :, 0, :], firsts[:, :, 0, :], dot[:], ALU.add)
                last.then_inc(msgs_ready, 1)
                dve.wait_ge(msgs_ready, made("messages", u))

            def take_sums(u, r, turn):
                block_of = dve.value_load(c.block_reg[0:1, bass.ds(u, 1)], min_val=0, max_val=NB - 1)
                dve.wait_ge(sums_ready, made("sums", u))
                dve.wait_ge(sums_added, free("added", u, 1))
                to = c.sums[:, bass.ds(block_of, 1), :]
                nc.vector.tensor_tensor(to, to, sum_ps[:].unsqueeze(1), ALU.add).then_inc(sums_added, 1)

            staged(dve, [(1, product), (3, shift), (0, one_hot_turned), (4, messages), (4, one_hot),
                         (5, take_sums), (3, weigh)])


def interaction_out(c):
    nc = c.nc
    own_added, turned, turned_out, out_ready, step = (semaphore(c, "inter_out_" + n) for n in (
        "own_added", "turned", "turned_out", "ready", "step"))
    with ExitStack() as stack, nc.Block() as block:
        sums_t = sbuf(c, "sums_t", [P, 4, N], F32, stack)
        scalars = sbuf(c, "scalars", [P, 2, MUL], F32, stack)
        measure, root, scale, measured = layer_norm(c, "interaction", stack)
        ps = [psum(c, f"inter_ps{b}", [P, D], stack) for b in range(4)]
        ps_out = [psum(c, f"inter_out_ps{b}", [P, D], stack) for b in range(4)]

        @block.vector
        def _(dve):
            chain, _, _ = chained(dve, step)
            for b in range(NB):
                nc.vector.tensor_tensor(c.sums[:, b, :], c.sums[:, b, :], c.table[:, b, X_AT:ROW], ALU.add) \
                    .then_inc(own_added, 1)
            for b in range(NB):
                dve.wait_ge(out_ready, b + 1)
                got = ps_out[b % 4]
                chain(nc.vector.tensor_tensor(scalars[:, b % 2, :], got[:, 0:MUL], c.b_o[:], ALU.add))
                vectors = c.x[:, b, MUL:D].rearrange("p (u m) -> p m u", m=3)
                nc.vector.scalar_tensor_tensor(vectors, vectors, 2.0, got[:, MUL:D].rearrange("p (m u) -> p m u", m=3),
                                               ALU.mult, ALU.add)
                chain(nc.vector.scalar_tensor_tensor(c.x[:, b, 0:MUL], c.x[:, b, 0:MUL], 2.0, scalars[:, b % 2, :],
                                                     ALU.mult, ALU.add))
                measure(b, c.x[:, b, :])
            scale(dve, chain, lambda b: c.x[:, b, :], lambda b: c.x[:, b, :])

        @block.scalar
        def _(act):
            for b in range(NB):
                act.wait_ge(turned, b + 1)
                nc.scalar.copy(sums_t[:, :, b * P:b * P + P], ps[b % 4][:].rearrange("p (f n) -> p f n", f=4)) \
                    .then_inc(turned_out, 1)
            root(act)

        @block.tensor
        def _(pe):
            for b in range(NB):
                pe.wait_ge(own_added, b + 1)
                if b >= 4:
                    pe.wait_ge(turned_out, b - 3)
                for f in range(4):
                    last = nc.tensor.transpose(ps[b % 4][:, f * P:f * P + P], c.sums[:, b, f * P:f * P + P],
                                               c.ident[:])
                last.then_inc(turned, 1)
            for b in range(NB):
                pe.wait_ge(turned_out, b + 1)
                if b >= 4:
                    pe.wait_ge(measured, b - 3)
                for f in range(4):
                    last = nc.tensor.matmul(ps_out[b % 4][:, f * P:f * P + P], sums_t[:, f, b * P:b * P + P],
                                            c.w_o[:, min(f, 1), :], start=True, stop=True)
                last.then_inc(out_ready, 1)


def graph_conv(c):
    nc = c.nc
    loaded, turned, turned_out, count_ready, beta_ready, beta_out, sum_ready, sum_out, own_ready, step, stored = (
        semaphore(c, "conv_" + n) for n in ("loaded", "turned", "turned_out", "counts_ready", "neighbour_ready",
                                     "neighbour_out", "sums_ready", "sums_out", "own_ready", "step", "stored"))
    with ExitStack() as stack, nc.Block() as block:
        sb = lambda name, shape, dtype=F32: sbuf(c, name, shape, dtype, stack)
        w_c = sb("w_c", [P, FB, D])
        w_n = sb("w_n", [P, FB, D])
        bias = sb("bias", [P, D])
        x_t = sb("x_t_conv", [P, FB, N])
        beta = sb("beta", [P, NB, D])
        inverse = sb("inverse", [P, NB])
        measure, root, scale, measured = layer_norm(c, "conv", stack)
        ps = [psum(c, f"conv_ps{b}", [P, D], stack) for b in range(4)]
        sum_ps = [psum(c, f"conv_sum_ps{b}", [P, D], stack) for b in range(2)]
        count_ps = psum(c, "count_ps", [P, NB], stack)

        @block.sync
        def _(sp):
            for to, name in ((w_n, "L3_gnn_wn"), (w_c, "L3_gnn_wc")):
                sp.dma_start(to[:], c.ins[name].rearrange("(f p) o -> p f o", p=P)).then_inc(loaded, 16)
            sp.dma_start(bias[:], c.ins["L3_gnn_bias"].partition_broadcast(P)).then_inc(loaded, 16)
            out = c.out.rearrange("(b p) d -> p b d", p=P)
            sp.wait_ge(step, 3 + 2 * NB)
            sp.dma_start(out, c.x[:]).then_inc(stored, 16)
            sp.wait_ge(stored, 16)

        @block.tensor
        def _(pe):
            for b in range(NB):
                if b >= 4:
                    pe.wait_ge(turned_out, b - 3)
                for f in range(FB):
                    last = nc.tensor.transpose(ps[b % 4][:, f * P:f * P + P], c.x[:, b, f * P:f * P + P], c.ident[:])
                last.then_inc(turned, 1)
            for i in range(NB):
                for b in range(NB):
                    last = nc.tensor.matmul(count_ps[:, i:i + 1], c.num_t[:, b, i * P:i * P + P], c.ones[:, 0:1],
                                            start=(b == 0), stop=(b == NB - 1))
            last.then_inc(count_ready, 1)
            pe.wait_ge(loaded, 48)
            pe.wait_ge(turned_out, NB)
            for b in range(NB):
                if b >= 4:
                    pe.wait_ge(beta_out, b - 3)
                for k in range(FB):
                    last = nc.tensor.matmul(ps[b % 4][:], x_t[:, k, b * P:b * P + P], w_n[:, k, :], start=(k == 0),
                                            stop=(k == FB - 1))
                last.then_inc(beta_ready, 1)
            pe.wait_ge(beta_out, NB)
            for i in range(NB):
                if i >= 2:
                    pe.wait_ge(sum_out, i - 1)
                for b in range(NB):
                    last = nc.tensor.matmul(sum_ps[i % 2][:], c.num_t[:, b, i * P:i * P + P], beta[:, b, :],
                                            start=(b == 0), stop=(b == NB - 1))
                last.then_inc(sum_ready, 1)
                if i >= 4:
                    pe.wait_ge(measured, i - 3)
                for k in range(FB):
                    last = nc.tensor.matmul(ps[i % 4][:], x_t[:, k, i * P:i * P + P], w_c[:, k, :], start=(k == 0),
                                            stop=(k == FB - 1))
                last.then_inc(own_ready, 1)

        @block.scalar
        def _(act):
            for b in range(NB):
                act.wait_ge(turned, b + 1)
                nc.scalar.copy(x_t[:, :, b * P:b * P + P], ps[b % 4][:].rearrange("p (f n) -> p f n", f=FB)) \
                    .then_inc(turned_out, 1)
            for b in range(NB):
                act.wait_ge(beta_ready, b + 1)
                nc.scalar.copy(beta[:, b, :], ps[b % 4][:]).then_inc(beta_out, 1)
            root(act)

        @block.vector
        def _(dve):
            chain, _, _ = chained(dve, step)
            dve.wait_ge(count_ready, 1)
            chain(nc.vector.reciprocal(inverse[:], count_ps[:]))
            dve.wait_ge(loaded, 48)
            dve.wait_ge(turned, NB)
            for b in range(NB):
                y = c.x[:, b, :]
                chain(nc.vector.tensor_tensor(y, y, bias[:], ALU.add))
                dve.wait_ge(sum_ready, b + 1)
                nc.vector.scalar_tensor_tensor(y, sum_ps[b % 2][:], inverse[:, b:b + 1], y, ALU.mult, ALU.add) \
                    .then_inc(sum_out, 1)
                dve.wait_ge(sum_out, b + 1)
                dve.wait_ge(own_ready, b + 1)
                chain(nc.vector.tensor_tensor(y, y, ps[b % 4][:], ALU.add))
                measure(b, y)
            scale(dve, chain, lambda b: c.x[:, b, :], lambda b: c.x[:, b, :])


def build_program(nc, ins, out):
    with ExitStack() as stack:
        c = Core()
        c.nc, c.stack, c.semaphores, c.used = nc, stack, ExitStack(), []
        c.ins, c.out = ins, out
        c.gathered = [stack.enter_context(nc.semaphore(f"gathered_{g}")) for g in range(GT + UNROLL * TPS)]
        constants(c)
        order_edges(c)
        clear_semaphores(c)
        c.x = sbuf(c, "x_sb", [P, NB, D])
        with ExitStack() as c.gcn_stack:
            build_adjacency(c)
            clear_semaphores(c)
            gcn(c)
            clear_semaphores(c)
        gat(c)
        clear_semaphores(c)
        interaction(c)
        clear_semaphores(c)
        graph_conv(c)



_INS = ['x', 'src', 'dst', 'edge_attr_32', 'edge_attr_4', 'edge_weight', 'L0_gnn_W_gcn', 'L0_gnn_b_gcn',
        'L0_gnn_W_mlp', 'L0_gnn_b_mlp', 'L1_gnn_Ws', 'L1_gnn_Wb', 'L1_gnn_a_w', 'L1_gnn_a_b', 'L2_gnn_W_pre0',
        'L2_gnn_b_pre0', 'L2_gnn_W_pre1', 'L2_gnn_W_nd0', 'L2_gnn_b_nd0', 'L2_gnn_W_nd1', 'L2_gnn_W_g1',
        'L2_gnn_b_g1', 'L2_gnn_W_g2', 'L2_gnn_b_g2', 'L2_gnn_W_f1', 'L2_gnn_W_f2', 'L2_gnn_W_s1', 'L2_gnn_W_s2',
        'L2_gnn_W_o0', 'L2_gnn_b_o0', 'L2_gnn_W_o1', 'L3_gnn_wc', 'L3_gnn_wn', 'L3_gnn_bias']


def kernel(**inputs):
    import numpy as _np
    import concourse.bacc as _bacc
    from concourse import mybir as _mybir
    from concourse.bass_utils import run_bass_kernel_spmd as _run

    nc = _bacc.Bacc("TRN2", target_bir_lowering=False, num_devices=1)
    arrays, aps = {}, {}
    for name in _INS:
        a = _np.ascontiguousarray(inputs[name])
        arrays[f"in_{name}"] = a
        aps[name] = nc.dram_tensor(f"in_{name}", a.shape, _mybir.dt.from_np(a.dtype), kind="ExternalInput").ap()
    out = nc.dram_tensor("out", (N, D), F32, kind="ExternalOutput").ap()
    build_program(nc, aps, out)
    r = _run(nc, [arrays], core_ids=[0])
    return r.results[0]["out"]
```

```python
from contextlib import ExitStack

import concourse.bass as bass
from concourse import mybir

F32 = mybir.dt.float32
BF16 = mybir.dt.bfloat16
I32 = mybir.dt.int32
I16 = mybir.dt.int16
ALU = mybir.AluOpType
ACT = mybir.ActivationFunctionType
AX = mybir.AxisListType.X

P = 128
N = 1024
NB = N // P
D = 512
FB = D // P
E = 17408
TE = E // P
SUP = 256
TPS = SUP // P
S = E // SUP + NB
T = S * TPS
GT = 8
REC = 39
R_SH, R_W, R_I, R_J = 32, 36, 37, 38
LAYERS = 2
HEADS, DH = 8, 64
MUL = 128
BIG = 1e30
EPS = 1e-5


class Core:
    pass


def sbuf(c, name, shape, dtype=F32, stack=None):
    return (stack or c.stack).enter_context(c.nc.sbuf_tensor(name, shape, dtype))


def psum(c, name, shape, stack, dtype=F32):
    return stack.enter_context(c.nc.psum_tensor(name, shape, dtype))


def semaphore(c, name):
    got = c.semaphores.enter_context(c.nc.semaphore(name))
    c.used.append(got)
    return got


def clear_semaphores(c):
    with c.nc.Block() as block:
        @block.sync
        def _(sp):
            for one in c.used:
                sp.sem_clear(one)
    c.semaphores.close()
    c.used = []


def chained(engine, finished):
    count, before, mark, size = [0], [0], [0], [0]

    def chain(instruction):
        instruction.then_inc(finished, 1)
        count[0] += 1
        engine.wait_ge(finished, before[0] + count[0])

    def turn(i, per):
        before[0], mark[0], size[0] = i * per, count[0], per

    def close(turns):
        assert count[0] - mark[0] == size[0], (count[0] - mark[0], size[0])
        before[0], count[0] = 0, mark[0] + turns * size[0]

    return chain, turn, close


def constants(c):
    nc = c.nc
    c.iota_node = sbuf(c, "iota_node", [P, N], I16)
    c.iota_row = sbuf(c, "iota_row", [P, P], BF16)
    c.iota_tile = sbuf(c, "iota_tile", [P, T], BF16)
    c.iota_sup = sbuf(c, "iota_sup", [P, S], F32)
    c.iota_col = sbuf(c, "iota_col", [P, 1])
    c.ident = sbuf(c, "ident", [P, P])
    c.before = sbuf(c, "before", [P, P])
    c.ones = sbuf(c, "ones", [P, P])
    made = semaphore(c, "constants_made")

    with nc.Block() as block:
        @block.gpsimd
        def _(pool):
            chain, _, _ = chained(pool, made)
            chain(nc.gpsimd.iota(c.iota_node[:], [[1, N]], base=0, channel_multiplier=0))
            chain(nc.gpsimd.iota(c.iota_row[:], [[1, P]], base=0, channel_multiplier=0,
                                 allow_small_or_imprecise_dtypes=True))
            chain(nc.gpsimd.iota(c.iota_tile[:], [[1, T]], base=0, channel_multiplier=0,
                                 allow_small_or_imprecise_dtypes=True))
            chain(nc.gpsimd.iota(c.iota_sup[:], [[1, S]], base=0, channel_multiplier=0,
                                 allow_small_or_imprecise_dtypes=True))
            chain(nc.gpsimd.iota(c.iota_col[:], [[0, 1]], base=0, channel_multiplier=1,
                                 allow_small_or_imprecise_dtypes=True))
            chain(nc.gpsimd.memset(c.ones[:], 1.0))
            chain(nc.gpsimd.memset(c.ident[:], 0.0))
            chain(nc.gpsimd.affine_select(out=c.ident[:], in_=c.ident[:], compare_op=ALU.not_equal, fill=1.0,
                                          base=0, pattern=[[-1, P]], channel_multiplier=1))
            chain(nc.gpsimd.memset(c.before[:], 0.0))
            chain(nc.gpsimd.affine_select(out=c.before[:], in_=c.before[:], compare_op=ALU.is_ge, fill=1.0,
                                          base=0, pattern=[[-1, P]], channel_multiplier=1))


def order_edges(c):
    nc = c.nc
    c.rows = nc.dram_tensor("records", [1 + E, REC], F32, kind="Internal").ap()
    loaded, loaded_attr, step, placed, attrs_in = (semaphore(c, n) for n in (
        "edges_loaded", "attributes_loaded", "order_step", "edges_placed", "attributes_copied"))
    rows_out, sums_ready, hot_ready, hot_used, perm_ready = (semaphore(c, n) for n in (
        "records_out", "prefix_ready", "places_hot", "places_hot_used", "rows_ready"))
    totals_ready, zero_made, row_numbers = semaphore(c, "totals_ready"), semaphore(c, "zero_made"), semaphore(c, "row_numbers")
    with ExitStack() as stack:
        sb = lambda name, shape, dtype=F32: sbuf(c, name, shape, dtype, stack)
        ends = sb("ends", [P, 2, TE], I32)
        attr32 = sb("attr32", [P, TE, 32])
        attr4 = sb("attr4", [P, TE, 4])
        weight = sb("weight", [P, TE])
        record = sb("record", [P, TE, REC])
        dummy = sb("empty_record", [1, REC])
        blk = sb("blk", [P, TE], I32)
        blk_f = sb("blk_f", [P, TE])
        in_block = sb("in_block", [P, NB, TE])
        upto = sb("upto", [P, NB, TE])
        onesrow = sb("onesrow", [P, TE])
        totals = sb("totals", [P, NB])
        first = sb("first", [P, NB])
        sups = sb("sups", [P, NB])
        sups_i = sb("sups_i", [P, NB], I32)
        sup_end = sb("sup_end", [P, NB])
        place = sb("place", [P, TE])
        term = sb("term", [P, TE])
        place_i = sb("place_i", [P, TE], I32)
        tmp_i = sb("tmp_i", [P, TE], I32)
        high = sb("high", [P, TE])
        low = sb("low", [P, TE])
        row_i = sb("row_i", [P, TE], I32)
        row_high = sb("row_high", [P, TE])
        row_low = sb("row_low", [P, TE])
        hot_low = sb("hot_low", [P, 2, GT, P], BF16)
        hot_row = sb("hot_row", [P, 2, GT, 2, T], BF16)
        zero = sb("zero", [P, 2 * T], BF16)
        row_f = sb("row_f", [P, T])
        sup_ge = sb("sup_ge", [P, S])
        counts_ps = psum(c, "counts_ps", [P, 2 * NB], stack)
        perm_ps = psum(c, "perm_ps", [P, 2 * T], stack)

        with nc.Block() as block:
            @block.sync
            def _(sp):
                sp.dma_start(ends[:, 0, :], c.ins["src"].rearrange("(p t) -> p t", p=P)).then_inc(loaded, 16)
                sp.dma_start(ends[:, 1, :], c.ins["dst"].rearrange("(p t) -> p t", p=P)).then_inc(loaded, 16)
                sp.dma_start(weight[:], c.ins["edge_weight"].rearrange("(p t) -> p t", p=P)).then_inc(loaded_attr, 16)
                sp.dma_start(attr4[:], c.ins["edge_attr_4"].rearrange("(p t) a -> p t a", p=P)).then_inc(loaded_attr, 16)
                sp.dma_start(attr32[:], c.ins["edge_attr_32"].rearrange("(p t) a -> p t a", p=P)).then_inc(loaded_attr, 16)
                load_gcn_inputs(c, sp)
                sp.wait_ge(attrs_in, 5)
                sp.dma_start(c.rows[1:, :].rearrange("(p t) r -> p (t r)", p=P),
                             record[:].rearrange("p t r -> p (t r)")).then_inc(rows_out, 16)
                sp.dma_start(c.rows[0:1, :], dummy[:]).then_inc(rows_out, 16)
                sp.wait_ge(rows_out, 32)

            @block.scalar
            def _(act):
                act.wait_ge(loaded, 32)
                nc.scalar.copy(record[:, :, R_I:R_I + 2], ends[:].rearrange("p e t -> p t e")).then_inc(attrs_in, 1)
                act.wait_ge(loaded_attr, 48)
                nc.scalar.copy(record[:, :, 0:32], attr32[:]).then_inc(attrs_in, 1)
                nc.scalar.copy(record[:, :, R_SH:R_SH + 4], attr4[:]).then_inc(attrs_in, 1)
                nc.scalar.copy(record[:, :, R_W], weight[:]).then_inc(attrs_in, 1)

            @block.gpsimd
            def _(pool):
                nc.gpsimd.iota(row_i[:], [[1, TE]], base=1, channel_multiplier=TE).then_inc(row_numbers, 1)
                pool.wait_ge(zero_made, 1)
                nc.gpsimd.memset(dummy[0:1, R_I:R_I + 1], -1.0).then_inc(attrs_in, 1)

            @block.vector
            def _(dve):
                nc.vector.memset(dummy[:], 0.0).then_inc(zero_made, 1)
                nc.vector.memset(zero[:], 0.0).then_inc(zero_made, 1)
                chain, _, _ = chained(dve, step)
                chain(nc.vector.memset(onesrow[:], 1.0))
                dve.wait_ge(loaded, 32)
                chain(nc.vector.tensor_single_scalar(blk[:], ends[:, 0, :], 7, op=ALU.arith_shift_right))
                chain(nc.vector.tensor_copy(blk_f[:], blk[:]))
                for b in range(NB):
                    last = nc.vector.tensor_scalar(in_block[:, b, :], blk_f[:], float(b), None, ALU.is_equal)
                chain(last)
                for b in range(NB):
                    last = nc.vector.tensor_tensor_scan(upto[:, b, :], onesrow[:], in_block[:, b, :], 0.0,
                                                        ALU.mult, ALU.add)
                chain(last)
                nc.vector.tensor_copy(totals[:], upto[:, :, TE - 1]).then_inc(totals_ready, 1)
                dve.wait_ge(sums_ready, 1)
                chain(nc.vector.tensor_scalar(sups[:], counts_ps[:, NB:2 * NB], float(SUP - 1), None, ALU.add))
                chain(nc.vector.tensor_copy(sups_i[:], sups[:]))
                chain(nc.vector.tensor_single_scalar(sups_i[:], sups_i[:], SUP.bit_length() - 1,
                                                     op=ALU.arith_shift_right))
                chain(nc.vector.tensor_copy(sups[:], sups_i[:]))
                chain(nc.vector.tensor_tensor_scan(sup_end[:], onesrow[:, 0:NB], sups[:], 0.0, ALU.mult, ALU.add))
                chain(nc.vector.tensor_tensor(first[:], sup_end[:], sups[:], ALU.subtract))
                chain(nc.vector.tensor_scalar(first[:], first[:], float(SUP), -1.0, ALU.mult, ALU.add))
                chain(nc.vector.tensor_tensor(first[:], first[:], counts_ps[:, 0:NB], ALU.add))
                for b in range(NB):
                    chain(nc.vector.scalar_tensor_tensor(term[:] if b else place[:], upto[:, b, :], first[:, b:b + 1],
                                                         in_block[:, b, :], ALU.add, ALU.mult))
                    if b:
                        chain(nc.vector.tensor_tensor(place[:], place[:], term[:], ALU.add))
                chain(nc.vector.tensor_copy(place_i[:], place[:]))
                chain(nc.vector.tensor_single_scalar(tmp_i[:], place_i[:], 7, op=ALU.arith_shift_right))
                chain(nc.vector.tensor_copy(high[:], tmp_i[:]))
                chain(nc.vector.tensor_single_scalar(tmp_i[:], place_i[:], P - 1, op=ALU.bitwise_and))
                chain(nc.vector.tensor_copy(low[:], tmp_i[:]))
                dve.wait_ge(row_numbers, 1)
                chain(nc.vector.tensor_single_scalar(tmp_i[:], row_i[:], 7, op=ALU.arith_shift_right))
                chain(nc.vector.tensor_copy(row_high[:], tmp_i[:]))
                chain(nc.vector.tensor_single_scalar(tmp_i[:], row_i[:], P - 1, op=ALU.bitwise_and))
                chain(nc.vector.tensor_copy(row_low[:], tmp_i[:]))
                with dve.Fori(0, TE // GT) as i:
                    half = i % 2
                    dve.wait_ge(hot_used, i + 1)
                    for g in range(GT):
                        t = i * GT + g
                        nc.vector.tensor_scalar(hot_low[:, bass.ds(half, 1), g, :], c.iota_row[:],
                                                low[:, bass.ds(t, 1)], None, ALU.is_equal)
                        nc.vector.tensor_scalar(hot_row[:, bass.ds(half, 1), g, 0, :], c.iota_tile[:],
                                                high[:, bass.ds(t, 1)], row_high[:, bass.ds(t, 1)],
                                                ALU.is_equal, ALU.mult)
                        last = nc.vector.tensor_scalar(hot_row[:, bass.ds(half, 1), g, 1, :], c.iota_tile[:],
                                                       high[:, bass.ds(t, 1)], row_low[:, bass.ds(t, 1)],
                                                       ALU.is_equal, ALU.mult)
                    last.then_inc(hot_ready, 1)
                dve.wait_ge(perm_ready, 1)
                chain(nc.vector.tensor_copy(row_f[:], perm_ps[:, T:2 * T]))
                chain(nc.vector.scalar_tensor_tensor(row_f[:], perm_ps[:, 0:T], float(P), row_f[:],
                                                     ALU.mult, ALU.add))
                chain(nc.vector.tensor_copy(c.row_of_place[:], row_f[:]))
                chain(nc.vector.tensor_scalar(c.block_of_sup[:], c.iota_sup[:], sup_end[:, 0:1], None, ALU.is_ge))
                for b in range(1, NB - 1):
                    chain(nc.vector.tensor_scalar(sup_ge[:], c.iota_sup[:], sup_end[:, b:b + 1], None, ALU.is_ge))
                    chain(nc.vector.tensor_tensor(c.block_of_sup[:], c.block_of_sup[:], sup_ge[:], ALU.add))
                chain(nc.vector.tensor_copy(c.block_reg[:], c.block_of_sup[:]))

            @block.tensor
            def _(pe):
                pe.wait_ge(totals_ready, 1)
                nc.tensor.matmul(counts_ps[:, 0:NB], c.before[:], totals[:], start=True, stop=True)
                nc.tensor.matmul(counts_ps[:, NB:2 * NB], c.ones[:], totals[:], start=True, stop=True) \
                    .then_inc(sums_ready, 1)
                pe.wait_ge(zero_made, 2)
                nc.tensor.matmul(perm_ps[:], zero[:, 0:P], zero[:], start=True, stop=False).then_inc(hot_used, 2)
                with pe.Fori(0, TE // GT) as i:
                    pe.wait_ge(hot_ready, i + 1)
                    half = i % 2
                    for g in range(GT):
                        last = nc.tensor.matmul(perm_ps[:], hot_low[:, bass.ds(half, 1), g, :],
                                                hot_row[:, bass.ds(half, 1), g, :, :], start=False, stop=False)
                    last.then_inc(hot_used, 1)
                nc.tensor.matmul(perm_ps[:], zero[:, 0:P], zero[:], start=False, stop=True).then_inc(perm_ready, 1)


def lasting_memory(c):
    c.recs = sbuf(c, "recs", [P, T, REC])
    c.i_local = sbuf(c, "i_local", [P, T])
    c.num_t = sbuf(c, "num_t", [P, NB, N])
    c.numbers = sbuf(c, "numbers", [P, NB])
    c.x = sbuf(c, "x_sb", [P, NB, D])
    c.block_reg = sbuf(c, "block_reg", [P, S], I32)
    c.block_of_sup = sbuf(c, "block_of_sup", [P, S], F32)
    c.row_of_place = sbuf(c, "row_of_place", [P, T], I32)


def build_adjacency(c):
    nc = c.nc
    turns = T // GT
    sups = GT // TPS
    cleared, row_copied, copied, step, onehots, parts, built, added = (semaphore(c, n) for n in (
        "matrices_cleared", "row_number_copied", "record_copied", "adjacency_step", "onehots_ready",
        "weighted_ready", "block_built", "block_added"))
    slot_free, row_seen = semaphore(c, "record_slot_free"), semaphore(c, "row_number_seen")
    arrived = c.gathered[0:GT]
    w_turned, w_turned_out, w_ready, w_out = (semaphore(c, n) for n in (
        "weights_turned", "weights_turned_out", "weights_multiplied", "weights_out"))
    stack = c.gcn_stack
    c.adj_t = sbuf(c, "adj_t", [P, NB, N], F32, stack)
    with ExitStack() as stack:
        sb = lambda name, shape, dtype=F32: sbuf(c, name, shape, dtype, stack)
        slots = sb("record_slots", [P, GT, REC])
        row_slots = sb("row_slots", [P, GT], I32)
        w_part = sb("w_part", [P, 3, 2, GT])
        w_rest = sb("w_rest", [P, GT])
        w_gcn_t = sb("w_gcn_t", [P, LAYERS, FB, D])
        b_wide = sb("b_wide", [P, LAYERS, FB, P])
        hot_j = sb("hot_j", [P, GT, N], BF16)
        hot_i = sb("hot_i", [P, GT, 4, P], BF16)
        built_ps = [psum(c, f"built_ps{b}", [P, NB, 2, P], stack) for b in range(2)]

        bank = [built_ps[q // 4][:, 2 * (q % 4):2 * (q % 4) + 2, :, :].rearrange("p a n e -> p (a n e)")
                for q in range(2 * FB)]

        with nc.Block() as block:
            @block.gpsimd
            def _(pool):
                nc.gpsimd.memset(c.adj_t[:], 0.0).then_inc(cleared, 1)
                nc.gpsimd.memset(c.num_t[:], 0.0).then_inc(cleared, 1)
                with pool.Fori(0, turns) as i:
                    for g in range(GT):
                        pool.wait_ge(slot_free, i * GT + (g + 1))
                        nc.gpsimd.tensor_copy(row_slots[:, g:g + 1], c.row_of_place[:, bass.ds(i * GT + g, 1)]) \
                            .then_inc(row_copied, 1)
                        pool.wait_ge(row_copied, i * GT + (g + 1))
                        pool.sem_inc(row_seen, 1)
                        nc.gpsimd.indirect_dma_start(
                            slots[:, g, :], None, c.rows[:, :],
                            bass.IndirectOffsetOnAxis(ap=row_slots[:, g:g + 1], axis=0)).then_inc(arrived[g], 16)

            @block.scalar
            def _(act):
                def copy_records(i):
                    for g in range(GT):
                        act.wait_ge(arrived[g], i * 16 + 16)
                        nc.scalar.copy(c.recs[:, bass.ds(i * GT + g, 1), :], slots[:, g:g + 1, :]) \
                            .then_inc(copied, 1)
                        act.wait_ge(copied, i * GT + (g + 1))
                        act.sem_inc(slot_free, 1)

                def weigh(i, s):
                    act.wait_ge(onehots, i * sups + (s + 1))
                    for t in range(TPS * s, TPS * s + TPS):
                        for part, at in enumerate((0, 2, 3)):
                            last = nc.scalar.activation(hot_i[:, t, at, :], hot_i[:, t, 1, :], ACT.Copy,
                                                        scale=w_part[:, part, 0, t:t + 1])
                    last.then_inc(parts, 1)

                act.sem_inc(slot_free, GT)
                act.wait_ge(c.gcn_in, c.gcn_inputs_in)
                for u in range(LAYERS * FB):
                    act.wait_ge(w_turned, u + 1)
                    nc.scalar.copy(w_gcn_t[:, u // FB, u % FB, :], bank[u]).then_inc(w_turned_out, 1)
                for l in range(LAYERS):
                    nc.scalar.copy(b_wide[:, l, :, :], c.b_gcn[:, l, :].unsqueeze(2).to_broadcast([P, FB, P])) \
                        .then_inc(w_turned_out, 1)
                copy_records(0)
                for u in range(LAYERS * FB):
                    act.wait_ge(w_ready, u + 1)
                    nc.scalar.copy(c.w_gcn[:, u // FB, u % FB, :], bank[u]).then_inc(w_out, 1)
                copy_records(1)
                for s in range(sups):
                    weigh(0, s)
                with act.Fori(0, turns - 2) as i:
                    weigh(i + 1, 0)
                    weigh(i + 1, 1)
                    copy_records(i + 2)
                    for s in range(2, sups):
                        weigh(i + 1, s)
                for s in range(sups):
                    weigh(turns - 1, s)

            @block.vector
            def _(dve):
                chain, turn, close = chained(dve, step)

                def split_weights(i):
                    dve.wait_ge(copied, i * GT + GT)
                    rec = c.recs[:, bass.ds(i * GT, GT), :]
                    w1, w2, w3 = (w_part[:, n, 0, :] for n in range(3))
                    chain(nc.vector.tensor_single_scalar(w1.bitcast(I32), rec[:, :, R_W].bitcast(I32), -65536,
                                                         op=ALU.bitwise_and))
                    chain(nc.vector.tensor_tensor(w_rest[:], rec[:, :, R_W], w1, ALU.subtract))
                    nc.vector.scalar_tensor_tensor(
                        c.i_local[:, bass.ds(i * GT, GT)].rearrange("p (s k) -> p s k", k=TPS),
                        c.block_of_sup[:, bass.ds(i * sups, sups)].unsqueeze(2).to_broadcast([P, sups, TPS]),
                        -float(P), rec[:, :, R_I].rearrange("p (s k) -> p s k", k=TPS), ALU.mult, ALU.add)
                    chain(nc.vector.tensor_single_scalar(w2.bitcast(I32), w_rest[:].bitcast(I32), -65536,
                                                         op=ALU.bitwise_and))
                    chain(nc.vector.tensor_tensor(w3, w_rest[:], w2, ALU.subtract))

                def one_hot(i, s):
                    t0 = TPS * s
                    nc.vector.tensor_tensor(
                        hot_i[:, t0:t0 + TPS, 1, :], c.iota_row[:].unsqueeze(1).to_broadcast([P, TPS, P]),
                        c.i_local[:, bass.ds(i * GT + t0, TPS)].unsqueeze(2).to_broadcast([P, TPS, P]), ALU.is_equal)
                    for t in range(t0, t0 + TPS):
                        last = nc.vector.tensor_scalar(hot_j[:, t, :], c.iota_node[:],
                                                       c.recs[:, bass.ds(i * GT + t, 1), R_J], None, ALU.is_equal)
                    last.then_inc(onehots, 1)

                def add_block(i, s):
                    k = dve.value_load(c.block_reg[0:1, bass.ds(i * sups + s, 1)], min_val=0, max_val=NB - 1)
                    dve.wait_ge(built, i * sups + (s + 1))
                    dve.wait_ge(added, i * sups + (s + 2))
                    for n, m in enumerate((c.adj_t, c.num_t)):
                        to = m[:, :, bass.ds(k * P, P)]
                        last = nc.vector.tensor_tensor(to, to, built_ps[s % 2][:, :, n, :], ALU.add)
                    last.then_inc(added, 1)

                dve.wait_ge(cleared, 2)
                split_weights(0)
                for s in range(sups):
                    one_hot(0, s)
                for l in range(LAYERS):
                    dve.wait_ge(w_ready, LAYERS * FB + l + 1)
                    chain(nc.vector.tensor_tensor(c.bias[:, l, :], bank[l], c.b_mlp[:, l, :], ALU.add))
                dve.sem_inc(added, 2)
                with dve.Fori(0, turns - 1) as i:
                    turn(i, 4)
                    add_block(i, 0)
                    dve.wait_ge(parts, i * sups + sups)
                    split_weights(i + 1)
                    one_hot(i + 1, 0)
                    for s in range(1, sups):
                        add_block(i, s)
                        one_hot(i + 1, s)
                close(turns - 1)
                for s in range(sups):
                    add_block(turns - 1, s)

            @block.tensor
            def _(pe):
                pe.wait_ge(c.gcn_in, c.gcn_inputs_in)
                for u in range(LAYERS * FB):
                    for k in range(FB):
                        last = nc.tensor.transpose(bank[u][:, k * P:k * P + P],
                                                   c.w_gcn[:, u // FB, k, (u % FB) * P:(u % FB) * P + P], c.ident[:])
                    last.then_inc(w_turned, 1)
                pe.wait_ge(w_turned_out, LAYERS * (FB + 1))
                for u in range(LAYERS * FB):
                    l, f = u // FB, u % FB
                    for k in range(FB):
                        last = nc.tensor.matmul(bank[u], w_gcn_t[:, l, k, f * P:f * P + P], c.w_mlp[:, l, k, :],
                                                start=(k == 0), stop=(k == FB - 1))
                    last.then_inc(w_ready, 1)
                for l in range(LAYERS):
                    pe.wait_ge(w_out, l + 1)
                    for k in range(FB):
                        last = nc.tensor.matmul(bank[l], b_wide[:, l, k, :], c.w_mlp[:, l, k, :],
                                                start=(k == 0), stop=(k == FB - 1))
                    last.then_inc(w_ready, 1)
                pe.wait_ge(w_out, LAYERS * FB)
                with pe.Fori(0, turns) as i:
                    for s in range(sups):
                        pe.wait_ge(onehots, i * sups + (s + 1))
                        pe.wait_ge(parts, i * sups + (s + 1))
                        pe.wait_ge(added, i * sups + (s + 1))
                        for b in range(NB):
                            to = built_ps[s % 2]
                            for k in range(TPS):
                                t = TPS * s + k
                                hj = hot_j[:, t, b * P:(b + 1) * P]
                                nc.tensor.matmul(to[:, b, :, :], hj, hot_i[:, t, 0:2, :], start=(k == 0), stop=False)
                                nc.tensor.matmul(to[:, b, 0, :], hj, hot_i[:, t, 2, :], start=False, stop=False)
                                last = nc.tensor.matmul(to[:, b, 0, :], hj, hot_i[:, t, 3, :], start=False,
                                                        stop=(k == TPS - 1))
                        last.then_inc(built, 1)


def layer_norm(c, name, stack):
    nc = c.nc
    stats = sbuf(c, f"stats_{name}", [P, NB, 6], F32, stack)
    moments = sbuf(c, f"moments_{name}", [P, NB, 2], F32, stack)
    spread = sbuf(c, f"spread_{name}", [P, NB], F32, stack)
    measured, variance_ready, root_ready = (
        semaphore(c, f"{what}_{name}") for what in ("blocks_measured", "variance_ready", "roots_ready"))

    def measure(b, y):
        nc.vector.bn_stats(stats[:, b, :], y).then_inc(measured, 1)

    def root(act):
        act.wait_ge(variance_ready, 2)
        nc.scalar.activation(spread[:], spread[:], ACT.Sqrt).then_inc(root_ready, 1)

    def scale(dve, chain, y, out):
        dve.wait_ge(measured, NB)
        for b in range(NB):
            last = nc.vector.bn_aggr(moments[:, b, :], stats[:, b, :])
        last.then_inc(variance_ready, 1)
        dve.wait_ge(variance_ready, 1)
        nc.vector.tensor_scalar(spread[:], moments[:, :, 1], EPS, None, ALU.add).then_inc(variance_ready, 1)
        dve.wait_ge(root_ready, 1)
        chain(nc.vector.reciprocal(spread[:], spread[:]))
        for b in range(NB):
            last = nc.vector.tensor_scalar(out(b), y(b), moments[:, b, 0:1], spread[:, b:b + 1],
                                           ALU.subtract, ALU.mult)
        chain(last)

    return measure, root, scale, measured


def gcn_inputs(c):
    stack = c.gcn_stack
    c.w_gcn = sbuf(c, "w_gcn", [P, LAYERS, FB, D], F32, stack)
    c.w_mlp = sbuf(c, "w_mlp", [P, LAYERS, FB, D], F32, stack)
    c.b_gcn = sbuf(c, "b_gcn", [P, LAYERS, FB], F32, stack)
    c.b_mlp = sbuf(c, "b_mlp", [P, LAYERS, D], F32, stack)
    c.bias = sbuf(c, "bias_gcn", [P, LAYERS, D], F32, stack)
    c.gcn_in = stack.enter_context(c.nc.semaphore("gcn_inputs_loaded"))


def load_gcn_inputs(c, sp):
    for l in range(LAYERS):
        sp.dma_start(c.w_gcn[:, l, :, :], c.ins["L0_gnn_W_gcn"][l].rearrange("(f p) o -> p f o", p=P)) \
            .then_inc(c.gcn_in, 16)
        sp.dma_start(c.w_mlp[:, l, :, :], c.ins["L0_gnn_W_mlp"][l].rearrange("(f p) o -> p f o", p=P)) \
            .then_inc(c.gcn_in, 16)
        sp.dma_start(c.b_gcn[:, l, :], c.ins["L0_gnn_b_gcn"][l].rearrange("(f p) -> p f", p=P),
                     allow_slow_non_contiguous=True).then_inc(c.gcn_in, 16)
        sp.dma_start(c.b_mlp[:, l, :], c.ins["L0_gnn_b_mlp"][l].partition_broadcast(P)).then_inc(c.gcn_in, 16)
    sp.dma_start(c.x[:], c.ins["x"].rearrange("(b p) d -> p b d", p=P)).then_inc(c.gcn_in, 16)
    c.gcn_inputs_in = 16 * (4 * LAYERS + 1)


def gcn(c):
    nc = c.nc
    layers = LAYERS
    deg_ready, safe_ready, root_ready, scaled, agg_ready, agg_out, out_ready, step, out_free = (
        semaphore(c, n) for n in ("degree_ready", "degree_safe", "degree_root", "gcn_scaled", "gcn_sums_ready",
                                  "gcn_sums_out", "gcn_out_ready", "gcn_step", "gcn_out_free"))
    roots_turned = semaphore(c, "degree_roots_turned")
    with ExitStack() as stack:
        sb = lambda name, shape, dtype=F32: sbuf(c, name, shape, dtype, stack)
        h = sb("h", [P, 4, D])
        hs = sb("hs", [P, NB, D])
        root_b = sb("root_b", [P, N])
        root_p = sb("root_p", [P, NB])
        junk = sb("junk_gcn", [P, 2, P])
        agg = sb("agg", [P, FB, N])
        there_b = agg[:, 0, :]
        measure, root, scale, measured = layer_norm(c, "gcn", stack)
        ps = [psum(c, f"gcn_ps{b}", [P, D], stack) for b in range(4)]
        deg_b = psum(c, "deg_b", [P, N], stack)
        out_ps = [psum(c, f"gcn_out_ps{b}", [P, D], stack) for b in range(2)]

        with nc.Block() as block:
            @block.tensor
            def _(pe):
                for half in range(2):
                    for b in range(NB):
                        last = nc.tensor.matmul(deg_b[:, half * D:half * D + D], c.ones[:],
                                                c.adj_t[:, b, half * D:half * D + D], start=(b == 0),
                                                stop=(b == NB - 1))
                last.then_inc(deg_ready, 1)
                for l in range(layers):
                    n = l * 2 * FB
                    for half in range(2):
                        for f in range(FB):
                            u = half * FB + f
                            if u >= 4 or l:
                                pe.wait_ge(agg_out, n + u - 3)
                            for b in range(NB):
                                pe.wait_ge(scaled, l * NB + b + 1)
                                last = nc.tensor.matmul(ps[u % 4][:], hs[:, b, f * P:f * P + P],
                                                        c.adj_t[:, b, half * D:half * D + D],
                                                        start=(b == 0), stop=(b == NB - 1))
                            last.then_inc(agg_ready, 1)
                    for b in range(NB):
                        pe.wait_ge(agg_out, n + (FB if b < NB // 2 else 2 * FB))
                        if b >= 2 or l:
                            pe.wait_ge(out_free, l * NB + b - 1)
                        for k in range(FB):
                            last = nc.tensor.matmul(out_ps[b % 2][:], agg[:, k, b * P:b * P + P],
                                                    c.w_gcn[:, l, k, :], start=(k == 0), stop=(k == FB - 1))
                        last.then_inc(out_ready, 1)

            @block.scalar
            def _(act):
                act.wait_ge(safe_ready, 1)
                nc.scalar.activation(root_b[:], root_b[:], ACT.Sqrt).then_inc(root_ready, 1)
                root(act)

            @block.vector
            def _(dve):
                chain, _, _ = chained(dve, step)
                dve.wait_ge(deg_ready, 1)
                chain(nc.vector.tensor_scalar(there_b, deg_b[:], 0.0, None, ALU.is_gt))
                chain(nc.vector.tensor_scalar(root_b[:], deg_b[:], 1e-30, None, ALU.max))
                nc.vector.reciprocal(root_b[:], root_b[:]).then_inc(safe_ready, 1)
                dve.wait_ge(root_ready, 1)
                chain(nc.vector.tensor_tensor(root_b[:], root_b[:], there_b, ALU.mult))
                for b in range(NB):
                    nc.vector.tensor_tensor_reduce(out=junk[:, b % 2, :], in0=root_b[:, b * P:b * P + P],
                                                   in1=c.ident[:], scale=1.0, scalar=0.0, op0=ALU.mult, op1=ALU.add,
                                                   accum_out=root_p[:, b:b + 1]).then_inc(roots_turned, 1)
                    if b:
                        dve.wait_ge(roots_turned, b)
                dve.wait_ge(roots_turned, NB)
                for b in range(NB):
                    nc.vector.tensor_scalar(hs[:, b, :], c.x[:, b, :], root_p[:, b:b + 1], None, ALU.mult) \
                        .then_inc(scaled, 1)
                for l in range(layers):
                    for half in range(2):
                        for f in range(FB):
                            u = half * FB + f
                            if l and u == 0:
                                dve.wait_ge(out_ready, l * NB)
                            dve.wait_ge(agg_ready, l * 2 * FB + u + 1)
                            nc.vector.tensor_tensor(agg[:, f, half * D:half * D + D], ps[u % 4][:],
                                                    root_b[:, half * D:half * D + D], ALU.mult).then_inc(agg_out, 1)
                    for b in range(NB):
                        dve.wait_ge(out_ready, l * NB + b + 1)
                        nc.vector.tensor_tensor(h[:, b % 4, :], out_ps[b % 2][:], c.bias[:, l, :], ALU.add) \
                            .then_inc(out_free, 1)
                        dve.wait_ge(out_free, l * NB + b + 1)
                        chain(nc.vector.scalar_tensor_tensor(h[:, b % 4, :], h[:, b % 4, :], 0.01, h[:, b % 4, :],
                                                             ALU.mult, ALU.max))
                        if l + 1 < layers:
                            nc.vector.tensor_scalar(hs[:, b, :], h[:, b % 4, :], root_p[:, b:b + 1], None, ALU.mult) \
                                .then_inc(scaled, 1)
                        else:
                            chain(nc.vector.tensor_tensor(c.x[:, b, :], c.x[:, b, :], h[:, b % 4, :], ALU.add))
                            measure(b, c.x[:, b, :])
                scale(dve, chain, lambda b: c.x[:, b, :], lambda b: c.x[:, b, :])


def gat(c):
    nc = c.nc
    AHEAD = 3
    SLOTS = 4
    PAIR = 2 * NB
    ON_POOL = (1, 4, 7)
    ON_DVE = tuple(b for b in range(NB) if b not in ON_POOL)
    SCORED0 = NB + SLOTS
    (loaded, turned, turned_out, wx_ready, wx_out, prod_ready, reduced, set_up, lnready, cnt_ready, cnt_out,
     mask_t_made, s_turned, s_taken, s_stored, maxed, step, args_made, args_turned, args_taken, args_stored,
     features_ready, low_ready, scored, masked_dve, masked_pool, probs_ready, probs_used, pv_out, turned_back,
     heads_out, chain_step, log_ready) = (semaphore(c, "gat_" + n) for n in (
         "loaded", "turned", "turned_out", "wx_ready", "wx_out", "products_ready", "reduced", "set_up",
         "logs_added", "counts_turned", "counts_out", "mask_t_made", "s_turned", "s_taken", "s_stored", "maxed",
         "step", "arguments_made", "arguments_turned", "arguments_taken", "arguments_stored", "features_ready",
         "low_slope", "scored", "masked_dve", "masked_pool", "probs_ready", "probs_used", "sums_out",
         "turned_back", "heads_out", "divide_step", "log_ready"))
    numbers_ready, numbers_out = semaphore(c, "gat_numbers_ready"), semaphore(c, "gat_numbers_out")
    s_arrived = [semaphore(c, f"gat_s_arrived_{n}") for n in range(2)]
    args_arrived = [semaphore(c, f"gat_arguments_arrived_{n}") for n in range(2)]
    s_rows = c.nc.dram_tensor("s_rows", [HEADS * NB, P], F32, kind="Internal").ap()
    arg_rows = c.nc.dram_tensor("arg_rows", [2 * HEADS * NB, P], F32, kind="Internal").ap()
    with ExitStack() as outer:
        sbo = lambda name, shape, dtype=F32: sbuf(c, name, shape, dtype, outer)
        wx = sbo("wx", [P, NB, HEADS, DH + 1])
        s_i = sbo("s_i", [P, HEADS, NB])
        s_low = sbo("s_low", [P, HEADS, NB])
        t_j = sbo("t_j", [P, HEADS, NB])
        top = sbo("top", [P, HEADS, NB])
        arg = sbo("arg", [P, 2, HEADS, NB])
        a_b = sbo("a_b", [P, HEADS])
        log_num = sbo("log_num", [P, NB, N])
        measure, root, scale, measured = layer_norm(c, "gat", outer)

        with ExitStack() as stack, nc.Block() as block:
            sb = lambda name, shape, dtype=F32: sbuf(c, name, shape, dtype, stack)
            w_s = sb("w_s", [P, FB, HEADS, DH])
            w_b = sb("w_b", [P, D])
            a_w = sb("a_w", [P, HEADS, 2 * DH])
            x_t = sb("x_t", [P, FB, N])
            prod = sb("prod", [P, 2, 2, D])
            mask_t = sb("mask_t", [P, NB, N])
            s_all = sb("s_all", [P, 2, N])
            row_sb = sb("row_sb", [P, P])
            atleast = s_all[:, 1, :].rearrange("p (u d) -> p u d", u=2)
            ps = [psum(c, f"gat_ps{b}", [P, 4, P], stack) for b in range(4)]
            cnt_ps = [psum(c, f"cnt_ps{b}", [P, 4, P], stack) for b in range(4)]

            @block.sync
            def _(sp):
                for h in range(HEADS):
                    sp.dma_start(w_s[:, :, h, :], c.ins["L1_gnn_Ws"][h].rearrange("(f p) d -> p f d", p=P)) \
                        .then_inc(loaded, 16)
                sp.dma_start(w_b[:], c.ins["L1_gnn_Wb"].rearrange("h d -> (h d)").partition_broadcast(P)) \
                    .then_inc(loaded, 16)
                sp.dma_start(a_w[:], c.ins["L1_gnn_a_w"].partition_broadcast(P)).then_inc(loaded, 16)
                sp.dma_start(a_b[:], c.ins["L1_gnn_a_b"].partition_broadcast(P)).then_inc(loaded, 16)
                sp.wait_ge(s_taken, 1)
                sp.dma_start(s_rows, row_sb[0:HEADS * NB, :]).then_inc(s_stored, 16)
                sp.wait_ge(s_stored, 16)
                sp.wait_ge(lnready, 2 * NB)
                for h in range(HEADS):
                    if h >= 2:
                        sp.wait_ge(maxed, NB * (h - 1))
                    row = s_rows[h * NB:(h + 1) * NB, :].rearrange("b n -> (b n)")
                    sp.dma_start(s_all[:, h % 2, :], row.partition_broadcast(P)).then_inc(s_arrived[h % 2], 16)
                sp.wait_ge(args_taken, 1)
                sp.dma_start(arg_rows, row_sb[:]).then_inc(args_stored, 16)
                sp.wait_ge(args_stored, 16)
            all_loaded = 16 * (HEADS + 3)

            @block.tensor
            def _(pe):
                for b in range(NB):
                    if b >= 4:
                        pe.wait_ge(turned_out, b - 3)
                    for f in range(FB):
                        last = nc.tensor.transpose(ps[b % 4][:, f, :], c.x[:, b, f * P:f * P + P], c.ident[:])
                    last.then_inc(turned, 1)
                pe.wait_ge(turned_out, NB)
                pe.wait_ge(loaded, all_loaded)
                for b in range(NB):
                    if b >= 4:
                        pe.wait_ge(wx_out, b - 3)
                    for f in range(FB):
                        last = nc.tensor.matmul(ps[b % 4][:], x_t[:, f, b * P:b * P + P], w_s[:, f, :, :],
                                                start=(f == 0), stop=(f == FB - 1))
                    last.then_inc(wx_ready, 1)
                    for half in range(2):
                        u = 2 * b + half
                        if u >= 4:
                            pe.wait_ge(cnt_out, 2 * (u - 3))
                        for j in range(4):
                            last = nc.tensor.transpose(cnt_ps[u % 4][:, j, :],
                                                       c.num_t[:, 4 * half + j, b * P:b * P + P], c.ident[:])
                        last.then_inc(cnt_ready, 1)
                pe.wait_ge(reduced, 2 * NB)
                nc.tensor.transpose(ps[0][0:HEADS * NB, 0, :], s_i[:].rearrange("p h b -> p (h b)"), c.ident[:]) \
                    .then_inc(s_turned, 1)
                for b in range(NB):
                    for k in range(NB):
                        last = nc.tensor.matmul(ps[2][:, 0, b:b + 1], c.num_t[:, k, b * P:b * P + P], c.ones[:, 0:1],
                                                start=(k == 0), stop=(k == NB - 1))
                last.then_inc(numbers_ready, 1)
                pe.wait_ge(args_made, 1)
                nc.tensor.transpose(ps[1][:, 0, :], arg[:].rearrange("p a h b -> p (a h b)"), c.ident[:]) \
                    .then_inc(args_turned, 1)

            @block.scalar
            def _(act):
                for b in range(NB):
                    act.wait_ge(turned, b + 1)
                    nc.scalar.copy(x_t[:, :, b * P:b * P + P], ps[b % 4][:]).then_inc(turned_out, 1)
                for u in range(2 * NB):
                    i, half = u // 2, u % 2
                    act.wait_ge(cnt_out, 2 * u + 2)
                    nc.scalar.activation(atleast[:, u % 2, :], atleast[:, u % 2, :], ACT.Ln).then_inc(log_ready, 1)
                act.wait_ge(s_turned, 1)
                nc.scalar.copy(row_sb[0:HEADS * NB, :], ps[0][0:HEADS * NB, 0, :]).then_inc(s_taken, 1)
                act.wait_ge(numbers_ready, 1)
                nc.scalar.copy(c.numbers[:], ps[2][:, 0, 0:NB]).then_inc(numbers_out, 1)
                act.wait_ge(args_turned, 1)
                act.wait_ge(s_stored, 16)
                nc.scalar.copy(row_sb[:], ps[1][:, 0, :]).then_inc(args_taken, 1)

            @block.gpsimd
            def _(pool):
                nc.gpsimd.memset(wx[:, :, :, DH:DH + 1], 1.0).then_inc(set_up, 1)
                pool.wait_ge(loaded, all_loaded)
                for b in range(NB):
                    pool.wait_ge(wx_out, b + 1)
                    if b >= 2:
                        pool.wait_ge(reduced, 2 * (b - 1))
                    for n in range(2):
                        nc.gpsimd.tensor_tensor(prod[:, b % 2, n, :].rearrange("p (h d) -> p h d", d=DH),
                                                wx[:, b, :, 0:DH], a_w[:, :, n * DH:n * DH + DH], ALU.mult) \
                            .then_inc(prod_ready, 1)
                    for u in range(2 * b, 2 * b + 2):
                        half = u % 2
                        pool.wait_ge(log_ready, u + 1)
                        nc.gpsimd.tensor_tensor(log_num[:, b, half * D:half * D + D],
                                                log_num[:, b, half * D:half * D + D], atleast[:, u % 2, :],
                                                ALU.add).then_inc(lnready, 1)

            @block.vector
            def _(dve):
                chain, _, _ = chained(dve, step)
                for b in range(NB):
                    nc.vector.tensor_scalar(mask_t[:, b, :], c.num_t[:, b, :], 0.5, -BIG, ALU.is_lt, ALU.mult) \
                        .then_inc(mask_t_made, 1)
                dve.wait_ge(loaded, all_loaded)
                dve.wait_ge(set_up, 1)

                def reduce(b):
                    for n, term in enumerate((t_j, s_i)):
                        dve.wait_ge(prod_ready, 2 * b + n + 1)
                        nc.vector.tensor_reduce(term[:, :, b], prod[:, b % 2, n, :].rearrange("p (h d) -> p h d", d=DH),
                                                AX, ALU.add).then_inc(reduced, 1)

                for b in range(NB):
                    dve.wait_ge(wx_ready, b + 1)
                    nc.vector.tensor_tensor(wx[:, b, :, 0:DH], ps[b % 4][:].rearrange("p a (g d) -> p (a g) d", d=DH),
                                            w_b[:].rearrange("p (h d) -> p h d", d=DH), ALU.add).then_inc(wx_out, 1)
                    for u in range(2 * b, 2 * b + 2):
                        half = u % 2
                        dve.wait_ge(cnt_ready, u + 1)
                        if u >= 2:
                            dve.wait_ge(lnready, u - 1)
                        got = cnt_ps[u % 4][:].rearrange("p a b -> p (a b)")
                        nc.vector.tensor_scalar(log_num[:, b, half * D:half * D + D], got, 0.5, -BIG, ALU.is_lt,
                                                ALU.mult).then_inc(cnt_out, 1)
                        nc.vector.tensor_scalar(atleast[:, u % 2, :], got, 1.0, None, ALU.max).then_inc(cnt_out, 1)
                    if b:
                        reduce(b - 1)
                reduce(NB - 1)
                dve.wait_ge(mask_t_made, NB)
                for h in range(HEADS):
                    dve.wait_ge(s_arrived[h % 2], 16 * (h // 2) + 16)
                    for b in range(NB):
                        if h * NB + b >= 2:
                            dve.wait_ge(maxed, h * NB + b - 1)
                        nc.vector.tensor_tensor_reduce(out=x_t[:, b % 2, :], in0=s_all[:, h % 2, :], in1=mask_t[:, b, :], scale=1.0,
                                                       scalar=-3e38, op0=ALU.add, op1=ALU.max,
                                                       accum_out=top[:, h, b:b + 1]).then_inc(maxed, 1)
                dve.wait_ge(maxed, HEADS * NB)
                chain(nc.vector.tensor_tensor(t_j[:], t_j[:], a_b[:].unsqueeze(2).to_broadcast([P, HEADS, NB]),
                                              ALU.add))
                chain(nc.vector.tensor_tensor(top[:], top[:], t_j[:], ALU.add))
                chain(nc.vector.scalar_tensor_tensor(top[:], top[:], 0.2, top[:], ALU.mult, ALU.max))
                chain(nc.vector.tensor_tensor(arg[:, 0, :, :], t_j[:], top[:], ALU.subtract))
                chain(nc.vector.scalar_tensor_tensor(arg[:, 1, :, :], t_j[:], 0.2, top[:], ALU.mult, ALU.subtract))
                dve.sem_inc(args_made, 1)
                chain(nc.vector.tensor_scalar(s_low[:], s_i[:], 0.2, None, ALU.mult))

        with ExitStack() as stack, nc.Block() as block:
            sb = lambda name, shape, dtype=F32: sbuf(c, name, shape, dtype, stack)
            args = sb("args", [P, 2, 2, N])
            low = sb("low_slope", [P, SLOTS, N])
            score = sb("score", [P, SLOTS, N])
            prob = sb("prob", [P, SLOTS, N])
            features = sb("features", [P, 2, NB, DH + 1])
            sums = sb("head_sums", [DH + 1, N])
            head = sb("head", [P, NB, DH])
            den = sb("den", [P, 2, NB])
            pv_ps = [psum(c, f"pv_ps{b}", [P, 2, D], stack) for b in range(2)]
            back_ps = psum(c, "back_ps", [P, 2, D], stack)
            turns = HEADS // 2

            @block.sync
            def _(sp):
                rows = arg_rows.rearrange("(a h b) n -> a h (b n)", a=2, h=HEADS)
                with sp.Fori(0, turns) as i:
                    for h in range(2):
                        sp.wait_ge(scored, i * PAIR + (NB * h + SLOTS))
                        for a in range(2):
                            sp.dma_start(args[:, h, a, :],
                                         rows[a, bass.ds(i * 2 + h, 1), :].rearrange("o n -> (o n)")
                                         .partition_broadcast(P)).then_inc(args_arrived[h], 16)

            @block.gpsimd
            def _(pool):
                def take_features(i, h):
                    pool.wait_ge(pv_out, i * 2 + (h + 1))
                    nc.gpsimd.tensor_copy(features[:, h % 2:h % 2 + 1, :, :].rearrange("p o b d -> p b o d"),
                                          wx[:, :, bass.ds(i * 2 + h, 1), :]).then_inc(features_ready, 1)

                def pair(i, ends=False):
                    for h in range(2):
                        for b in ON_POOL:
                            n = NB * h + b
                            pool.wait_ge(scored, i * PAIR + (SCORED0 + n + 1))
                            nc.gpsimd.tensor_tensor(score[:, b % SLOTS, :], score[:, b % SLOTS, :], log_num[:, b, :],
                                                    ALU.add).then_inc(masked_pool, 1)
                            if b == ON_POOL[1] and not (ends and h):
                                take_features(i, h + 1)

                take_features(0, 0)
                with pool.Fori(0, turns - 1) as i:
                    pair(i)
                pair(turns - 1, True)

            @block.tensor
            def _(pe):
                def turn_back(e):
                    pe.wait_ge(pv_out, e + 3)
                    pe.wait_ge(heads_out, e + 1)
                    for j in range(NB):
                        at = (j % 4) * (DH + 1)
                        last = nc.tensor.transpose(back_ps[:, j // 4, at:at + DH + 1], sums[:, j * P:j * P + P],
                                                   c.ident[0:DH + 1, 0:DH + 1])
                    last.then_inc(turned_back, 1)

                def pair(i, first=False):
                    for h in range(2):
                        pe.wait_ge(pv_out, i * 2 + (h + 1))
                        pe.wait_ge(features_ready, i * 2 + (h + 1))
                        for b in range(NB):
                            pe.wait_ge(probs_ready, i * PAIR + (NB * h + b + SLOTS + 1))
                            for half in range(2):
                                last = nc.tensor.matmul(pv_ps[h][0:DH + 1, half, :], features[:, h, b, :],
                                                        prob[:, b % SLOTS, half * D:half * D + D],
                                                        start=(b == 0), stop=(b == NB - 1))
                            last.then_inc(probs_used, 1)
                            if b == 3 and not (first and h == 0):
                                turn_back(i * 2 + (h - 1))

                pe.sem_inc(turned_back, 1)
                pair(0, True)
                with pe.Fori(0, turns - 1) as i:
                    pair(i + 1)
                turn_back(HEADS - 1)

            @block.scalar
            def _(act):
                def take_sums(e, h):
                    act.wait_ge(probs_used, e * NB + (NB + SLOTS))
                    act.wait_ge(turned_back, e + 1)
                    nc.scalar.copy(sums[:].rearrange("p (k n) -> p k n", k=2), pv_ps[h][0:DH + 1, :, :]) \
                        .then_inc(pv_out, 1)

                def low_slope(i, n):
                    h, b = n // NB, n % NB
                    act.wait_ge(args_arrived[h % 2], (i + h // 2) * 32 + 32)
                    act.wait_ge(scored, i * PAIR + (n + 1 + SCORED0 - SLOTS))
                    nc.scalar.activation(low[:, b % SLOTS, :], args[:, h % 2, 1, :], ACT.Identity,
                                         bias=s_low[:, bass.ds(i * 2 + h, 1), b]).then_inc(low_ready, 1)

                def exponential(i, n):
                    h, b = n // NB, n % NB
                    if b in ON_POOL:
                        act.wait_ge(masked_pool, i * (2 * len(ON_POOL)) + (len(ON_POOL) * h + ON_POOL.index(b) + 1))
                    else:
                        act.wait_ge(masked_dve, i * (2 * len(ON_DVE)) + (len(ON_DVE) * h + ON_DVE.index(b) + 1))
                    act.wait_ge(probs_used, i * PAIR + (n + 1))
                    nc.scalar.activation(prob[:, b % SLOTS, :], score[:, b % SLOTS, :], ACT.Exp) \
                        .then_inc(probs_ready, 1)

                def pair(i, first=False, ends=False):
                    for n in range(PAIR):
                        h, b = n // NB, n % NB
                        if not (ends and n + AHEAD >= PAIR):
                            low_slope(i, n + AHEAD)
                        exponential(i, n)
                        if b == 2 and not (first and h == 0):
                            take_sums(i * 2 + (h - 1), (h - 1) % 2)

                act.sem_inc(pv_out, 2)
                act.sem_inc(probs_ready, SLOTS)
                act.sem_inc(probs_used, SLOTS)
                for n in range(AHEAD):
                    low_slope(0, n)
                pair(0, first=True)
                with act.Fori(0, turns - 2) as i:
                    pair(i + 1)
                pair(turns - 1, ends=True)
                take_sums(HEADS - 1, 1)
                root(act)

            @block.vector
            def _(dve):
                chain, turn, close = chained(dve, chain_step)
                dve.sem_inc(scored, SCORED0)
                dve.sem_inc(heads_out, 1)

                def make_score(i, n):
                    h, b = n // NB, n % NB
                    dve.wait_ge(args_arrived[h], i * 32 + 32)
                    dve.wait_ge(low_ready, i * PAIR + (n + 1))
                    dve.wait_ge(probs_ready, i * PAIR + (n + 1))
                    nc.vector.scalar_tensor_tensor(score[:, b % SLOTS, :], args[:, h, 0, :],
                                                   s_i[:, bass.ds(i * 2 + h, 1), b], low[:, b % SLOTS, :],
                                                   ALU.add, ALU.max).then_inc(scored, 1)

                def mask(i, n):
                    b = n % NB
                    dve.wait_ge(scored, i * PAIR + (SCORED0 + n + 1))
                    nc.vector.tensor_tensor(score[:, b % SLOTS, :], score[:, b % SLOTS, :], log_num[:, b, :],
                                            ALU.add).then_inc(masked_dve, 1)

                def divide(e, column):
                    got = back_ps[:, :, 0:4 * (DH + 1)].rearrange("p k (j d) -> p k j d", d=DH + 1)
                    d = den[:, 0, :].rearrange("p (k j) -> p k j", j=4)
                    dve.wait_ge(turned_back, e + 2)
                    chain(nc.vector.tensor_scalar(d, got[:, :, :, DH], 1e-30, None, ALU.max))
                    chain(nc.vector.reciprocal(d, d))
                    nc.vector.tensor_tensor(head[:].rearrange("p (k j) d -> p k j d", j=4), got[:, :, :, 0:DH],
                                            d.unsqueeze(3).to_broadcast([P, 2, 4, DH]), ALU.mult) \
                        .then_inc(heads_out, 1)
                    dve.wait_ge(heads_out, e + 2)
                    to = c.x[:, :, column]
                    chain(nc.vector.tensor_tensor(to, to, head[:], ALU.add))

                def pair(i, first=False):
                    for n in range(PAIR):
                        h = n // NB
                        make_score(i, n)
                        if n % NB and (n - 1) % NB in ON_DVE:
                            mask(i, n - 1)
                        if n % NB == 6 and not (first and h == 0):
                            divide(i * 2 + (h - 1), bass.ds(i * (2 * DH) + (h - 1) * DH, DH))
                        if n % NB == NB - 1 and NB - 1 in ON_DVE:
                            mask(i, n)

                pair(0, True)
                with dve.Fori(0, turns - 1) as i:
                    turn(i, 6)
                    pair(i + 1)
                close(turns - 1)
                divide(HEADS - 1, slice(D - DH, D))
                for b in range(NB):
                    measure(b, c.x[:, b, :])
                scale(dve, chain, lambda b: c.x[:, b, :], lambda b: c.x[:, b, :])


HID = 32
Q_AT, P1_AT, X_AT = 0, HID, HID + 3 * MUL
ROW = X_AT + D
FAR = ROW - P1_AT
LAGS = 5
UNROLL = 6
HEAD = 10


def staged(engine, stages):
    assert (S - HEAD) % UNROLL == 0 and HEAD >= LAGS
    for u in range(HEAD):
        for lag, stage in stages:
            if u >= lag:
                stage(u - lag, (u - lag) % UNROLL, (u - lag) // UNROLL)
    with engine.Fori(0, (S - HEAD) // UNROLL) as i:
        for k in range(UNROLL):
            for lag, stage in stages:
                ahead = HEAD + k - lag
                stage(i * UNROLL + ahead, ahead % UNROLL, i + ahead // UNROLL)
    for u in range(S, S + LAGS):
        for lag, stage in stages:
            if u - lag < S:
                stage(u - lag, (u - lag) % UNROLL, (u - lag) // UNROLL)


def interaction(c):
    nc = c.nc
    with ExitStack() as stack:
        c.far = nc.dram_tensor("far_rows", [N, FAR], F32, kind="Internal").ap()
        c.local_rows = nc.dram_tensor("local_rows", [T * P], F32, kind="Internal").ap()
        c.table = sbuf(c, "table", [P, NB, ROW], F32, stack)
        c.w_o = sbuf(c, "w_o", [P, 2, MUL], F32, stack)
        c.b_o = sbuf(c, "b_o", [P, MUL], F32, stack)
        c.w_s1 = sbuf(c, "w_s1", [P, 3, HID], F32, stack)
        c.w_f1 = sbuf(c, "w_f1", [HID, HID], F32, stack)
        c.w_2 = sbuf(c, "w_2", [2 * HID, 4 * MUL], F32, stack)
        interaction_nodes(c)
        c.sums = sbuf(c, "sums", [P, NB, D], F32, stack)
        interaction_edges(c)
        interaction_out(c)


def interaction_nodes(c):
    nc = c.nc
    (loaded, turned, turned_out, step, square_ready, norm_ready, g1_ready, g1_out, act_ready, hid_ready, g2_ready,
     g_ready, xg_ready, p0_ready, p0_out, near_ready, near_out, self_ready, table_ready, stored, exp_ready) = (
        semaphore(c, "node_" + n) for n in (
            "loaded", "turned", "turned_out", "step", "square_ready", "norm_ready", "g1_ready", "g1_out",
            "neg_bias", "hidden_ready", "g2_ready", "g_ready", "gated", "p0_ready", "p0_out", "near_ready",
            "near_out", "self_ready", "table_ready", "stored", "exp_ready"))
    places_turned, places_out = semaphore(c, "places_turned"), semaphore(c, "places_out")
    with ExitStack() as stack, nc.Block() as block:
        sb = lambda name, shape, dtype=F32: sbuf(c, name, shape, dtype, stack)
        tile_rows = sb("tile_rows", [P, 2, P])
        w_pre = sb("w_pre", [P, 2, MUL])
        w_nd = sb("w_nd", [P, 2, MUL])
        w_g = sb("w_g", [P, 2, 2, 2 * MUL])
        b_g = sb("b_g", [P, 2, 2])
        b_g_neg = sb("b_g_neg", [P, 2])
        b_pre = sb("b_pre", [P, 1])
        b_nd = sb("b_nd", [P, MUL])
        x_t = sb("x_t4", [P, 4, N])
        length = sb("length", [P, N])
        hidden = sb("hidden", [P, 2, N])
        gate = sb("gate", [P, 2, N])
        expo = sb("expo", [P, 2, D])
        p0_t = sb("p0_t", [P, N])
        ps = [psum(c, f"node_ps{b}", [P, D], stack) for b in range(8)]
        cols = dict(allow_slow_non_contiguous=True)

        @block.sync
        def _(sp):
            loads = [(w_pre[:, 0, :], "W_pre0"), (w_pre[:, 1, :], "W_pre1"), (w_nd[:, 0, :], "W_nd0"),
                     (w_nd[:, 1, :], "W_nd1"), (c.w_o[:, 0, :], "W_o0"), (c.w_o[:, 1, :], "W_o1"),
                     (c.w_f1[:], "W_f1"), (c.w_2[0:HID, :], "W_f2"), (c.w_2[HID:2 * HID, :], "W_s2")]
            for to, name in loads:
                sp.dma_start(to, c.ins["L2_gnn_" + name]).then_inc(loaded, 16)
            sp.dma_start(c.w_s1[:], c.ins["L2_gnn_W_s1"].rearrange("(a p) h -> p a h", p=P)).then_inc(loaded, 16)
            for n, name in enumerate(("g1", "g2")):
                sp.dma_start(w_g[:, n, :, :], c.ins["L2_gnn_W_" + name].rearrange("(a p) h -> p a h", p=P)) \
                    .then_inc(loaded, 16)
                sp.dma_start(b_g[:, n, :], c.ins["L2_gnn_b_" + name].rearrange("(a p) -> p a", p=P), **cols) \
                    .then_inc(loaded, 16)
            sp.dma_start(b_pre[:], c.ins["L2_gnn_b_pre0"].rearrange("(a p) -> p a", p=P), **cols) \
                .then_inc(loaded, 16)
            sp.dma_start(b_nd[:], c.ins["L2_gnn_b_nd0"].partition_broadcast(P)).then_inc(loaded, 16)
            sp.dma_start(c.b_o[:], c.ins["L2_gnn_b_o0"].partition_broadcast(P)).then_inc(loaded, 16)
            sp.wait_ge(places_out, 2)
            for n in range(2):
                t0, t1 = n * P, min(T, n * P + P)
                sp.dma_start(c.local_rows[t0 * P:t1 * P].rearrange("(t e) -> t e", e=P),
                             tile_rows[0:t1 - t0, n, :]).then_inc(stored, 16)
            sp.wait_ge(near_out, NB)
            sp.wait_ge(table_ready, NB)
            sp.dma_start(c.far.rearrange("(b p) r -> p b r", p=P), c.table[:, :, P1_AT:ROW]).then_inc(stored, 16)
            sp.wait_ge(stored, 48)
        all_loaded = 16 * 17

        @block.tensor
        def _(pe):
            for n in range(2):
                t0, t1 = n * P, min(T, n * P + P)
                nc.tensor.transpose(ps[6 + n][0:t1 - t0, 0:P], c.i_local[:, t0:t1], c.ident[:]) \
                    .then_inc(places_turned, 1)
            for b in range(NB):
                if b >= 4:
                    pe.wait_ge(turned_out, b - 3)
                to = ps[b % 4][:].rearrange("p (f n) -> p f n", f=4)
                nc.tensor.transpose(to[:, 0, :], c.x[:, b, 0:MUL], c.ident[:])
                vectors = c.x[:, b, MUL:D].rearrange("p (u m) -> p m u", m=3)
                for m in range(3):
                    last = nc.tensor.transpose(to[:, 1 + m, :], vectors[:, m, :], c.ident[:])
                last.then_inc(turned, 1)
            pe.wait_ge(turned_out, NB)
            pe.wait_ge(loaded, all_loaded)
            for half in range(2):
                nc.tensor.matmul(ps[4 + half][:], w_pre[:, 0, :], x_t[:, 0, half * D:half * D + D],
                                 start=True, stop=True).then_inc(p0_ready, 1)
            pe.wait_ge(norm_ready, 1)
            for o in range(2):
                for half in range(2):
                    cut = slice(half * D, half * D + D)
                    nc.tensor.matmul(ps[2 * o + half][:], w_g[:, 0, 0, o * P:o * P + P], x_t[:, 0, cut],
                                     start=True, stop=False)
                    nc.tensor.matmul(ps[2 * o + half][:], w_g[:, 0, 1, o * P:o * P + P], length[:, cut],
                                     start=False, stop=True).then_inc(g1_ready, 1)
            pe.wait_ge(p0_out, 2)
            pe.wait_ge(places_out, 2)
            for b in range(NB):
                if b >= 4:
                    pe.wait_ge(near_out, b - 3)
                to, cut = ps[4 + b % 4], slice(b * P, b * P + P)
                nc.tensor.matmul(to[:, Q_AT:Q_AT + HID], p0_t[:, cut], c.w_s1[:, 0, :], start=True, stop=False)
                nc.tensor.matmul(to[:, Q_AT:Q_AT + HID], p0_t[:, cut], c.w_s1[:, 1, :], start=False, stop=True)
                for m in range(3):
                    last = nc.tensor.matmul(to[:, P1_AT + m * MUL:P1_AT + (m + 1) * MUL], x_t[:, 1 + m, cut],
                                            w_pre[:, 1, :], start=True, stop=True)
                last.then_inc(near_ready, 1)
            pe.wait_ge(hid_ready, 4)
            for o in range(2):
                for half in range(2):
                    for k in range(2):
                        last = nc.tensor.matmul(ps[2 * o + half][:], w_g[:, 1, k, o * P:o * P + P],
                                                hidden[:, k, half * D:half * D + D], start=(k == 0), stop=(k == 1))
                    last.then_inc(g2_ready, 1)
            pe.wait_ge(g_ready, 4)
            pe.wait_ge(xg_ready, 3)
            for b in range(NB):
                if b >= 4:
                    pe.wait_ge(table_ready, b - 3)
                to, cut = ps[b % 4], slice(b * P, b * P + P)
                nc.tensor.matmul(to[:, 0:MUL], gate[:, 0, cut], w_nd[:, 0, :], start=True, stop=True)
                for m in range(3):
                    last = nc.tensor.matmul(to[:, (1 + m) * MUL:(2 + m) * MUL], x_t[:, 1 + m, cut], w_nd[:, 1, :],
                                            start=True, stop=True)
                last.then_inc(self_ready, 1)

        @block.scalar
        def _(act):
            for n in range(2):
                tiles = min(T, n * P + P) - n * P
                act.wait_ge(places_turned, n + 1)
                nc.scalar.copy(tile_rows[0:tiles, n, :], ps[6 + n][0:tiles, 0:P]).then_inc(places_out, 1)
            for b in range(NB):
                act.wait_ge(turned, b + 1)
                nc.scalar.copy(x_t[:, :, b * P:b * P + P], ps[b % 4][:].rearrange("p (f n) -> p f n", f=4)) \
                    .then_inc(turned_out, 1)
            act.wait_ge(loaded, all_loaded)
            for half in range(2):
                act.wait_ge(p0_ready, half + 1)
                nc.scalar.activation(p0_t[:, half * D:half * D + D], ps[4 + half][:], ACT.Identity,
                                     bias=b_pre[:, 0:1]).then_inc(p0_out, 1)
            act.wait_ge(square_ready, 1)
            nc.scalar.activation(length[:], length[:], ACT.Sqrt, scale=1.0 / 3.0).then_inc(norm_ready, 1)
            act.wait_ge(act_ready, 1)
            for o in range(2):
                for half in range(2):
                    u = 2 * o + half
                    act.wait_ge(g1_ready, u + 1)
                    if u >= 2:
                        act.wait_ge(hid_ready, u - 1)
                    nc.scalar.activation(expo[:, half, :], ps[u][:], ACT.Exp, bias=b_g_neg[:, o:o + 1],
                                         scale=-1.0).then_inc(exp_ready, 1)
            for b in range(NB):
                act.wait_ge(near_ready, b + 1)
                nc.scalar.copy(c.table[:, b, 0:X_AT], ps[4 + b % 4][:, 0:X_AT]).then_inc(near_out, 1)
            for o in range(2):
                for half in range(2):
                    u = 2 * o + half
                    act.wait_ge(g2_ready, u + 1)
                    nc.scalar.activation(gate[:, o, half * D:half * D + D], ps[u][:], ACT.Identity,
                                         bias=b_g[:, 1, o:o + 1]).then_inc(g_ready, 1)

        @block.vector
        def _(dve):
            chain, _, _ = chained(dve, step)
            dve.wait_ge(loaded, all_loaded)
            nc.vector.tensor_scalar(b_g_neg[:], b_g[:, 0, :], -1.0, None, ALU.mult).then_inc(act_ready, 1)
            chain(nc.vector.tensor_scalar(c.w_2[0:HID, 3 * MUL:], c.w_2[0:HID, 3 * MUL:], 3.0 ** -0.5, None,
                                          ALU.mult))
            dve.wait_ge(turned_out, NB)
            chain(nc.vector.tensor_tensor(length[:], x_t[:, 1, :], x_t[:, 1, :], ALU.mult))
            square = hidden[:, 0, :]
            for m in (2, 3):
                chain(nc.vector.tensor_tensor(square, x_t[:, m, :], x_t[:, m, :], ALU.mult))
                last = nc.vector.tensor_tensor(length[:], length[:], square, ALU.add)
                if m == 2:
                    chain(last)
            last.then_inc(square_ready, 1)
            for o in range(2):
                for half in range(2):
                    u = 2 * o + half
                    dve.wait_ge(exp_ready, u + 1)
                    e = expo[:, half, :]
                    chain(nc.vector.tensor_scalar(e, e, 1.0, None, ALU.add))
                    chain(nc.vector.reciprocal(e, e))
                    nc.vector.scalar_tensor_tensor(hidden[:, o, half * D:half * D + D], ps[u][:],
                                                   b_g[:, 0, o:o + 1], e, ALU.add, ALU.mult).then_inc(hid_ready, 1)
            dve.wait_ge(near_ready, NB)
            dve.wait_ge(g_ready, 4)
            for m in range(3):
                nc.vector.tensor_tensor(x_t[:, 1 + m, :], x_t[:, 1 + m, :], gate[:, 1, :], ALU.mult) \
                    .then_inc(xg_ready, 1)
            for b in range(NB):
                dve.wait_ge(self_ready, b + 1)
                chain(nc.vector.tensor_tensor(c.table[:, b, X_AT:X_AT + MUL], ps[b % 4][:, 0:MUL], b_nd[:], ALU.add))
                nc.vector.tensor_copy(c.table[:, b, X_AT + MUL:ROW], ps[b % 4][:, MUL:D]).then_inc(table_ready, 1)


def interaction_edges(c):
    nc = c.nc
    FIRST = dict(onehots_turned=3, near=3, products=1, inner=2, turned=2, turned_out=1, hidden=3, shifted=1,
                 filtered=2, filter_out=1, weights=2, dots=UNROLL, thirds=UNROLL, messages=UNROLL, sums=2, added=1)
    made = lambda name, u, per=1: u * per + (1 + FIRST[name]) * per
    free = lambda name, u, ring, per=1: u * per + (1 + FIRST[name] - ring) * per
    (hot_t_ready, near_ready, prod_ready, ip_ready, turned, turned_out, hid_ready, soft_shifted, filtered, filter_out,
     weights_ready, dots_ready, thirds_ready, msgs_ready, sums_ready, sums_added) = (semaphore(c, "edge_" + n) for n in FIRST)
    (hot_ready, soft_ready, soft_step, filt_f, step, index_copied, index_seen, index_made, sums_cleared, attr_ready,
     q_ready, fourth_ready) = (
         semaphore(c, "edge_" + n) for n in (
             "onehot_ready", "softplus_ready", "softplus_step", "attributes_filtered", "step", "index_copied",
             "index_seen", "indices_made", "sums_cleared", "attributes_ready", "near_scalars_ready", "fourth_ready"))
    arrived = c.gathered[GT:]
    places_arrived = [semaphore(c, f"places_arrived_{g}") for g in range(3)]
    STEPS = 3
    with ExitStack() as stack, nc.Block() as block:
        sb = lambda name, shape, dtype=F32: sbuf(c, name, shape, dtype, stack)
        far_node = sb("far_node", [P, T], I32)
        index = sb("far_index", [P, UNROLL * TPS], I32)
        half = sb("half", [P, 1])
        far = sb("far", [P, UNROLL, TPS, FAR])
        places = sb("places", [P, 3, SUP])
        hot_t = sb("hot_t", [P, 3, SUP])
        hot = sb("hot", [P, 2, TPS, P])
        attr = sb("attr", [P, 2, TPS, 32])
        attr_t = sb("attr_t", [HID, 2, SUP])
        q = sb("q", [P, 2, HID])
        inner = sb("inner", [P, 2, TPS, MUL])
        inner_t = sb("inner_t", [P, 2, SUP])
        soft = sb("soft", [2 * HID, 2, SUP])
        weight = sb("weight_e", [P, 2, TPS, 4, MUL])
        msg = sb("msg", [P, 2, TPS, 4, MUL])
        firsts = sb("firsts", [P, TPS, 2, MUL])
        dot = sb("dot", [P, TPS, MUL])
        near_ps = psum(c, "near_ps", [P, TPS, D], stack)
        turn_ps = psum(c, "turn_ps", [P, 2, SUP], stack)
        hid_ps = psum(c, "hid_ps", [P, 2 * SUP], stack)
        f_ps = psum(c, "f_ps", [P, D], stack)
        s_ps = psum(c, "s_ps", [P, TPS, D], stack)
        sum_ps = psum(c, "sum_ps", [P, D], stack)

        @block.sync
        def _(sp):
            def load_places(u, r, turn):
                sp.wait_ge(hot_t_ready, free("onehots_turned", u, 3))
                sp.dma_start(places[:, r % 3, :], c.local_rows[bass.ds(u * SUP, SUP)].partition_broadcast(P)) \
                    .then_inc(places_arrived[r % 3], 16)

            staged(sp, [(0, load_places)])

        @block.gpsimd
        def _(pool):
            pool.sem_inc(ip_ready, 2 * FIRST["inner"])
            pool.sem_inc(thirds_ready, FIRST["thirds"])

            def gather(u, r, turn):
                pool.wait_ge(msgs_ready, free("messages", u, UNROLL))
                pool.wait_ge(thirds_ready, free("thirds", u, UNROLL))
                for k in range(TPS):
                    g = TPS * r + k
                    nc.gpsimd.tensor_copy(index[:, g:g + 1], far_node[:, bass.ds(u * TPS + k, 1)]) \
                        .then_inc(index_copied, 1)
                    pool.wait_ge(index_copied, u * TPS + (k + 1))
                    pool.sem_inc(index_seen, 1)
                    nc.gpsimd.indirect_dma_start(far[:, r, k, :], None, c.far[:, :],
                                                 bass.IndirectOffsetOnAxis(ap=index[:, g:g + 1], axis=0)) \
                        .then_inc(arrived[g], 16)

            def take_fixed(u, r, turn):
                pool.wait_ge(turned, free("turned", u, 2))
                nc.gpsimd.tensor_copy(attr[:, r % 2, :, :], c.recs[:, bass.ds(u * TPS, TPS), 0:32]) \
                    .then_inc(attr_ready, 1)
                block_of = pool.value_load(c.block_reg[0:1, bass.ds(u, 1)], min_val=0, max_val=NB - 1)
                pool.wait_ge(hid_ready, free("hidden", u, 2))
                nc.gpsimd.tensor_copy(q[:, r % 2:r % 2 + 1, :], c.table[:, bass.ds(block_of, 1), Q_AT:Q_AT + HID]) \
                    .then_inc(q_ready, 1)

            def add_inner(u, r, turn):
                b = r % 2
                pool.wait_ge(prod_ready, made("products", u))
                pool.wait_ge(turned, free("turned", u, 2))
                nc.gpsimd.tensor_tensor(inner[:, b, :, :], far[:, r, :, 0:MUL], far[:, r, :, MUL:2 * MUL], ALU.add) \
                    .then_inc(ip_ready, 1)
                pool.wait_ge(ip_ready, u * 2 + (1 + 2 * FIRST["inner"]))
                nc.gpsimd.tensor_tensor(inner[:, b, :, :], inner[:, b, :, :], far[:, r, :, 2 * MUL:3 * MUL],
                                        ALU.add) \
                    .then_inc(ip_ready, 1)

            def thirds(u, r, turn):
                b = r % 2
                pool.wait_ge(weights_ready, made("weights", u))
                pool.wait_ge(sums_ready, free("sums", u, 2))
                nc.gpsimd.tensor_tensor(
                    msg[:, b, :, 1:4, :], far[:, r, :, 4 * MUL:].rearrange("p k (m v) -> p k m v", m=3),
                    weight[:, b, :, 2:3, :].to_broadcast([P, TPS, 3, MUL]), ALU.mult).then_inc(thirds_ready, 1)

            pool.wait_ge(index_made, 1)
            staged(pool, [(0, gather), (1, take_fixed), (1, add_inner), (3, thirds)])

        @block.tensor
        def _(pe):
            for semaphore, name in ((near_ready, "near"), (turned, "turned"), (hid_ready, "hidden"),
                                    (filtered, "filtered"), (sums_ready, "sums")):
                pe.sem_inc(semaphore, FIRST[name])

            def gather_near(u, r, turn):
                block_of = pe.value_load(c.block_reg[0:1, bass.ds(u, 1)], min_val=0, max_val=NB - 1)
                pe.wait_ge(hot_t_ready, made("onehots_turned", u))
                pe.wait_ge(prod_ready, free("products", u, 1))
                for k in range(TPS):
                    last = nc.tensor.matmul(near_ps[:, k, 0:3 * MUL], hot_t[:, r % 3, k * P:k * P + P],
                                            c.table[:, bass.ds(block_of, 1), P1_AT:X_AT], start=True, stop=True)
                last.then_inc(near_ready, 1)

            def turn_inner(u, r, turn):
                pe.wait_ge(attr_ready, u + 1)
                pe.wait_ge(ip_ready, made("inner", u, 2))
                pe.wait_ge(turned_out, free("turned_out", u, 1, 2))
                for k in range(TPS):
                    nc.tensor.transpose(turn_ps[:, 0, k * P:k * P + P], inner[:, r % 2, k, :], c.ident[:])
                for k in range(TPS):
                    last = nc.tensor.transpose(turn_ps[0:HID, 1, k * P:k * P + P], attr[:, r % 2, k, :], c.ident[:])
                last.then_inc(turned, 1)

            def hidden(u, r, turn):
                b = r % 2
                pe.wait_ge(turned_out, made("turned_out", u, 2))
                pe.wait_ge(q_ready, u + 1)
                pe.wait_ge(soft_shifted, free("shifted", u, 1))
                nc.tensor.matmul(hid_ps[HID:2 * HID, 0:SUP], c.w_s1[:, 2, :], inner_t[:, b, :], start=True, stop=False)
                nc.tensor.matmul(hid_ps[HID:2 * HID, 0:SUP], q[:, b, :], hot_t[:, r % 3, :], start=False, stop=True)
                nc.tensor.matmul(hid_ps[0:HID, 0:SUP], c.w_f1[:], attr_t[:, b, :], start=True, stop=True) \
                    .then_inc(hid_ready, 1)

            def filters(u, r, turn):
                b = r % 2
                pe.wait_ge(soft_shifted, made("shifted", u))
                pe.wait_ge(weights_ready, free("weights", u, 1))

                def of_attributes(k):
                    pe.wait_ge(filter_out, u * (2 * TPS) + (2 * k + 2 * TPS * FIRST["filter_out"]))
                    nc.tensor.matmul(f_ps[:], soft[0:HID, b, k * P:k * P + P], c.w_2[0:HID, :], start=True,
                                     stop=True).then_inc(filt_f, 1)

                def of_scalars(k):
                    return nc.tensor.matmul(s_ps[:, k, :], soft[HID:2 * HID, b, k * P:k * P + P],
                                            c.w_2[HID:2 * HID, :], start=True, stop=True)

                of_attributes(0)
                of_scalars(0)
                of_scalars(1).then_inc(filtered, 1)
                of_attributes(1)

            def add_up(u, r, turn):
                pe.wait_ge(hot_ready, u + 1)
                pe.wait_ge(msgs_ready, made("messages", u))
                pe.wait_ge(sums_added, free("added", u, 1))
                for k in range(TPS):
                    last = nc.tensor.matmul(sum_ps[:], hot[:, r % 2, k, :], msg[:, r % 2, k, :, :], start=(k == 0),
                                            stop=(k == TPS - 1))
                last.then_inc(sums_ready, 1)

            staged(pe, [(1, gather_near), (5, add_up), (2, turn_inner), (3, filters), (2, hidden)])

        @block.scalar
        def _(act):
            for semaphore, name in ((turned_out, "turned_out"), (filter_out, "filter_out")):
                act.sem_inc(semaphore, FIRST[name] * (2 if name == "turned_out" else 2 * TPS))

            act.wait_ge(sums_cleared, 2)
            nc.scalar.preload_act_table_set("natural_log_exp_and_others")

            def take_turned(u, r, turn):
                b = r % 2
                act.wait_ge(turned, made("turned", u))
                act.wait_ge(hid_ready, free("hidden", u, 2))
                nc.scalar.mul(inner_t[:, b, :], turn_ps[:, 0, :], 1.0 / 3.0).then_inc(turned_out, 1)
                nc.scalar.copy(attr_t[:, b, :], turn_ps[0:HID, 1, :]).then_inc(turned_out, 1)

            def take_hidden(u, r, turn):
                b = r % 2
                act.wait_ge(hid_ready, made("hidden", u))
                act.wait_ge(filtered, free("filtered", u, 2))
                to = soft[:, b, :]
                nc.scalar.activation(to, hid_ps[0:2 * HID, 0:SUP], ACT.Abs).then_inc(soft_step, 1)
                act.wait_ge(soft_step, u * 2 + 1)
                nc.scalar.activation(to, to, ACT.Exp, scale=-1.0).then_inc(soft_step, 1)
                act.wait_ge(soft_step, u * 2 + 2)
                nc.scalar.activation(to, to, ACT.Ln, scale=0.5, bias=half[0:2 * HID, 0:1]).then_inc(soft_ready, 1)

            def take_filter(u, r, turn):
                b = r % 2
                act.wait_ge(thirds_ready, free("thirds", u, 2))
                act.wait_ge(msgs_ready, free("messages", u, 2))
                for k in range(TPS):
                    act.wait_ge(filt_f, u * TPS + (k + 1))
                    got = f_ps[:].rearrange("p (a o v) -> p o a v", a=2, o=2)
                    to = weight[:, b, k, :, :].rearrange("p (a o) v -> p o a v", a=2)
                    sh0 = c.recs[:, bass.ds(u * TPS + k, 1), R_SH]
                    nc.scalar.activation(to[:, 0, :, :], got[:, 0, :, :], ACT.Copy, scale=sh0).then_inc(filter_out, 1)
                    nc.scalar.copy(to[:, 1, :, :], got[:, 1, :, :]).then_inc(filter_out, 1)

            def scale_vectors(u, r, turn):
                act.wait_ge(ip_ready, made("inner", u, 2))
                for k in range(TPS):
                    for m in range(3):
                        last = nc.scalar.activation(
                            far[:, r, k, m * MUL:(m + 1) * MUL], far[:, r, k, (4 + m) * MUL:(5 + m) * MUL], ACT.Copy,
                            scale=c.recs[:, bass.ds(u * TPS + k, 1), R_SH + 1 + m])
                last.then_inc(dots_ready, 1)

            act.sem_inc(dots_ready, FIRST["dots"])
            staged(act, [(3, scale_vectors), (2, take_turned), (3, take_filter), (2, take_hidden)])

        @block.vector
        def _(dve):
            nc.vector.tensor_copy(far_node[:], c.recs[:, :, R_J]).then_inc(index_made, 1)
            nc.vector.memset(c.sums[:], 0.0).then_inc(sums_cleared, 1)
            nc.vector.memset(half[:], 0.5).then_inc(sums_cleared, 1)
            dve.wait_ge(sums_cleared, 2)
            for semaphore, name in ((hot_t_ready, "onehots_turned"), (prod_ready, "products"),
                                    (soft_shifted, "shifted"), (weights_ready, "weights"),
                                    (msgs_ready, "messages"), (sums_added, "added")):
                dve.sem_inc(semaphore, FIRST[name])

            def one_hot_turned(u, r, turn):
                dve.wait_ge(places_arrived[r % 3], (turn * 2 + r // 3) * 16 + 16)
                dve.wait_ge(near_ready, free("near", u, 3))
                dve.wait_ge(hid_ready, free("hidden", u, 3))
                nc.vector.tensor_scalar(hot_t[:, r % 3, :], places[:, r % 3, :], c.iota_col[:, 0:1], None,
                                        ALU.is_equal).then_inc(hot_t_ready, 1)

            def one_hot(u, r, turn):
                dve.wait_ge(sums_ready, free("sums", u, 2))
                nc.vector.tensor_tensor(
                    hot[:, r % 2, :, :], c.iota_row[:].unsqueeze(1).to_broadcast([P, TPS, P]),
                    c.i_local[:, bass.ds(u * TPS, TPS)].unsqueeze(2).to_broadcast([P, TPS, P]), ALU.is_equal) \
                    .then_inc(hot_ready, 1)

            def product(u, r, turn):
                dve.wait_ge(near_ready, made("near", u))
                for k in range(TPS):
                    dve.wait_ge(arrived[TPS * r + k], turn * 16 + 16)
                nc.vector.tensor_tensor(far[:, r, :, 0:3 * MUL],
                                        near_ps[:, :, 0:3 * MUL], far[:, r, :, 0:3 * MUL], ALU.mult) \
                    .then_inc(prod_ready, 1)

            def shift(u, r, turn):
                dve.wait_ge(soft_ready, u + 1)
                nc.vector.scalar_tensor_tensor(soft[:, r % 2, :], hid_ps[0:2 * HID, 0:SUP], 0.0, soft[:, r % 2, :],
                                               ALU.max, ALU.add).then_inc(soft_shifted, 1)

            def weigh(u, r, turn):
                b = r % 2
                dve.wait_ge(filter_out, made("filter_out", u, 2 * TPS))
                dve.wait_ge(filtered, made("filtered", u))
                nc.vector.tensor_tensor(weight[:, b, :, :, :].rearrange("p k a v -> p k (a v)"),
                                        weight[:, b, :, :, :].rearrange("p k a v -> p k (a v)"), s_ps[:],
                                        ALU.mult).then_inc(weights_ready, 1)

            blocks = []
            block_of = lambda u: dve.value_load(c.block_reg[0:1, bass.ds(u, 1)], min_val=0, max_val=NB - 1)

            def messages(u, r, turn):
                b = r % 2
                scaled = lambda m: far[:, r, :, m * MUL:(m + 1) * MUL]
                dve.wait_ge(dots_ready, made("dots", u))
                nc.vector.tensor_tensor(dot[:], scaled(0), scaled(1), ALU.add).then_inc(step, 1)
                dve.wait_ge(weights_ready, made("weights", u))
                nc.vector.tensor_tensor(
                    firsts[:], far[:, r, :, 3 * MUL:4 * MUL].unsqueeze(2).to_broadcast([P, TPS, 2, MUL]),
                    weight[:, b, :, 0:2, :], ALU.mult).then_inc(step, 1)
                dve.wait_ge(step, u * STEPS + 1)
                nc.vector.tensor_tensor(dot[:], dot[:], scaled(2), ALU.add).then_inc(step, 1)
                dve.wait_ge(thirds_ready, made("thirds", u))
                dve.wait_ge(step, u * STEPS + 2)
                for k in range(TPS):
                    for m in range(3):
                        nc.vector.scalar_tensor_tensor(
                            msg[:, b, k, 1 + m, :], firsts[:, k, 1, :],
                            c.recs[:, bass.ds(u * TPS + k, 1), R_SH + 1 + m], msg[:, b, k, 1 + m, :], ALU.mult,
                            ALU.add)
                if not (isinstance(u, int) and u == 0):
                    blocks.append(block_of(u - 1))
                dve.wait_ge(step, u * STEPS + 3)
                nc.vector.tensor_tensor(dot[:], dot[:], weight[:, b, :, 3, :], ALU.mult).then_inc(fourth_ready, 1)
                dve.wait_ge(fourth_ready, u + 1)
                last = nc.vector.tensor_tensor(msg[:, b, :, 0, :], firsts[:, :, 0, :], dot[:], ALU.add)
                last.then_inc(msgs_ready, 1)
                dve.wait_ge(msgs_ready, made("messages", u))

            def take_sums(u, r, turn):
                block = blocks.pop() if blocks else block_of(u)
                dve.wait_ge(sums_ready, made("sums", u))
                dve.wait_ge(sums_added, free("added", u, 1))
                to = c.sums[:, bass.ds(block, 1), :]
                nc.vector.tensor_tensor(to, to, sum_ps[:].unsqueeze(1), ALU.add).then_inc(sums_added, 1)

            staged(dve, [(1, product), (3, shift), (0, one_hot_turned), (4, messages), (5, take_sums), (4, one_hot),
                         (3, weigh)])


def interaction_out(c):
    nc = c.nc
    own_added, turned, turned_out, out_ready, step = (semaphore(c, "inter_out_" + n) for n in (
        "own_added", "turned", "turned_out", "ready", "step"))
    with ExitStack() as stack, nc.Block() as block:
        sums_t = sbuf(c, "sums_t", [P, 4, N], F32, stack)
        scalars = sbuf(c, "scalars", [P, 2, MUL], F32, stack)
        measure, root, scale, measured = layer_norm(c, "interaction", stack)
        ps = [psum(c, f"inter_ps{b}", [P, D], stack) for b in range(4)]
        ps_out = [psum(c, f"inter_out_ps{b}", [P, D], stack) for b in range(4)]

        @block.vector
        def _(dve):
            chain, _, _ = chained(dve, step)
            for b in range(NB):
                nc.vector.tensor_tensor(c.sums[:, b, :], c.sums[:, b, :], c.table[:, b, X_AT:ROW], ALU.add) \
                    .then_inc(own_added, 1)
            for b in range(NB):
                dve.wait_ge(out_ready, b + 1)
                got = ps_out[b % 4]
                chain(nc.vector.tensor_tensor(scalars[:, b % 2, :], got[:, 0:MUL], c.b_o[:], ALU.add))
                vectors = c.x[:, b, MUL:D].rearrange("p (u m) -> p m u", m=3)
                nc.vector.scalar_tensor_tensor(vectors, vectors, 2.0, got[:, MUL:D].rearrange("p (m u) -> p m u", m=3),
                                               ALU.mult, ALU.add)
                chain(nc.vector.scalar_tensor_tensor(c.x[:, b, 0:MUL], c.x[:, b, 0:MUL], 2.0, scalars[:, b % 2, :],
                                                     ALU.mult, ALU.add))
                measure(b, c.x[:, b, :])
            scale(dve, chain, lambda b: c.x[:, b, :], lambda b: c.x[:, b, :])

        @block.scalar
        def _(act):
            for b in range(NB):
                act.wait_ge(turned, b + 1)
                nc.scalar.copy(sums_t[:, :, b * P:b * P + P], ps[b % 4][:].rearrange("p (f n) -> p f n", f=4)) \
                    .then_inc(turned_out, 1)
            root(act)

        @block.tensor
        def _(pe):
            for b in range(NB):
                pe.wait_ge(own_added, b + 1)
                if b >= 4:
                    pe.wait_ge(turned_out, b - 3)
                for f in range(4):
                    last = nc.tensor.transpose(ps[b % 4][:, f * P:f * P + P], c.sums[:, b, f * P:f * P + P],
                                               c.ident[:])
                last.then_inc(turned, 1)
            for b in range(NB):
                pe.wait_ge(turned_out, b + 1)
                if b >= 4:
                    pe.wait_ge(measured, b - 3)
                for f in range(4):
                    last = nc.tensor.matmul(ps_out[b % 4][:, f * P:f * P + P], sums_t[:, f, b * P:b * P + P],
                                            c.w_o[:, min(f, 1), :], start=True, stop=True)
                last.then_inc(out_ready, 1)


def graph_conv(c):
    nc = c.nc
    loaded, turned, turned_out, beta_ready, beta_out, sum_ready, sum_out, own_ready, step, stored = (
        semaphore(c, "conv_" + n) for n in ("loaded", "turned", "turned_out", "neighbour_ready",
                                     "neighbour_out", "sums_ready", "sums_out", "own_ready", "step", "stored"))
    with ExitStack() as stack, nc.Block() as block:
        sb = lambda name, shape, dtype=F32: sbuf(c, name, shape, dtype, stack)
        w_c = sb("w_c", [P, FB, D])
        w_n = sb("w_n", [P, FB, D])
        bias = sb("bias", [P, D])
        x_t = sb("x_t_conv", [P, FB, N])
        beta = sb("beta", [P, NB, D])
        inverse = sb("inverse", [P, NB])
        measure, root, scale, measured = layer_norm(c, "conv", stack)
        ps = [psum(c, f"conv_ps{b}", [P, D], stack) for b in range(4)]
        sum_ps = [psum(c, f"conv_sum_ps{b}", [P, D], stack) for b in range(2)]

        @block.sync
        def _(sp):
            for to, name in ((w_n, "L3_gnn_wn"), (w_c, "L3_gnn_wc")):
                sp.dma_start(to[:], c.ins[name].rearrange("(f p) o -> p f o", p=P)).then_inc(loaded, 16)
            sp.dma_start(bias[:], c.ins["L3_gnn_bias"].partition_broadcast(P)).then_inc(loaded, 16)
            out = c.out.rearrange("(b p) d -> p b d", p=P)
            sp.wait_ge(step, 3 + 2 * NB)
            sp.dma_start(out, c.x[:]).then_inc(stored, 16)
            sp.wait_ge(stored, 16)

        @block.tensor
        def _(pe):
            for b in range(NB):
                if b >= 4:
                    pe.wait_ge(turned_out, b - 3)
                for f in range(FB):
                    last = nc.tensor.transpose(ps[b % 4][:, f * P:f * P + P], c.x[:, b, f * P:f * P + P], c.ident[:])
                last.then_inc(turned, 1)
            pe.wait_ge(loaded, 48)
            pe.wait_ge(turned_out, NB)
            for b in range(NB):
                if b >= 4:
                    pe.wait_ge(beta_out, b - 3)
                for k in range(FB):
                    last = nc.tensor.matmul(ps[b % 4][:], x_t[:, k, b * P:b * P + P], w_n[:, k, :], start=(k == 0),
                                            stop=(k == FB - 1))
                last.then_inc(beta_ready, 1)
            pe.wait_ge(beta_out, NB)
            for i in range(NB):
                if i >= 2:
                    pe.wait_ge(sum_out, i - 1)
                for b in range(NB):
                    last = nc.tensor.matmul(sum_ps[i % 2][:], c.num_t[:, b, i * P:i * P + P], beta[:, b, :],
                                            start=(b == 0), stop=(b == NB - 1))
                last.then_inc(sum_ready, 1)
                if i >= 4:
                    pe.wait_ge(measured, i - 3)
                for k in range(FB):
                    last = nc.tensor.matmul(ps[i % 4][:], x_t[:, k, i * P:i * P + P], w_c[:, k, :], start=(k == 0),
                                            stop=(k == FB - 1))
                last.then_inc(own_ready, 1)

        @block.scalar
        def _(act):
            for b in range(NB):
                act.wait_ge(turned, b + 1)
                nc.scalar.copy(x_t[:, :, b * P:b * P + P], ps[b % 4][:].rearrange("p (f n) -> p f n", f=FB)) \
                    .then_inc(turned_out, 1)
            for b in range(NB):
                act.wait_ge(beta_ready, b + 1)
                nc.scalar.copy(beta[:, b, :], ps[b % 4][:]).then_inc(beta_out, 1)
            root(act)

        @block.vector
        def _(dve):
            chain, _, _ = chained(dve, step)
            chain(nc.vector.reciprocal(inverse[:], c.numbers[:]))
            dve.wait_ge(loaded, 48)
            dve.wait_ge(turned, NB)
            for b in range(NB):
                y = c.x[:, b, :]
                chain(nc.vector.tensor_tensor(y, y, bias[:], ALU.add))
                dve.wait_ge(sum_ready, b + 1)
                nc.vector.scalar_tensor_tensor(y, sum_ps[b % 2][:], inverse[:, b:b + 1], y, ALU.mult, ALU.add) \
                    .then_inc(sum_out, 1)
                dve.wait_ge(sum_out, b + 1)
                dve.wait_ge(own_ready, b + 1)
                chain(nc.vector.tensor_tensor(y, y, ps[b % 4][:], ALU.add))
                measure(b, y)
            scale(dve, chain, lambda b: c.x[:, b, :], lambda b: c.x[:, b, :])


def build_program(nc, ins, out):
    with ExitStack() as stack:
        c = Core()
        c.nc, c.stack, c.semaphores, c.used = nc, stack, ExitStack(), []
        c.ins, c.out = ins, out
        c.gathered = [stack.enter_context(nc.semaphore(f"gathered_{g}")) for g in range(GT + UNROLL * TPS)]
        constants(c)
        lasting_memory(c)
        with ExitStack() as c.gcn_stack:
            gcn_inputs(c)
            order_edges(c)
            clear_semaphores(c)
            build_adjacency(c)
            clear_semaphores(c)
            gcn(c)
            clear_semaphores(c)
        gat(c)
        clear_semaphores(c)
        interaction(c)
        clear_semaphores(c)
        graph_conv(c)



_INS = ['x', 'src', 'dst', 'edge_attr_32', 'edge_attr_4', 'edge_weight', 'L0_gnn_W_gcn', 'L0_gnn_b_gcn',
        'L0_gnn_W_mlp', 'L0_gnn_b_mlp', 'L1_gnn_Ws', 'L1_gnn_Wb', 'L1_gnn_a_w', 'L1_gnn_a_b', 'L2_gnn_W_pre0',
        'L2_gnn_b_pre0', 'L2_gnn_W_pre1', 'L2_gnn_W_nd0', 'L2_gnn_b_nd0', 'L2_gnn_W_nd1', 'L2_gnn_W_g1',
        'L2_gnn_b_g1', 'L2_gnn_W_g2', 'L2_gnn_b_g2', 'L2_gnn_W_f1', 'L2_gnn_W_f2', 'L2_gnn_W_s1', 'L2_gnn_W_s2',
        'L2_gnn_W_o0', 'L2_gnn_b_o0', 'L2_gnn_W_o1', 'L3_gnn_wc', 'L3_gnn_wn', 'L3_gnn_bias']


def kernel(**inputs):
    import numpy as _np
    import concourse.bacc as _bacc
    from concourse import mybir as _mybir
    from concourse.bass_utils import run_bass_kernel_spmd as _run

    nc = _bacc.Bacc("TRN2", target_bir_lowering=False, num_devices=1)
    arrays, aps = {}, {}
    for name in _INS:
        a = _np.ascontiguousarray(inputs[name])
        arrays[f"in_{name}"] = a
        aps[name] = nc.dram_tensor(f"in_{name}", a.shape, _mybir.dt.from_np(a.dtype), kind="ExternalInput").ap()
    out = nc.dram_tensor("out", (N, D), F32, kind="ExternalOutput").ap()
    build_program(nc, aps, out)
    r = _run(nc, [arrays], core_ids=[0])
    return r.results[0]["out"]
```
